# Optimizing a Trainium2 kernel written in Bass

```python
import numpy as np
import jax
import jax.numpy as jnp

def _softmax(x, axis=-1):
    return jax.nn.softmax(x, axis=axis)

def _gelu(x):
    return jax.nn.gelu(x, approximate=True)

def _silu(x):
    return jax.nn.silu(x)

def _sigmoid(x):
    return jax.nn.sigmoid(x)

def _layernorm(x, axis=-1, eps=1e-05):
    m = jnp.mean(x, axis=axis, keepdims=True)
    v = jnp.var(x, axis=axis, keepdims=True)
    return (x - m) / jnp.sqrt(v + eps)

def _scatter_add(tgt, idx, src, axis=0):
    return tgt.at[idx].add(src)

def _segment_sum(src, seg, n):
    return jax.ops.segment_sum(src, seg, n)
kernel_name = 'mk_gnn_resnorm_d2_gnn_r8_692da6'

def setup_inputs(seed: int=0):
    np.random.seed(seed)
    _w = jnp.asarray

    def _rec_inputs():
        import jax
        import jax.numpy as jnp
        _gk = jax.random.key(seed)
        x = -0.000202 + 1 * jax.random.normal(jax.random.fold_in(_gk, 1), (6250, 128), jnp.float32)
        _s = jax.random.randint(jax.random.fold_in(_gk, 2), (50000,), 0, 6250, jnp.int32)
        _d = jax.random.randint(jax.random.fold_in(_gk, 3), (50000,), 0, 6250, jnp.int32)
        _loop = jnp.arange(6250, dtype=jnp.int32)
        src = jnp.concatenate([_s, _d, _loop])
        dst = jnp.concatenate([_d, _s, _loop])
        _o = jnp.argsort(dst, stable=True)
        src = src[_o]
        dst = dst[_o]
        edge_attr_2 = -0.000414295 + 0.999828 * jax.random.normal(jax.random.fold_in(_gk, 12), (106250, 2), jnp.float32)
        edge_attr_3 = -0.000451519 + 1.00018 * jax.random.normal(jax.random.fold_in(_gk, 13), (106250, 3), jnp.float32)
        edge_weight = jax.random.uniform(jax.random.fold_in(_gk, 15), (106250,), jnp.float32, 0.0, 0.999998)
        return (x, src, dst, edge_attr_2, edge_attr_3, edge_weight)
    x, src, dst, edge_attr_2, edge_attr_3, edge_weight = _rec_inputs()

    def _L0_gnn_setup():
        import jax, jax.numpy as jnp
        import numpy as np
        N = 6250
        E = 100000
        MUL = 32
        NB = 8
        R_MAX = 1.0
        AVG = 16.0
        SQ3 = 3.0 ** 0.5

        def _radial_embedding(r):
            x = jnp.clip(r / R_MAX, 0.0, 1.0)
            centers = jnp.arange(NB, dtype=jnp.float32) / (NB - 1)
            sigma = 1.0 / (NB - 1)
            emb = jnp.exp(-0.5 * ((x[:, None] - centers[None, :]) / sigma) ** 2)
            emb = emb * NB ** 0.5 * (r <= R_MAX).astype(jnp.float32)[:, None]
            return emb
        key = jax.random.key(seed)
        k = jax.random.split(key, 12)
        inp = {'node_feats': jax.random.normal(k[0], (N, 4 * MUL), dtype=jnp.float32), 'edge_vec': jax.random.normal(k[1], (E, 3), dtype=jnp.float32), 'edge_length': jax.random.uniform(k[2], (E,), dtype=jnp.float32), 'senders': jax.random.randint(k[3], (E,), 0, N, dtype=jnp.int32), 'receivers': jax.random.randint(k[4], (E,), 0, N, dtype=jnp.int32), 'num_nodes': N, 'W_up0': jax.random.normal(k[5], (MUL, MUL), dtype=jnp.float32), 'W_up1': jax.random.normal(k[6], (MUL, MUL), dtype=jnp.float32), 'mlp_w0': jax.random.normal(k[7], (NB, 64), dtype=jnp.float32) / NB ** 0.5, 'mlp_b0': jnp.zeros((64,), dtype=jnp.float32), 'mlp_w1': jax.random.normal(k[8], (64, 64), dtype=jnp.float32) / 8.0, 'mlp_b1': jnp.zeros((64,), dtype=jnp.float32), 'mlp_w2': jax.random.normal(k[9], (64, 4 * MUL), dtype=jnp.float32) / 8.0, 'mlp_b2': jnp.zeros((4 * MUL,), dtype=jnp.float32), 'W_out0': jax.random.normal(k[10], (2 * MUL, MUL), dtype=jnp.float32), 'W_out1': jax.random.normal(k[11], (2 * MUL, MUL), dtype=jnp.float32)}
        return inp
    _L0_gnn_all = _L0_gnn_setup()
    _L0_gnn_in = {k: v for k, v in _L0_gnn_all.items() if k in ('W_up0', 'W_up1', 'mlp_w0', 'mlp_b0', 'mlp_w1', 'mlp_b1', 'mlp_w2', 'mlp_b2', 'W_out0', 'W_out1')}
    del _L0_gnn_all

    def _L1_gnn_setup():
        import jax, jax.numpy as jnp
        import numpy as np
        N_NODES = 6250
        N_EDGES = 100000
        IN_DIM = 128
        OUT_DIM = 128
        EDGE_DIM = 2
        LN_EPS = 1e-05
        key = jax.random.key(seed)
        ks = jax.random.split(key, 8)
        s = lambda fan_in: 1.0 / np.sqrt(fan_in)
        x = jax.random.normal(ks[0], (N_NODES, IN_DIM), dtype=jnp.float32)
        edge_attr = jax.random.normal(ks[1], (N_EDGES, EDGE_DIM), dtype=jnp.float32)
        mW1 = jax.random.normal(ks[2], (2 * IN_DIM + EDGE_DIM, OUT_DIM), dtype=jnp.float32) * s(2 * IN_DIM + EDGE_DIM)
        mb1 = jnp.zeros((OUT_DIM,), jnp.float32)
        mW2 = jax.random.normal(ks[3], (OUT_DIM, OUT_DIM), dtype=jnp.float32) * s(OUT_DIM)
        mb2 = jnp.zeros((OUT_DIM,), jnp.float32)
        uW1 = jax.random.normal(ks[4], (IN_DIM + OUT_DIM, OUT_DIM), dtype=jnp.float32) * s(IN_DIM + OUT_DIM)
        ub1 = jnp.zeros((OUT_DIM,), jnp.float32)
        uW2 = jax.random.normal(ks[5], (OUT_DIM, OUT_DIM), dtype=jnp.float32) * s(OUT_DIM)
        ub2 = jnp.zeros((OUT_DIM,), jnp.float32)
        gamma = jnp.ones((OUT_DIM,), jnp.float32)
        beta = jnp.zeros((OUT_DIM,), jnp.float32)
        edge_index = jax.random.randint(ks[6], (2, N_EDGES), 0, N_NODES, dtype=jnp.int64 if jax.config.jax_enable_x64 else jnp.int32)
        return {'x': x, 'edge_attr': edge_attr, 'mW1': mW1, 'mb1': mb1, 'mW2': mW2, 'mb2': mb2, 'uW1': uW1, 'ub1': ub1, 'uW2': uW2, 'ub2': ub2, 'gamma': gamma, 'beta': beta, 'edge_index': edge_index}
    _L1_gnn_all = _L1_gnn_setup()
    _L1_gnn_in = {k: v for k, v in _L1_gnn_all.items() if k in ('mW1', 'mb1', 'mW2', 'mb2', 'uW1', 'ub1', 'uW2', 'ub2', 'gamma', 'beta')}
    del _L1_gnn_all
    return {'x': x, 'src': src, 'dst': dst, 'edge_attr_2': edge_attr_2, 'edge_attr_3': edge_attr_3, 'edge_weight': edge_weight, 'L0_gnn_W_up0': _L0_gnn_in['W_up0'], 'L0_gnn_W_up1': _L0_gnn_in['W_up1'], 'L0_gnn_mlp_w0': _L0_gnn_in['mlp_w0'], 'L0_gnn_mlp_b0': _L0_gnn_in['mlp_b0'], 'L0_gnn_mlp_w1': _L0_gnn_in['mlp_w1'], 'L0_gnn_mlp_b1': _L0_gnn_in['mlp_b1'], 'L0_gnn_mlp_w2': _L0_gnn_in['mlp_w2'], 'L0_gnn_mlp_b2': _L0_gnn_in['mlp_b2'], 'L0_gnn_W_out0': _L0_gnn_in['W_out0'], 'L0_gnn_W_out1': _L0_gnn_in['W_out1'], 'L1_gnn_mW1': _L1_gnn_in['mW1'], 'L1_gnn_mb1': _L1_gnn_in['mb1'], 'L1_gnn_mW2': _L1_gnn_in['mW2'], 'L1_gnn_mb2': _L1_gnn_in['mb2'], 'L1_gnn_uW1': _L1_gnn_in['uW1'], 'L1_gnn_ub1': _L1_gnn_in['ub1'], 'L1_gnn_uW2': _L1_gnn_in['uW2'], 'L1_gnn_ub2': _L1_gnn_in['ub2'], 'L1_gnn_gamma': _L1_gnn_in['gamma'], 'L1_gnn_beta': _L1_gnn_in['beta']}

def reference(x, src, dst, edge_attr_2, edge_attr_3, edge_weight, L0_gnn_W_up0, L0_gnn_W_up1, L0_gnn_mlp_w0, L0_gnn_mlp_b0, L0_gnn_mlp_w1, L0_gnn_mlp_b1, L0_gnn_mlp_w2, L0_gnn_mlp_b2, L0_gnn_W_out0, L0_gnn_W_out1, L1_gnn_mW1, L1_gnn_mb1, L1_gnn_mW2, L1_gnn_mb2, L1_gnn_uW1, L1_gnn_ub1, L1_gnn_uW2, L1_gnn_ub2, L1_gnn_gamma, L1_gnn_beta):
    import jax
    import jax.numpy as jnp

    def _L0_gnn_ref(node_feats, edge_vec, edge_length, senders, receivers, num_nodes, W_up0, W_up1, mlp_w0, mlp_b0, mlp_w1, mlp_b1, mlp_w2, mlp_b2, W_out0, W_out1):
        import jax, jax.numpy as jnp
        import numpy as np
        N = 6250
        E = 100000
        MUL = 32
        NB = 8
        R_MAX = 1.0
        AVG = 16.0
        SQ3 = 3.0 ** 0.5

        def _radial_embedding(r):
            x = jnp.clip(r / R_MAX, 0.0, 1.0)
            centers = jnp.arange(NB, dtype=jnp.float32) / (NB - 1)
            sigma = 1.0 / (NB - 1)
            emb = jnp.exp(-0.5 * ((x[:, None] - centers[None, :]) / sigma) ** 2)
            emb = emb * NB ** 0.5 * (r <= R_MAX).astype(jnp.float32)[:, None]
            return emb
        f32 = jnp.float32
        rhat = edge_vec / (jnp.linalg.norm(edge_vec, axis=-1, keepdims=True) + 1e-12)
        Y1 = SQ3 * rhat
        emb = _radial_embedding(edge_length)
        h = jax.nn.silu(emb @ mlp_w0 + mlp_b0)
        h = jax.nn.silu(h @ mlp_w1 + mlp_b1)
        w = (h @ mlp_w2 + mlp_b2).reshape(-1, 4, MUL)
        s = node_feats[:, :MUL]
        v = node_feats[:, MUL:].reshape(-1, MUL, 3)
        xs = s @ W_up0 / f32(MUL) ** 0.5
        xv = jnp.einsum('nmc,mk->nkc', v, W_up1) / f32(MUL) ** 0.5
        ss = xs[senders]
        vv = xv[senders]
        m0 = w[:, 0] * ss
        m1 = w[:, 1][:, :, None] * ss[:, :, None] * Y1[:, None, :]
        m2 = w[:, 2][:, :, None] * vv
        m3 = w[:, 3] * (jnp.einsum('emc,ec->em', vv, Y1) / SQ3)
        mid_s = jnp.concatenate([m0, m3], axis=1)
        mid_v = jnp.concatenate([m1, m2], axis=1)
        msg_s = jax.ops.segment_sum(mid_s, receivers, num_segments=num_nodes)
        msg_v = jax.ops.segment_sum(mid_v, receivers, num_segments=num_nodes)
        out_s = msg_s @ W_out0 / f32(2 * MUL) ** 0.5
        out_v = jnp.einsum('nmc,mk->nkc', msg_v, W_out1) / f32(2 * MUL) ** 0.5
        out = jnp.concatenate([out_s, out_v.reshape(-1, 3 * MUL)], axis=1)
        return out / max(AVG, 1e-08)

    def _L1_gnn_ref(x, edge_attr, mW1, mb1, mW2, mb2, uW1, ub1, uW2, ub2, gamma, beta, edge_index):
        import jax, jax.numpy as jnp
        import numpy as np
        N_NODES = 6250
        N_EDGES = 100000
        IN_DIM = 128
        OUT_DIM = 128
        EDGE_DIM = 2
        LN_EPS = 1e-05
        num_nodes = x.shape[0]
        src, dst = (edge_index[0], edge_index[1])
        msg_in = jnp.concatenate([x[src], x[dst], edge_attr], axis=-1)
        msgs = jnp.maximum(msg_in @ mW1 + mb1, 0.0) @ mW2 + mb2
        agg = jax.ops.segment_sum(msgs, dst, num_segments=num_nodes)
        cnt = jax.ops.segment_sum(jnp.ones((dst.shape[0],), x.dtype), dst, num_segments=num_nodes)
        agg = agg / jnp.clip(cnt, 1.0)[:, None]
        upd_in = jnp.concatenate([x, agg], axis=-1)
        upd = jnp.maximum(upd_in @ uW1 + ub1, 0.0) @ uW2 + ub2
        upd = upd + x
        mu = jnp.mean(upd, axis=-1, keepdims=True)
        var = jnp.mean(jnp.square(upd - mu), axis=-1, keepdims=True)
        return (upd - mu) * jax.lax.rsqrt(var + LN_EPS) * gamma + beta
    edge_index = jnp.stack([src, dst])
    x = _layernorm(x + _L0_gnn_ref(x, edge_attr_3, edge_weight, src, dst, 6250, L0_gnn_W_up0, L0_gnn_W_up1, L0_gnn_mlp_w0, L0_gnn_mlp_b0, L0_gnn_mlp_w1, L0_gnn_mlp_b1, L0_gnn_mlp_w2, L0_gnn_mlp_b2, L0_gnn_W_out0, L0_gnn_W_out1), axis=-1)
    x = _layernorm(x + _L1_gnn_ref(x, edge_attr_2, L1_gnn_mW1, L1_gnn_mb1, L1_gnn_mW2, L1_gnn_mb2, L1_gnn_uW1, L1_gnn_ub1, L1_gnn_uW2, L1_gnn_ub2, L1_gnn_gamma, L1_gnn_beta, edge_index), axis=-1)
    return x

_drawn_inputs = setup_inputs


def setup_inputs(seed=0):
    import zlib

    import numpy as np

    out = dict(_drawn_inputs(seed))
    spreads = {'L0_gnn_mlp_b0': (0.0, 0.8),
     'L0_gnn_mlp_b1': (0.0, 0.574),
     'L0_gnn_mlp_b2': (0.0, 0.348),
     'L1_gnn_mb1': (0.0, 0.613),
     'L1_gnn_mb2': (0.0, 0.39),
     'L1_gnn_ub1': (0.0, 0.1),
     'L1_gnn_ub2': (0.0, 0.1),
     'L1_gnn_gamma': (1.0, 0.2),
     'L1_gnn_beta': (0.0, 0.1)}
    factors = {'edge_attr_2': 8.0}
    for name, (base, spread) in spreads.items():
        noise = np.random.default_rng([zlib.crc32(name.encode()), seed]).standard_normal(out[name].shape)
        drawn = base * np.exp(spread * noise) if base else spread * noise
        out[name] = jnp.asarray(drawn.astype(out[name].dtype))
    for name, factor in factors.items():
        out[name] = (out[name] * factor).astype(out[name].dtype)
    return out
```

```python
from contextlib import ExitStack

import concourse.bass as bass
from concourse import mybir

F32 = mybir.dt.float32
BF16 = mybir.dt.bfloat16
I32 = mybir.dt.int32
ALU = mybir.AluOpType
ACT = mybir.ActivationFunctionType
AX = mybir.AxisListType.X

P = 128
N = 6250
E = 106250
F = 128
MUL = 32
NB = 8
HID = 64
W = 64
HALF = 512
TPG = 8
GROUP = TPG * P
NG = -(-E // GROUP)
EP = NG * GROUP
NH = 2 * NG
NT = NG * TPG
CHUNK = 512
NC = -(-(N + W) // CHUNK)
NP = NC * CHUNK
NW = NP // W
EMB_STEP = P // NB
NE = NH // EMB_STEP
LN_EPS = 1e-5
SQ3 = 3.0 ** 0.5
OUT_SCALE = 1.0 / ((2 * MUL) ** 0.5 * 16.0)
assert NH % EMB_STEP == 0 and NG % 2 == 0


def along(ap, axis, n):
    shape = list(ap.shape)
    return ap.unsqueeze(axis).broadcast_to(shape[:axis] + [n] + shape[axis:])


def run_steps(eng, steps, lag, head, step):
    for n in range(head):
        step(n, n % 2, n // 2)
    loops = (steps - head) // 2
    with eng.Fori(0, loops) as i:
        for s in range(2):
            step(i * 2 + (head + s), s, i + head // 2)
    for n in range(head + 2 * loops, steps + lag):
        step(n, n % 2, n // 2)


def live(n, steps):
    return not isinstance(n, int) or 0 <= n < steps


def gnn_kernel(nc, a, out):
    with ExitStack() as ctx:
        def sb(name, shape, dt=F32):
            return ctx.enter_context(nc.sbuf_tensor(name, shape, dt))

        def sem(name):
            return ctx.enter_context(nc.semaphore(name))

        def pair(name):
            return [sem(f"{name}{s}") for s in range(2)]

        def dram(name, shape, dt=F32):
            return nc.dram_tensor(name, shape, dt).ap()

        x_table = dram("x_table", [NP, F])
        src_table = dram("src_table", [NP, F])
        dst_table = dram("dst_table", [NP, F])
        emb_d = dram("emb_d", [NH * NB, HALF])
        rel_d = dram("rel_d", [NG, GROUP])
        base_i_d = dram("base_i_d", [NG, 2], I32)
        base_f_d = dram("base_f_d", [NG, 2])
        span_d = dram("span_d", [NG, 1])
        b2_parts_d = dram("b2_parts_d", [1, 3 * F], BF16)

        ps = ctx.enter_context(nc.psum_tensor("ps", [P, 8, 512], F32))

        acc = sb("acc", [P, 2, NP])
        x1n = sb("x1n", [P, NC * 4, F])
        x1T = sb("x1T", [P, NP])
        rhat = sb("rhat", [P, NT, 3])
        rel = sb("rel", [P, NH, 4])
        dcol = sb("dcol", [P, NT])
        base_sb = sb("base_sb", [1, NH], I32)
        gen_i = sb("gen_i", [1, 1], I32)
        w_up = sb("w_up", [P, F])
        w0 = sb("w0", [2 * NB, P])
        w1 = sb("w1", [P, P])
        w2 = sb("w2", [P, F])
        b0 = sb("b0", [P, 1])
        b1 = sb("b1", [P, 1])
        b2_row = sb("b2_row", [1, F])
        b2_part = sb("b2_part", [1, 3, F], BF16)
        b2p = sb("b2p", [P, 4, F], BF16)
        ones_bf = sb("ones_bf", [P, P], BF16)
        w_out = sb("w_out", [P, 2, 2 * MUL])
        m_w1 = sb("m_w1", [P, 2, F])
        mb1 = sb("mb1", [P, F])
        m_w2 = sb("m_w2", [P, F])
        mb2 = sb("mb2", [1, F])
        u_w1 = sb("u_w1", [P, 2, F])
        ub1 = sb("ub1", [P, 1])
        u_w2 = sb("u_w2", [P, F])
        ub2 = sb("ub2", [P, F])
        gamma = sb("gamma", [P, F])
        beta = sb("beta", [P, F])
        ones = sb("ones", [P, P])
        ident = sb("ident", [P, P])
        expand = sb("expand", [EMB_STEP, P])
        iota_i = sb("iota_i", [P, W], I32)
        iota_n = sb("iota_n", [P, W])
        part_i = sb("part_i", [P, 2], I32)
        iota_p = sb("iota_p", [P, 1])
        center = sb("center", [P, 1])
        eps = sb("eps", [P, 1])
        zero = sb("zero", [P, 1])
        gen_col = sb("gen_col", [P, 2])
        ids = [sb(f"ids{s}", [P, 2 * TPG], I32) for s in range(2)]
        gx = [sb(f"gx{s}", [P, TPG, F]) for s in range(2)]
        mid = [sb(f"mid{s}", [P, TPG, 2 * F]) for s in range(2)]
        onehot = [sb(f"onehot{s}", [P, TPG, W]) for s in range(2)]
        relw = sb("relw", [P, TPG])
        emb_in = [sb(f"emb_in{s}", [2 * NB, HALF]) for s in range(2)]
        hid = [sb(f"hid{s}", [P, 2, HALF]) for s in range(2)]
        prod = sb("prod", [P, TPG, 3, MUL])
        dot = sb("dot", [P, TPG, MUL])
        onehot_t = [sb(f"onehot_t{s}", [W + 2, GROUP]) for s in range(2)]
        bwin = [sb(f"bwin{s}", [W + 2, 2, F]) for s in range(2)]
        hrelu = [sb(f"hrelu{s}", [P, TPG, F]) for s in range(2)]
        stats = [sb(f"stats{s}", [P, 4, 6]) for s in range(2)]
        mean_var = [sb(f"mean_var{s}", [P, 4, 2]) for s in range(2)]
        std = [sb(f"std{s}", [P, 4]) for s in range(2)]
        stats_b = [sb(f"stats_b{s}", [P, 4, 6]) for s in range(2)]
        mean_var_b = [sb(f"mean_var_b{s}", [P, 4, 2]) for s in range(2)]
        std_b = [sb(f"std_b{s}", [P, 4]) for s in range(2)]

        def flat(t):
            return t[:].rearrange("p a b -> p (a b)")

        def quad(ap):
            return ap.rearrange("p (q f) -> p q f", f=F)

        x1n_flat = x1n[:].rearrange("p a b -> p (a b)")
        evec_sq = x1n_flat[:, 0:3 * NT].rearrange("p (t c) -> p t c", c=3)
        norm = x1n_flat[:, 3 * NT:4 * NT]
        inv = x1n_flat[:, 4 * NT:5 * NT]
        dcol_i = x1n_flat[:, 5 * NT:6 * NT].bitcast(I32)
        drow_i = x1T[0:NG, 0:GROUP].bitcast(I32)
        drow = x1T[0:NG, GROUP:2 * GROUP]
        rel_row = x1T[0:NG, 2 * GROUP:3 * GROUP]
        base_all = x1T[:, 3 * GROUP:3 * GROUP + NH]
        span_all = x1T[:, 3 * GROUP + NH:3 * GROUP + NH + NG]
        small = x1T[:, 4 * GROUP:4 * GROUP + 16]
        small_i = x1T[:, 4 * GROUP + 16:4 * GROUP + 18].bitcast(I32)
        r_in = [onehot_t[s][0:EMB_STEP, 0:HALF] for s in range(2)]
        r_far = [onehot_t[s][0:EMB_STEP, HALF:2 * HALF] for s in range(2)]
        emb_sq = [flat(hrelu[s])[:, 0:HALF] for s in range(2)]
        emb_st = [flat(hrelu[s])[:, HALF:2 * HALF] for s in range(2)]
        xt_in = [gx[s][:, 0:4, :] for s in range(2)]
        xt_stage = [gx[s][:, 4:8, :] for s in range(2)]
        msum = [flat(gx[s]).rearrange("p (c n) -> p c n", c=2) for s in range(2)]
        xin = [hrelu[s][:, 0:4, :] for s in range(2)]
        y = [hrelu[s][:, 4:8, :] for s in range(2)]
        mid_flat = [flat(mid[s]) for s in range(2)]
        x1s = [quad(mid_flat[s][:, 0:512]) for s in range(2)]
        x1Ts = [mid_flat[s][:, 512:1024] for s in range(2)]
        tab = [mid[s][:, 4:8, :] for s in range(2)]
        gb = [mid[s][:, :, 0:F] for s in range(2)]
        sums = [mid[s][:, :, F:2 * F] for s in range(2)]
        relb = [flat(hid[s])[0:W, :] for s in range(2)]
        cnt_inv = [flat(gx[s])[:, 0:512] for s in range(2)]
        agg_t = [flat(gx[s])[:, 512:1024] for s in range(2)]
        h_u = [flat(hrelu[s])[:, 0:512] for s in range(2)]
        t_sum = [quad(mid_flat[s][:, 0:512]) for s in range(2)]
        z = [quad(mid_flat[s][:, 512:1024]) for s in range(2)]
        res = [quad(mid_flat[s][:, 1024:1536]) for s in range(2)]

        weights_in = sem("weights_in")
        cleared = sem("cleared")
        pool_consts = sem("pool_consts")
        consts = sem("consts")
        xt_loaded, xt_stored = pair("xt_loaded"), pair("xt_stored")
        xt_mm, xt_staged = sem("xt_mm"), sem("xt_staged")
        drow_in, dcol_in, evec_in = sem("drow_in"), sem("dcol_in"), sem("evec_in")
        dprep, ranges_ready, ranges_out, ranges_in = (
            sem("dprep"), sem("ranges_ready"), sem("ranges_out"), sem("ranges_in"))
        gen_ready, rel_ready, rel_out = sem("gen_ready"), sem("rel_ready"), sem("rel_out")
        norm_sq, norm_ready, vprep = sem("norm_sq"), sem("norm_ready"), sem("vprep")
        b2_split, b2_out, b2_in = sem("b2_split"), sem("b2_out"), sem("b2_in")
        r_loaded, emb_stored = pair("r_loaded"), pair("emb_stored")
        r_prep, r_ready, emb_mm, emb_sqd, emb_ready = (
            sem("r_prep"), sem("r_ready"), sem("emb_mm"), sem("emb_sqd"), sem("emb_ready"))
        ids_loaded, emb_loaded, gathered = pair("ids_loaded"), pair("emb_loaded"), pair("gathered")
        h1_mm, h1_act, h2_mm, h2_act, w_mm = (
            sem("h1_mm"), sem("h1_act"), sem("h2_mm"), sem("h2_act"), sem("w_mm"))
        vstep, mid_ready, seg_done, acc_add, acc_all = (
            sem("vstep"), sem("mid_ready"), sem("seg_done"), sem("acc_add"), sem("acc_all"))
        relw_step, win_ready, win_done = sem("relw_step"), sem("win_ready"), sem("win_done")
        msum_ready, po_mm, y_ready, xin_loaded = (
            sem("msum_ready"), sem("po_mm"), sem("y_ready"), pair("xin_loaded"))
        bn_done, mv_ready, std_ready, rstd_ready, x1_ready = (
            sem("bn_done"), sem("mv_ready"), sem("std_ready"), sem("rstd_ready"), sem("x1_ready"))
        x1_kept, x1t_mm, x1t_copied, x1t_kept = (
            sem("x1_kept"), sem("x1t_mm"), sem("x1t_copied"), sem("x1t_kept"))
        tab_mm, tab_a, tab_b, tab_stored = (
            sem("tab_mm"), sem("tab_a"), sem("tab_b"), pair("tab_stored"))
        acc_cleared, var_ready, var_a, var_b = (
            sem("acc_cleared"), sem("var_ready"), sem("var_a"), sem("var_b"))
        ids2_loaded, relb_loaded, pre_loaded, gathered2 = (
            pair("ids2_loaded"), pair("relb_loaded"), pair("pre_loaded"), pair("gathered2"))
        gathered_b = pair("gathered_b")
        we_loaded = sem("we_loaded")
        oht_ready, pre_mm, sum_step, sums_ready, relu_done = (
            sem("oht_ready"), sem("pre_mm"), sem("sum_step"), sem("sums_ready"), sem("relu_done"))
        seg2_done, acc2_add, acc2_all = sem("seg2_done"), sem("acc2_add"), sem("acc2_all")
        relw2_step, win2_ready, win2_done = sem("relw2_step"), sem("win2_ready"), sem("win2_done")
        cnt_max, cnt_ready, pa_mm, agg_ready, ph_mm, hu_ready, pu_mm = (
            sem("cnt_max"), sem("cnt_ready"), sem("pa_mm"), sem("agg_ready"), sem("ph_mm"),
            sem("hu_ready"), sem("pu_mm"))
        t_part, t_ready, bna, mva, stda, rstda, z_ready = (
            sem("t_part"), sem("t_ready"), sem("bna"), sem("mva"), sem("stda"), sem("rstda"),
            sem("z_ready"))
        zg, zb, zx = sem("zg"), sem("zb"), sem("zx")
        bnb, mvb, stdb, rstdb, res_ready = (
            sem("bnb"), sem("mvb"), sem("stdb"), sem("rstdb"), sem("res_ready"))
        out_stored = pair("out_stored")

        passed = sem("passed")

        def hold(eng):
            eng.sem_inc(passed, 1)

        block = ctx.enter_context(nc.Block())

        N_WEIGHTS = 31
        x_rows = a["x_rows"].rearrange("(q p) f -> p q f", p=P)
        x_table_rows = x_table.rearrange("(q p) f -> p q f", p=P)
        src_rows = src_table.rearrange("(q p) f -> p q f", p=P)
        dst_rows = dst_table.rearrange("(q p) f -> p q f", p=P)
        out_rows = out.rearrange("(q p) f -> p q f", p=P)

        @block.sync
        def _(sp):
            def load_xt(n, s, r):
                if live(n - 2, NC):
                    sp.wait_ge(xt_mm, n - 1)
                sp.dma_start(xt_in[s], quad(a["x_t"][:, bass.ds(n * CHUNK, CHUNK)])).then_inc(
                    xt_loaded[s], 16)
                if isinstance(n, int) and n == 1:
                    sp.dma_start(drow_i, a["dst_row"]).then_inc(drow_in, 16)
                    sp.dma_start(rhat[:], a["evec"]).then_inc(evec_in, 16)
                    sp.dma_start(dcol_i, a["dst_col"]).then_inc(dcol_in, 16)
            run_steps(sp, NC, 0, 2, load_xt)

            sp.wait_ge(ranges_ready, 1)
            sp.dma_start(base_f_d, small[0:NG, 0:2]).then_inc(ranges_out, 16)
            sp.dma_start(span_d, small[0:NG, 6:7]).then_inc(ranges_out, 16)
            sp.dma_start(base_i_d, small_i[0:NG, 0:2]).then_inc(ranges_out, 16)
            sp.wait_ge(ranges_out, 48)
            sp.dma_start(base_all, base_f_d.rearrange("g h -> (g h)").unsqueeze(0).broadcast_to(
                [P, NH])).then_inc(ranges_in, 16)
            sp.dma_start(span_all, span_d.rearrange("g h -> (g h)").unsqueeze(0).broadcast_to(
                [P, NG])).then_inc(ranges_in, 16)
            sp.dma_start(base_sb[:], base_i_d.rearrange("g h -> (g h)").unsqueeze(0)).then_inc(
                ranges_in, 16)
            sp.wait_ge(b2_split, 5)
            sp.dma_start(b2_parts_d, b2_part[:].rearrange("o k f -> o (k f)")).then_inc(b2_out, 16)
            sp.wait_ge(b2_out, 16)
            parts = b2_parts_d.rearrange("o (k f) -> (o k) f", k=3)
            for row in (0, HID):
                for q in range(4):
                    sp.dma_start(b2p[row:row + 3, q, :], parts).then_inc(b2_in, 16)
            sp.wait_ge(rel_ready, 1)
            sp.dma_start(rel_d, rel_row).then_inc(rel_out, 16)

            def load_r(n, s, r):
                if live(n - 2, NE):
                    sp.wait_ge(r_ready, n - 1)
                sp.dma_start(r_in[s], a["lengths"][bass.ds(n * EMB_STEP, EMB_STEP), :]).then_inc(
                    r_loaded[s], 16)
            run_steps(sp, NE, 0, 2, load_r)
            for s in range(2):
                sp.wait_ge(emb_stored[s], 16 * ((NE + 1 - s) // 2))

            def load_edges(n, s, r):
                if live(n - 2, NG):
                    sp.wait_ge(gathered[s], 128 * r)
                sp.dma_start(ids[s][:], a["ids"][bass.ds(n * P, P), :]).then_inc(
                    ids_loaded[s], 16)
                if live(n - 2, NG):
                    sp.wait_ge(h1_mm, n - 1)
                sp.dma_start(emb_in[s][:], emb_d[bass.ds(n * 2 * NB, 2 * NB), :]).then_inc(
                    emb_loaded[s], 16)
            run_steps(sp, NG, 0, 2, load_edges)

            def nodes(n, s, r):
                if live(n, NC):
                    if live(n - 2, NC):
                        sp.wait_ge(y_ready, 2 * n - 2)
                    sp.dma_start(xin[s], x_rows[:, bass.ds(n * 4, 4), :]).then_inc(
                        xin_loaded[s], 16)
                if live(n - 3, NC):
                    sp.wait_ge(tab_a, n - 2)
                    sp.wait_ge(tab_b, n - 2)
                    rows = bass.ds((n - 3) * 4, 4)
                    sp.dma_start(src_rows[:, rows, :], tab[1 - s][:, :, 0:F]).then_inc(
                        tab_stored[1 - s], 16)
                    sp.dma_start(dst_rows[:, rows, :], tab[1 - s][:, :, F:2 * F]).then_inc(
                        tab_stored[1 - s], 16)
            sp.wait_ge(acc_all, 1)
            run_steps(sp, NC, 3, 4, nodes)
            for s in range(2):
                sp.wait_ge(tab_stored[s], 32 * ((NC + 1 - s) // 2))
                for h in range(2):
                    sp.dma_start(bwin[s][W:W + 2, h, :], a["m_w1"][2 * F:2 * F + 2, :]).then_inc(
                        we_loaded, 16)

            sp.wait_ge(rel_out, 16)

            def load_edges2(n, s, r):
                if live(n - 2, NG):
                    sp.wait_ge(gathered2[s], 128 * r)
                sp.dma_start(ids[s][:], a["ids"][bass.ds(n * P, P), :]).then_inc(
                    ids2_loaded[s], 16)
                if live(n - 2, NG):
                    sp.wait_ge(oht_ready, n - 1)
                sp.dma_start(relb[s], rel_d[bass.ds(n, 1), :].broadcast_to([W, GROUP])).then_inc(
                    relb_loaded[s], 16)
                if live(n - 2, NG):
                    sp.wait_ge(pre_mm, n - 1)
                sp.dma_start(onehot_t[s][W:W + 2, :], a["attr2"][bass.ds(n * 2, 2), :]).then_inc(
                    pre_loaded[s], 16)
                for h in range(2):
                    base = sp.value_load(base_sb[0:1, bass.ds(n * 2 + h, 1)], min_val=0,
                                         max_val=NP - W)
                    sp.dma_start(bwin[s][0:W, h, :], dst_table[bass.ds(base, W), :]).then_inc(
                        pre_loaded[s], 16)
            run_steps(sp, NG, 0, 2, load_edges2)

            def store_out(n, s, r):
                sp.wait_ge(res_ready, 4 * n + 4)
                sp.dma_start(out_rows[:, bass.ds(n * 4, 4), :], res[s]).then_inc(
                    out_stored[s], 16)
            run_steps(sp, NC, 0, 2, store_out)
            for s in range(2):
                sp.wait_ge(out_stored[s], 16 * ((NC + 1 - s) // 2))

        @block.gpsimd
        def _(pool):
            pool.memset(expand[:], 1.0).then_inc(pool_consts, 1)
            pool.memset(ident[:], 0.0).then_inc(pool_consts, 1)
            pool.iota(iota_i[:], pattern=[[1, W]], base=0, channel_multiplier=0).then_inc(
                pool_consts, 1)
            pool.iota(part_i[:], pattern=[[0, 2]], base=0, channel_multiplier=1).then_inc(
                pool_consts, 1)
            pool.wait_ge(pool_consts, 2)
            pool.affine_select(out=expand[:], in_=expand[:], compare_op=ALU.is_ge, fill=0.0,
                               base=0, pattern=[[1, P]], channel_multiplier=-NB).then_inc(
                                   pool_consts, 1)
            pool.affine_select(out=ident[:], in_=ident[:], compare_op=ALU.not_equal, fill=1.0,
                               base=0, pattern=[[-1, P]], channel_multiplier=1).then_inc(
                                   pool_consts, 1)
            pool.wait_ge(pool_consts, 5)
            pool.affine_select(out=expand[:], in_=expand[:], compare_op=ALU.is_ge, fill=0.0,
                               base=NB - 1, pattern=[[-1, P]], channel_multiplier=NB).then_inc(
                                   pool_consts, 1)

            for s in range(2):
                pool.wait_ge(xt_stored[s], 16 * ((NC + 1 - s) // 2))

            def gather(n, s, r):
                pool.wait_ge(ids_loaded[s], 16 * r + 16)
                if live(n - 2, NG):
                    pool.wait_ge(mid_ready, n - 1)
                    hold(pool)
                for t in range(TPG):
                    pool.indirect_dma_start(
                        out=gx[s][:, t, :], out_offset=None, in_=x_table,
                        in_offset=bass.IndirectOffsetOnAxis(ap=ids[s][:, t:t + 1], axis=0),
                    ).then_inc(gathered[s], 16)
            run_steps(pool, NG, 0, 2, gather)

            def keep(n, s, r):
                pool.wait_ge(x1_ready, 4 * n + 4)
                pool.tensor_copy(x1n[:, bass.ds(n * 4, 4), :], x1s[s]).then_inc(x1_kept, 1)
                pool.wait_ge(x1t_copied, n + 1)
                pool.tensor_copy(x1T[:, bass.ds(n * CHUNK, CHUNK)], x1Ts[s]).then_inc(x1t_kept, 1)
            run_steps(pool, NC, 0, 2, keep)

            pool.wait_ge(x1_kept, NC)
            pool.wait_ge(x1t_kept, NC)
            for s in range(2):
                pool.wait_ge(tab_stored[s], 32 * ((NC + 1 - s) // 2))

            def gathers2(general):
                def gather2(n, s, r):
                    pool.wait_ge(ids2_loaded[s], 16 * r + 16)
                    if live(n - 2, NG):
                        pool.wait_ge(sums_ready, n - 1)
                        hold(pool)
                    if general:
                        for t in range(TPG):
                            pool.indirect_dma_start(
                                out=gb[s][:, t, :], out_offset=None, in_=dst_table,
                                in_offset=bass.IndirectOffsetOnAxis(
                                    ap=ids[s][:, TPG + t:TPG + t + 1], axis=0),
                            ).then_inc(gathered_b[s], 16)
                        pool.wait_ge(gathered_b[s], 128 * r + 128)
                        hold(pool)
                    for t in range(TPG):
                        pool.indirect_dma_start(
                            out=gx[s][:, t, :], out_offset=None, in_=src_table,
                            in_offset=bass.IndirectOffsetOnAxis(ap=ids[s][:, t:t + 1], axis=0),
                        ).then_inc(gathered2[s], 16)
                run_steps(pool, NG, 0, 2, gather2)

            general = pool.value_load(gen_i[0:1, 0:1], min_val=0, max_val=1)
            with pool.If(general == 1):
                gathers2(True)
            with pool.Else():
                gathers2(False)

            def finish(n, s, r):
                pool.wait_ge(z_ready, 4 * n + 4)
                pool.tensor_tensor(z[s], z[s], along(gamma[:], 1, 4), ALU.mult).then_inc(zg, 1)
                pool.wait_ge(zg, n + 1)
                pool.tensor_tensor(z[s], z[s], along(beta[:], 1, 4), ALU.add).then_inc(zb, 1)
                pool.wait_ge(zb, n + 1)
                pool.tensor_tensor(z[s], z[s], x1n[:, bass.ds(n * 4, 4), :], ALU.add).then_inc(
                    zx, 1)
            run_steps(pool, NC, 0, 2, finish)

        @block.scalar
        def _(act):
            def load(dst, src):
                act.dma_start(dst, src).then_inc(weights_in, 16)

            def row(x):
                return x.unsqueeze(0)

            def col(x):
                return x.unsqueeze(1)

            act.wait_ge(cleared, 4)
            for c in range(4):
                load(w_up[32 * c:32 * c + 32, 32 * c:32 * c + 32], a["w_up0" if c == 0 else "w_up1"])
            load(w0[0:NB, 0:HID], a["mlp_w0"])
            load(w0[NB:2 * NB, HID:P], a["mlp_w0"])
            for h in range(2):
                rows = slice(h * HID, h * HID + HID)
                load(w1[rows, rows], a["mlp_w1"])
                load(w2[rows, :], a["mlp_w2"])
                load(b0[rows, :], col(a["mlp_b0"]))
                load(b1[rows, :], col(a["mlp_b1"]))
                load(m_w1[:, h, :], a["m_w1"][h * F:h * F + F, :])
                load(u_w1[:, h, :], a["u_w1"][h * F:h * F + F, :])
            load(b2_row[:], row(a["mlp_b2"]))
            load(w_out[0:64, 0, 0:32], a["w_out0"])
            load(w_out[64:128, 0, 32:64], a["w_out1"])
            load(w_out[0:64, 1, 0:32], a["w_out1"])
            load(w_out[64:128, 1, 32:64], a["w_out1"])
            load(mb1[:], row(a["mb1"]).broadcast_to([P, F]))
            load(m_w2[:], a["m_w2"])
            load(mb2[:], row(a["mb2"]))
            load(ub1[:], col(a["ub1"]))
            load(u_w2[:], a["u_w2"])
            load(ub2[:], row(a["ub2"]).broadcast_to([P, F]))
            load(gamma[:], row(a["gamma"]).broadcast_to([P, F]))
            load(beta[:], row(a["beta"]).broadcast_to([P, F]))

            def stage_xt(n, s, r):
                act.wait_ge(xt_mm, n + 1)
                if live(n - 2, NC):
                    act.wait_ge(xt_stored[s], 16 * r)
                act.activation(xt_stage[s], quad(ps[:, s, :]), ACT.Copy,
                               scale=1.0 / MUL ** 0.5).then_inc(xt_staged, 1)
                act.wait_ge(xt_staged, n + 1)
                act.dma_start(x_table_rows[:, bass.ds(n * 4, 4), :], xt_stage[s]).then_inc(
                    xt_stored[s], 16)
            run_steps(act, NC, 0, 2, stage_xt)

            act.wait_ge(norm_sq, 1)
            act.activation(norm, norm, ACT.Sqrt).then_inc(norm_ready, 1)

            act.wait_ge(consts, 1)
            def embed(n, s, r):
                act.wait_ge(emb_mm, n + 1)
                act.activation(emb_sq[s], ps[:, 2 + s, :], ACT.Square, bias=center[:, 0:1],
                               scale=float(NB - 1)).then_inc(emb_sqd, 1)
                act.wait_ge(emb_sqd, n + 1)
                if live(n - 2, NE):
                    act.wait_ge(emb_stored[s], 16 * r)
                act.activation(emb_st[s], emb_sq[s], ACT.Exp, scale=-0.5).then_inc(emb_ready, 1)
                act.wait_ge(emb_ready, n + 1)
                act.dma_start(emb_d[bass.ds(n * P, P), :], emb_st[s]).then_inc(emb_stored[s], 16)
            run_steps(act, NE, 0, 2, embed)

            act.preload_act_table(ACT.Silu)

            def mlp(n, s, r):
                act.wait_ge(h1_mm, n + 1)
                if live(n - 2, NG):
                    act.wait_ge(h2_mm, n - 1)
                act.activation(hid[s][:, 0, :], ps[:, 0, :], ACT.Silu, bias=b0[:, 0:1]).then_inc(
                    h1_act, 1)
                act.wait_ge(h2_mm, n + 1)
                if live(n - 2, NG):
                    act.wait_ge(w_mm, n - 1)
                act.activation(hid[s][:, 1, :], ps[:, 1, :], ACT.Silu, bias=b1[:, 0:1]).then_inc(
                    h2_act, 1)
            run_steps(act, NG, 0, 2, mlp)

            act.preload_act_table(ACT.Sqrt)
            act.wait_ge(acc_all, 1)

            def nodes(n, s, r):
                if live(n, NC):
                    if live(n - 2, NC):
                        act.wait_ge(po_mm, n - 1)
                    act.copy(msum[s], acc[:, :, bass.ds(n * CHUNK, CHUNK)]).then_inc(msum_ready, 1)
                if live(n - 1, NC):
                    act.wait_ge(mv_ready, 4 * n)
                    act.activation(std[1 - s][:], mean_var[1 - s][:, :, 1], ACT.Sqrt).then_inc(
                        std_ready, 1)
                    act.wait_ge(x1t_mm, n)
                    if live(n - 3, NC):
                        act.wait_ge(tab_mm, n - 2)
                        act.wait_ge(x1t_kept, n - 2)
                    act.copy(x1Ts[1 - s], ps[:, 2 + (1 - s), :]).then_inc(x1t_copied, 1)
                if live(n - 2, NC):
                    act.wait_ge(tab_mm, n - 1)
                    if live(n - 4, NC):
                        act.wait_ge(tab_stored[s], 32 * r - 32)
                    act.copy(tab[s][:, :, 0:F], quad(ps[:, 4 + 2 * s, :])).then_inc(tab_a, 1)
            run_steps(act, NC, 2, 4, nodes)

            def relu(n, s, r):
                act.wait_ge(sums_ready, n + 1)
                if live(n - 2, NG):
                    act.wait_ge(seg2_done, n - 1)
                act.activation(hrelu[s][:], sums[s], ACT.Relu).then_inc(relu_done, 1)
            run_steps(act, NG, 0, 2, relu)

            act.preload_act_table(ACT.Sqrt)

            def update(n, s, r):
                if live(n, NC):
                    act.wait_ge(ph_mm, n + 1)
                    if live(n - 2, NC):
                        act.wait_ge(pu_mm, n - 1)
                    act.activation(h_u[s], ps[:, 2 + s, :], ACT.Relu, bias=ub1[:, 0:1]).then_inc(
                        hu_ready, 1)
                if live(n - 1, NC):
                    act.wait_ge(mva, 4 * n)
                    act.activation(std[1 - s][:], mean_var[1 - s][:, :, 1], ACT.Sqrt).then_inc(
                        stda, 1)
                if live(n - 2, NC):
                    act.wait_ge(mvb, 4 * n - 4)
                    act.activation(std_b[s][:], mean_var_b[s][:, :, 1], ACT.Sqrt).then_inc(stdb, 1)
            run_steps(act, NC, 2, 4, update)

        @block.tensor
        def _(pe):
            pe.wait_ge(weights_in, 16 * N_WEIGHTS)

            def project(n, s, r):
                pe.wait_ge(xt_loaded[s], 16 * r + 16)
                if live(n - 2, NC):
                    pe.wait_ge(xt_staged, n - 1)
                for q in range(4):
                    mm = pe.matmul(ps[:, s, q * F:q * F + F], xt_in[s][:, q, :], w_up[:],
                                   start=True, stop=True)
                mm.then_inc(xt_mm, 1)
            run_steps(pe, NC, 0, 2, project)

            pe.wait_ge(pool_consts, 7)

            def spread(n, s, r):
                pe.wait_ge(r_ready, n + 1)
                if live(n - 2, NE):
                    pe.wait_ge(emb_sqd, n - 1)
                pe.matmul(ps[:, 2 + s, :], expand[:], r_far[s], start=True,
                          stop=True).then_inc(emb_mm, 1)
            run_steps(pe, NE, 0, 2, spread)

            pe.wait_ge(consts, 2)
            pe.wait_ge(b2_in, 128)

            def mlp(n, s, r):
                pe.wait_ge(emb_loaded[s], 16 * r + 16)
                if live(n - 1, NG):
                    pe.wait_ge(h1_act, n)
                pe.matmul(ps[:, 0, :], w0[:], emb_in[s][:], start=True, stop=True).then_inc(
                    h1_mm, 1)
                pe.wait_ge(h1_act, n + 1)
                if live(n - 1, NG):
                    pe.wait_ge(h2_act, n)
                pe.matmul(ps[:, 1, :], w1[:], hid[s][:, 0, :], start=True, stop=True).then_inc(
                    h2_mm, 1)
                pe.wait_ge(h2_act, n + 1)
                if live(n - 2, NG):
                    pe.wait_ge(mid_ready, n - 1)
                for h in range(2):
                    r0 = h * HID
                    pe.matmul(ps[:, 2 + 2 * s + h, :], ones_bf[r0:r0 + 3, :],
                              b2p[r0:r0 + 3, :, :].rearrange("k q f -> k (q f)"), start=True,
                              stop=False)
                for t in range(4):
                    for h in range(2):
                        rows = slice(h * HID, h * HID + HID)
                        mm = pe.matmul(ps[:, 2 + 2 * s + h, t * F:t * F + F],
                                       hid[s][rows, 1, t * P:t * P + P], w2[rows, :],
                                       start=False, stop=(t == 3))
                mm.then_inc(w_mm, 1)

            def layer1(general):
                def step(n, s, r):
                    if live(n, NG):
                        mlp(n, s, r)
                    if live(n - 1, NG):
                        pe.wait_ge(mid_ready, n)
                        if general:
                            hold(pe)
                            with pe.Fori(0, NW) as w:
                                pe.wait_ge(win_ready, (n - 1) * NW + w + 1)
                                for c in range(2):
                                    for t in range(TPG):
                                        mm = pe.matmul(
                                            ps[:, 6, c * W:c * W + W],
                                            mid[1 - s][:, t, c * F:c * F + F],
                                            onehot[1 - s][:, t, :], start=(t == 0),
                                            stop=(t == TPG - 1))
                                mm.then_inc(win_done, 1)
                            return
                        if live(n - 3, NG):
                            pe.wait_ge(acc_add, 2 * n - 4)
                        for h in range(2):
                            for c in range(2):
                                for t in range(4 * h, 4 * h + 4):
                                    col = (2 * h + c) * W
                                    mm = pe.matmul(
                                        ps[:, 6 + (1 - s), col:col + W],
                                        mid[1 - s][:, t, c * F:c * F + F],
                                        onehot[1 - s][:, t, :], start=(t == 4 * h),
                                        stop=(t == 4 * h + 3))
                        mm.then_inc(seg_done, 1)
                run_steps(pe, NG, 1, 4, step)

            pe.wait_ge(gen_ready, 1)
            general = pe.value_load(gen_i[0:1, 0:1], min_val=0, max_val=1)
            with pe.If(general == 1):
                layer1(True)
            with pe.Else():
                layer1(False)

            def nodes(n, s, r):
                if live(n, NC):
                    pe.wait_ge(msum_ready, n + 1)
                    if live(n - 2, NC):
                        pe.wait_ge(y_ready, 2 * n - 2)
                    for q in range(4):
                        for c in range(2):
                            mm = pe.matmul(ps[:, s, q * F + c * 64:q * F + c * 64 + 64],
                                           msum[s][:, c, q * P:q * P + P], w_out[:, c, :],
                                           start=True, stop=True)
                    mm.then_inc(po_mm, 1)
                if live(n - 1, NC):
                    pe.wait_ge(x1_ready, 4 * n)
                    if live(n - 3, NC):
                        pe.wait_ge(x1t_copied, n - 2)
                    for q in range(4):
                        mm = pe.transpose(ps[:, 2 + (1 - s), q * P:q * P + P], x1s[1 - s][:, q, :],
                                          ident[:])
                    mm.then_inc(x1t_mm, 1)
                if live(n - 2, NC):
                    pe.wait_ge(x1t_copied, n - 1)
                    if live(n - 4, NC):
                        pe.wait_ge(tab_a, n - 3)
                        pe.wait_ge(tab_b, n - 3)
                    for h in range(2):
                        for q in range(4):
                            mm = pe.matmul(ps[:, 4 + 2 * s + h, q * F:q * F + F],
                                           x1Ts[s][:, q * P:q * P + P], m_w1[:, h, :],
                                           start=True, stop=True)
                    mm.then_inc(tab_mm, 1)
            run_steps(pe, NC, 2, 4, nodes)

            pe.wait_ge(we_loaded, 64)

            def layer2(general):
                def step(n, s, r):
                    if live(n, NG):
                        pe.wait_ge(oht_ready, n + 1)
                        pe.wait_ge(pre_loaded[s], 48 * r + 48)
                        if live(n - 2, NG):
                            pe.wait_ge(sums_ready, n - 1)
                        for t in range(TPG):
                            col = (t % 4) * F
                            mm = pe.matmul(ps[:, 2 * s + t // 4, col:col + F],
                                           onehot_t[s][:, t * P:t * P + P], bwin[s][:, t // 4, :],
                                           start=True, stop=True)
                        mm.then_inc(pre_mm, 1)
                    if live(n - 1, NG):
                        pe.wait_ge(relu_done, n)
                        if general:
                            hold(pe)
                            with pe.Fori(0, NW) as w:
                                pe.wait_ge(win2_ready, (n - 1) * NW + w + 1)
                                for c in range(2):
                                    for t in range(TPG):
                                        mm = pe.matmul(
                                            ps[:, 4, c * W:c * W + W],
                                            hrelu[1 - s][:, t, :] if c == 0 else ones[:],
                                            onehot[1 - s][:, t, :], start=(t == 0),
                                            stop=(t == TPG - 1))
                                mm.then_inc(win2_done, 1)
                            pe.sem_inc(seg2_done, 1)
                            return
                        if live(n - 3, NG):
                            pe.wait_ge(acc2_add, 2 * n - 4)
                        for h in range(2):
                            for c in range(2):
                                for t in range(4 * h, 4 * h + 4):
                                    col = (2 * h + c) * W
                                    mm = pe.matmul(
                                        ps[:, 4 + (1 - s), col:col + W],
                                        hrelu[1 - s][:, t, :] if c == 0 else ones[:],
                                        onehot[1 - s][:, t, :], start=(t == 4 * h),
                                        stop=(t == 4 * h + 3))
                        mm.then_inc(seg2_done, 1)
                run_steps(pe, NG, 1, 4, step)

            general = pe.value_load(gen_i[0:1, 0:1], min_val=0, max_val=1)
            with pe.If(general == 1):
                layer2(True)
            with pe.Else():
                layer2(False)

            pe.wait_ge(acc2_all, 1)
            pe.wait_ge(x1t_kept, NC)

            def update(n, s, r):
                cols = bass.ds(n * CHUNK, CHUNK)
                if live(n, NC):
                    if live(n - 2, NC):
                        pe.wait_ge(agg_ready, n - 1)
                    pe.matmul(ps[:, s, :], m_w2[:], acc[:, 0, cols], start=True, stop=False)
                    pe.matmul(ps[:, s, :], mb2[:], acc[0:1, 1, cols], start=False,
                              stop=True).then_inc(pa_mm, 1)
                    pe.wait_ge(agg_ready, n + 1)
                    if live(n - 2, NC):
                        pe.wait_ge(hu_ready, n - 1)
                    pe.matmul(ps[:, 2 + s, :], u_w1[:, 0, :], x1T[:, cols], start=True, stop=False)
                    pe.matmul(ps[:, 2 + s, :], u_w1[:, 1, :], agg_t[s], start=False,
                              stop=True).then_inc(ph_mm, 1)
                if live(n - 1, NC):
                    pe.wait_ge(hu_ready, n)
                    if live(n - 3, NC):
                        pe.wait_ge(t_part, n - 2)
                    for q in range(4):
                        mm = pe.matmul(ps[:, 4 + (1 - s), q * F:q * F + F],
                                       h_u[1 - s][:, q * P:q * P + P], u_w2[:], start=True,
                                       stop=True)
                    mm.then_inc(pu_mm, 1)
            run_steps(pe, NC, 2, 4, update)

        @block.vector
        def _(dve):
            for t in (w_up, w0, w1, w_out):
                dve.memset(t[:], 0.0).then_inc(cleared, 1)
            dve.memset(ones[:], 1.0)
            dve.memset(ones_bf[:], 1.0)
            dve.memset(acc[:], 0.0).then_inc(acc_cleared, 1)
            dve.wait_ge(pool_consts, 4)
            dve.tensor_copy(iota_n[:], iota_i[:])
            dve.tensor_copy(iota_p[:], part_i[:, 0:1])
            dve.tensor_scalar(part_i[:, 1:2], part_i[:, 0:1], NB - 1, None,
                              ALU.bitwise_and).then_inc(dprep, 1)
            dve.wait_ge(dprep, 1)
            dve.tensor_copy(center[:], part_i[:, 1:2]).then_inc(dprep, 1)
            dve.wait_ge(dprep, 2)
            dve.tensor_scalar(center[:], center[:], -1.0, None, ALU.mult).then_inc(consts, 1)

            dve.wait_ge(drow_in, 16)
            dve.tensor_copy(drow, drow_i).then_inc(dprep, 1)
            dve.wait_ge(dprep, 3)
            halves = drow.rearrange("g (h e) -> g h e", h=2)
            dve.tensor_reduce(small[0:NG, 0:2], halves, AX, ALU.min).then_inc(dprep, 1)
            dve.tensor_reduce(small[0:NG, 2:4], halves, AX, ALU.max).then_inc(dprep, 1)
            dve.wait_ge(dprep, 5)
            dve.tensor_copy(small_i[0:NG, 0:2], small[0:NG, 0:2])
            dve.tensor_tensor(small[0:NG, 4:6], small[0:NG, 2:4], small[0:NG, 0:2],
                              ALU.subtract).then_inc(dprep, 1)
            dve.wait_ge(dprep, 6)
            dve.tensor_reduce(small[0:NG, 6:7], small[0:NG, 4:6], AX, ALU.max).then_inc(
                ranges_ready, 1)
            dve.tensor_tensor(rel_row.rearrange("g (h e) -> g h e", h=2), halves,
                              along(small[0:NG, 0:2], 2, HALF), ALU.subtract).then_inc(dprep, 1)

            dve.wait_ge(evec_in, 16)
            dve.tensor_tensor(evec_sq, rhat[:], rhat[:], ALU.mult).then_inc(vprep, 1)
            dve.wait_ge(vprep, 1)
            dve.tensor_reduce(norm, evec_sq, AX, ALU.add).then_inc(norm_sq, 1)

            dve.wait_ge(ranges_in, 48)
            dve.tensor_reduce(small[:, 8:9], span_all, AX, ALU.max).then_inc(dprep, 1)
            dve.wait_ge(dprep, 8)
            dve.tensor_scalar(gen_col[:, 0:1], small[:, 8:9], float(W), None,
                              ALU.is_ge).then_inc(dprep, 1)
            dve.wait_ge(dprep, 9)
            dve.tensor_copy(gen_i[:], gen_col[0:1, 0:1]).then_inc(gen_ready, 1)
            dve.tensor_scalar(gen_col[:, 1:2], gen_col[:, 0:1], -1.0, 1.0, ALU.mult,
                              ALU.add).then_inc(dprep, 1)
            dve.wait_ge(dprep, 10)
            dve.tensor_scalar(rel_row, rel_row, gen_col[0:NG, 1:2], gen_col[0:NG, 0:1], ALU.mult,
                              ALU.subtract).then_inc(rel_ready, 1)
            dve.wait_ge(dcol_in, 16)
            dve.tensor_copy(dcol[:], dcol_i).then_inc(dprep, 1)
            dve.wait_ge(dprep, 11)
            dve.tensor_tensor(rel[:], dcol[:].rearrange("p (h t) -> p h t", t=4),
                              along(base_all, 2, 4), ALU.subtract).then_inc(dprep, 1)

            dve.wait_ge(weights_in, 16 * N_WEIGHTS)
            dve.tensor_scalar(w0[:], w0[:], float(NB) ** 0.5, None, ALU.mult)
            dve.tensor_scalar(w_out[:], w_out[:], OUT_SCALE, None, ALU.mult).then_inc(vprep, 1)
            dve.wait_ge(vprep, 2)
            for rows, c in ((slice(64, 96), 0), (slice(0, 32), 1), (slice(64, 96), 1)):
                dve.tensor_scalar(w_out[rows, c, :], w_out[rows, c, :], SQ3, None, ALU.mult)
            dve.memset(eps[:], LN_EPS)
            dve.tensor_copy(b2_part[:, 0, :], b2_row[:]).then_inc(consts, 1)
            dve.wait_ge(consts, 2)
            for k in range(2):
                dve.tensor_tensor(b2_row[:], b2_row[:], b2_part[:, k, :], ALU.subtract).then_inc(
                    b2_split, 1)
                dve.wait_ge(b2_split, 2 * k + 1)
                dve.tensor_copy(b2_part[:, k + 1, :], b2_row[:]).then_inc(b2_split, 1)
                dve.wait_ge(b2_split, 2 * k + 2)
            dve.sem_inc(b2_split, 1)

            dve.wait_ge(norm_ready, 1)
            dve.tensor_scalar(norm, norm, 1e-12, None, ALU.add).then_inc(vprep, 1)
            dve.wait_ge(vprep, 3)
            dve.reciprocal(inv, norm).then_inc(vprep, 1)
            dve.wait_ge(vprep, 4)
            dve.tensor_tensor(rhat[:], rhat[:], along(inv, 2, 3), ALU.mult).then_inc(vprep, 1)

            def clip(n, s, r):
                dve.wait_ge(r_loaded[s], 16 * r + 16)
                if live(n - 2, NE):
                    dve.wait_ge(emb_mm, n - 1)
                dve.tensor_scalar(r_far[s], r_in[s], 1.0, 1000.0, ALU.is_gt, ALU.mult).then_inc(
                    r_prep, 1)
                dve.tensor_scalar(r_in[s], r_in[s], 0.0, 1.0, ALU.max, ALU.min).then_inc(r_prep, 1)
                dve.wait_ge(r_prep, 2 * n + 2)
                dve.tensor_tensor(r_far[s], r_far[s], r_in[s], ALU.add).then_inc(r_ready, 1)
            run_steps(dve, NE, 0, 2, clip)

            dve.wait_ge(vprep, 5)
            dve.wait_ge(dprep, 12)

            def build_onehot(n, s):
                dve.tensor_tensor(
                    onehot[s][:], along(iota_n[:], 1, TPG),
                    along(rel[:].rearrange("p h t -> p (h t)")[:, bass.ds(n * TPG, TPG)], 2, W),
                    ALU.is_equal)

            def all_windows(n, s, bank, step_sem, ready_sem, done_sem):
                dve.tensor_copy(relw[:], dcol[:, bass.ds(n * TPG, TPG)]).then_inc(step_sem, 1)
                with dve.Fori(0, NW) as w:
                    dve.wait_ge(step_sem, n * (NW + 1) + w + 1)
                    dve.tensor_tensor(onehot[s][:], along(iota_n[:], 1, TPG),
                                      along(relw[:], 2, W), ALU.is_equal).then_inc(ready_sem, 1)
                    dve.tensor_scalar(relw[:], relw[:], -float(W), None, ALU.add).then_inc(
                        step_sem, 1)
                    dve.wait_ge(done_sem, n * NW + w + 1)
                    win = acc[:, :, bass.ds(w * W, W)]
                    dve.tensor_tensor(win, win, ps[:, bank, 0:2 * W].rearrange(
                        "p (c n) -> p c n", c=2), ALU.add)

            def add_windows(n, s, bank, add_sem):
                for h in range(2):
                    base = dve.value_load(base_sb[0:1, bass.ds(n * 2 + h, 1)], min_val=0,
                                          max_val=NP - W)
                    if h == 1 or live(n - 1, NG):
                        dve.wait_ge(add_sem, n * 2 + h)
                    win = acc[:, :, bass.ds(base, W)]
                    dve.tensor_tensor(win, win, ps[:, bank, 2 * W * h:2 * W * h + 2 * W].rearrange(
                        "p (c n) -> p c n", c=2), ALU.add).then_inc(add_sem, 1)

            VS = 6

            def messages(n, s, r, general):
                if live(n - 2, NG) and not general:
                    dve.wait_ge(seg_done, n - 1)
                if not general:
                    build_onehot(n, s)
                m = mid[s][:]
                vec = m[:, :, 2 * MUL:].rearrange("p t (c u k) -> p t c u k", c=3, u=2)
                w = ps[:, 2 + 2 * s:4 + 2 * s, :].rearrange("p b (t f) -> p (b t) f", t=4)
                xs, xv = gx[s][:, :, 0:MUL], gx[s][:, :, MUL:].rearrange(
                    "p t (c k) -> p t c k", c=3)
                unit = along(rhat[:, bass.ds(n * TPG, TPG), :], 3, MUL)
                dve.wait_ge(gathered[s], 128 * r + 128)
                dve.tensor_tensor(prod[:], xv, unit, ALU.mult).then_inc(vstep, 1)
                dve.wait_ge(w_mm, n + 1)
                dve.tensor_tensor(m[:, :, 0:2 * MUL].rearrange("p t (u k) -> p t u k", u=2),
                                  w[:, :, 0:2 * MUL].rearrange("p t (u k) -> p t u k", u=2),
                                  along(xs, 2, 2), ALU.mult).then_inc(vstep, 1)
                dve.wait_ge(vstep, n * VS + 1)
                dve.tensor_tensor(dot[:], prod[:, :, 0, :], prod[:, :, 1, :], ALU.add).then_inc(
                    vstep, 1)
                dve.wait_ge(vstep, n * VS + 2)
                dve.tensor_tensor(vec[:, :, :, 0, :], along(m[:, :, MUL:2 * MUL], 2, 3), unit,
                                  ALU.mult).then_inc(vstep, 1)
                dve.wait_ge(vstep, n * VS + 3)
                dve.tensor_tensor(dot[:], dot[:], prod[:, :, 2, :], ALU.add).then_inc(vstep, 1)
                dve.tensor_tensor(vec[:, :, :, 1, :], along(w[:, :, 2 * MUL:3 * MUL], 2, 3), xv,
                                  ALU.mult).then_inc(vstep, 1)
                dve.wait_ge(vstep, n * VS + 5)
                dve.tensor_tensor(m[:, :, MUL:2 * MUL], w[:, :, 3 * MUL:], dot[:],
                                  ALU.mult).then_inc(mid_ready, 1)

            def layer1(general):
                def step(n, s, r):
                    if live(n, NG):
                        messages(n, s, r, general)
                        if general:
                            all_windows(n, s, 6, relw_step, win_ready, win_done)
                    if live(n - 1, NG) and not general:
                        dve.wait_ge(seg_done, n)
                        add_windows(n - 1, 1 - s, 6 + (1 - s), acc_add)
                run_steps(dve, NG, 1, 4, step)

            dve.wait_ge(acc_cleared, 1)
            general = dve.value_load(gen_i[0:1, 0:1], min_val=0, max_val=1)
            with dve.If(general == 1):
                layer1(True)
            with dve.Else():
                layer1(False)
            dve.engine_nop().then_inc(acc_all, 1)

            def norm_stats(src, st, mv, bn_sem, mv_sem, n):
                for q in range(4):
                    dve.bn_stats(st[:, q, :], src[:, q, :]).then_inc(bn_sem, 1)
                dve.wait_ge(bn_sem, 4 * n + 4)
                hold(dve)
                for q in range(4):
                    dve.bn_aggr(mv[:, q, :], st[:, q, :]).then_inc(mv_sem, 1)

            def normalize(dst, src, mv, rstd, done):
                for q in range(4):
                    dve.tensor_scalar(dst[:, q, :], src[:, q, :], mv[:, q, 0:1], rstd[:, q:q + 1],
                                      ALU.subtract, ALU.mult).then_inc(done, 1)

            def nodes(n, s, r):
                if live(n, NC):
                    dve.wait_ge(po_mm, n + 1)
                    dve.wait_ge(xin_loaded[s], 16 * r + 16)
                    po = quad(ps[:, s, :])
                    dve.tensor_tensor(y[s][:, :, 0:MUL], po[:, :, 0:MUL], xin[s][:, :, 0:MUL],
                                      ALU.add).then_inc(y_ready, 1)
                    dve.tensor_tensor(
                        y[s][:, :, MUL:].rearrange("p q (k c) -> p q c k", c=3),
                        po[:, :, MUL:].rearrange("p q (c k) -> p q c k", c=3),
                        xin[s][:, :, MUL:].rearrange("p q (k c) -> p q c k", c=3),
                        ALU.add).then_inc(y_ready, 1)
                    dve.wait_ge(y_ready, 2 * n + 2)
                    norm_stats(y[s], stats[s], mean_var[s], bn_done, var_ready, n)
                    dve.wait_ge(var_ready, 4 * n + 4)
                    dve.tensor_scalar(mean_var[s][:, :, 1], mean_var[s][:, :, 1], LN_EPS, None,
                                      ALU.add).then_inc(mv_ready, 4)
                if live(n - 1, NC):
                    dve.wait_ge(std_ready, n)
                    dve.reciprocal(std[1 - s][:], std[1 - s][:]).then_inc(rstd_ready, 1)
                    dve.wait_ge(rstd_ready, n)
                    if live(n - 3, NC):
                        dve.wait_ge(x1t_mm, n - 2)
                        dve.wait_ge(x1_kept, n - 2)
                    normalize(x1s[1 - s], y[1 - s], mean_var[1 - s], std[1 - s], x1_ready)
                if live(n - 2, NC):
                    dve.wait_ge(tab_mm, n - 1)
                    if live(n - 4, NC):
                        dve.wait_ge(tab_stored[s], 32 * r - 32)
                    dve.tensor_tensor(tab[s][:, :, F:2 * F], quad(ps[:, 5 + 2 * s, :]),
                                      along(mb1[:], 1, 4), ALU.add).then_inc(tab_b, 1)
            run_steps(dve, NC, 2, 4, nodes)

            dve.wait_ge(msum_ready, NC)
            dve.memset(acc[:], 0.0).then_inc(acc_cleared, 1)

            def layer2(general):
                def step(n, s, r):
                    if live(n, NG):
                        dve.wait_ge(relb_loaded[s], 16 * r + 16)
                        if live(n - 2, NG):
                            dve.wait_ge(pre_mm, n - 1)
                        dve.tensor_scalar(onehot_t[s][0:W, :], relb[s], iota_p[0:W, 0:1], None,
                                          ALU.is_equal).then_inc(oht_ready, 1)
                        if not general:
                            if live(n - 2, NG):
                                dve.wait_ge(seg2_done, n - 1)
                            build_onehot(n, s)
                        dve.wait_ge(gathered2[s], 128 * r + 128)
                        dve.wait_ge(pre_mm, n + 1)
                        if live(n - 2, NG):
                            dve.wait_ge(relu_done, n - 1)
                        pre = ps[:, 2 * s:2 * s + 2, :].rearrange("p b (t f) -> p (b t) f", t=4)
                        add = dve.tensor_tensor(sums[s], pre, gx[s][:], ALU.add)
                        if general:
                            add.then_inc(sum_step, 1)
                            dve.wait_ge(sum_step, n + 1)
                            add = dve.tensor_tensor(sums[s], sums[s], gb[s], ALU.add)
                        add.then_inc(sums_ready, 1)
                        if general:
                            all_windows(n, s, 4, relw2_step, win2_ready, win2_done)
                    if live(n - 1, NG) and not general:
                        dve.wait_ge(seg2_done, n)
                        add_windows(n - 1, 1 - s, 4 + (1 - s), acc2_add)
                run_steps(dve, NG, 1, 4, step)

            dve.wait_ge(acc_cleared, 2)
            with dve.If(general == 1):
                layer2(True)
            with dve.Else():
                layer2(False)
            dve.engine_nop().then_inc(acc2_all, 1)
            dve.wait_ge(acc2_all, 1)

            def update(n, s, r):
                if live(n, NC):
                    cols = bass.ds(n * CHUNK, CHUNK)
                    dve.tensor_scalar(cnt_inv[s], acc[:, 1, cols], 1.0, None, ALU.max).then_inc(
                        cnt_max, 1)
                    dve.wait_ge(cnt_max, n + 1)
                    dve.reciprocal(cnt_inv[s], cnt_inv[s]).then_inc(cnt_ready, 1)
                    dve.wait_ge(pa_mm, n + 1)
                    dve.wait_ge(cnt_ready, n + 1)
                    if live(n - 2, NC):
                        dve.wait_ge(ph_mm, n - 1)
                    dve.tensor_tensor(agg_t[s], ps[:, s, :], cnt_inv[s], ALU.mult).then_inc(
                        agg_ready, 1)
                if live(n - 1, NC):
                    o = 1 - s
                    dve.wait_ge(pu_mm, n)
                    dve.tensor_tensor(t_sum[o], quad(ps[:, 4 + o, :]), along(ub2[:], 1, 4),
                                      ALU.add).then_inc(t_part, 1)
                    dve.wait_ge(t_part, n)
                    dve.tensor_tensor(t_sum[o], t_sum[o], x1n[:, bass.ds((n - 1) * 4, 4), :],
                                      ALU.add).then_inc(t_ready, 1)
                    dve.wait_ge(t_ready, n)
                    norm_stats(t_sum[o], stats[o], mean_var[o], bna, var_a, n - 1)
                    dve.wait_ge(var_a, 4 * n)
                    dve.tensor_scalar(mean_var[o][:, :, 1], mean_var[o][:, :, 1], LN_EPS, None,
                                      ALU.add).then_inc(mva, 4)
                if live(n - 2, NC):
                    dve.wait_ge(zx, n - 1)
                    norm_stats(z[s], stats_b[s], mean_var_b[s], bnb, var_b, n - 2)
                    dve.wait_ge(var_b, 4 * n - 4)
                    dve.tensor_scalar(mean_var_b[s][:, :, 1], mean_var_b[s][:, :, 1], LN_EPS, None,
                                      ALU.add).then_inc(mvb, 4)
                if live(n - 1, NC):
                    o = 1 - s
                    dve.wait_ge(stda, n)
                    dve.reciprocal(std[o][:], std[o][:]).then_inc(rstda, 1)
                    dve.wait_ge(rstda, n)
                    normalize(z[o], t_sum[o], mean_var[o], std[o], z_ready)
                if live(n - 2, NC):
                    dve.wait_ge(stdb, n - 1)
                    dve.reciprocal(std_b[s][:], std_b[s][:]).then_inc(rstdb, 1)
                    dve.wait_ge(rstdb, n - 1)
                    if live(n - 4, NC):
                        dve.wait_ge(out_stored[s], 16 * r - 16)
                    normalize(res[s], z[s], mean_var_b[s], std_b[s], res_ready)
            run_steps(dve, NC, 2, 4, update)
    return nc


def kernel(**inputs):
    import numpy as np
    import concourse.bacc as bacc
    from concourse.bass_utils import run_bass_kernel_spmd

    given = {k: np.ascontiguousarray(v) for k, v in inputs.items()}

    def pad(x, n, value=0):
        fill = np.full((n - x.shape[0],) + x.shape[1:], value, x.dtype)
        return np.concatenate([x, fill])

    x = pad(given["x"], NP)
    order = np.concatenate([np.arange(MUL)] + [MUL + 3 * np.arange(MUL) + c for c in range(3)])
    src, dst = pad(given["src"], EP), pad(given["dst"], EP, N)

    def by_tile(v):
        return v.reshape(NT, P, *v.shape[1:]).swapaxes(0, 1)

    def ids(v):
        return v.reshape(NG, TPG, P).transpose(0, 2, 1)

    arrays = {
        "x_t": x[:, order].T,
        "x_rows": x,
        "ids": np.concatenate([ids(src), ids(dst)], axis=2).reshape(NG * P, 2 * TPG),
        "dst_row": dst.reshape(NG, GROUP),
        "dst_col": by_tile(dst),
        "evec": by_tile(pad(given["edge_attr_3"], EP)),
        "lengths": pad(given["edge_weight"], EP).reshape(NH, HALF),
        "attr2": pad(given["edge_attr_2"], EP).reshape(NG, GROUP, 2).transpose(0, 2, 1).reshape(
            2 * NG, GROUP),
    }
    for name, key in (("w_up0", "L0_gnn_W_up0"), ("w_up1", "L0_gnn_W_up1"),
                      ("mlp_w0", "L0_gnn_mlp_w0"), ("mlp_b0", "L0_gnn_mlp_b0"),
                      ("mlp_w1", "L0_gnn_mlp_w1"), ("mlp_b1", "L0_gnn_mlp_b1"),
                      ("mlp_w2", "L0_gnn_mlp_w2"), ("mlp_b2", "L0_gnn_mlp_b2"),
                      ("w_out0", "L0_gnn_W_out0"), ("w_out1", "L0_gnn_W_out1"),
                      ("m_w1", "L1_gnn_mW1"), ("mb1", "L1_gnn_mb1"), ("m_w2", "L1_gnn_mW2"),
                      ("mb2", "L1_gnn_mb2"), ("u_w1", "L1_gnn_uW1"), ("ub1", "L1_gnn_ub1"),
                      ("u_w2", "L1_gnn_uW2"), ("ub2", "L1_gnn_ub2"), ("gamma", "L1_gnn_gamma"),
                      ("beta", "L1_gnn_beta")):
        arrays[name] = given[key]
    arrays = {f"in_{k}": np.ascontiguousarray(v) for k, v in arrays.items()}

    nc = bacc.Bacc("TRN2", target_bir_lowering=False, num_devices=1)
    a = {k[3:]: nc.dram_tensor(k, v.shape, mybir.dt.from_np(v.dtype), kind="ExternalInput").ap()
         for k, v in arrays.items()}
    out = nc.dram_tensor("out_rows", [NP, F], F32, kind="ExternalOutput").ap()
    gnn_kernel(nc, a, out)
    r = run_bass_kernel_spmd(nc, [arrays], core_ids=[0])
    return r.results[0]["out_rows"][:N]
```

```python
from contextlib import ExitStack

import concourse.bass as bass
from concourse import mybir

F32 = mybir.dt.float32
BF16 = mybir.dt.bfloat16
I32 = mybir.dt.int32
ALU = mybir.AluOpType
ACT = mybir.ActivationFunctionType
AX = mybir.AxisListType.X

P = 128
N = 6250
E = 106250
F = 128
MUL = 32
NB = 8
HID = 64
TPG = 8
GROUP = TPG * P
NG = -(-E // GROUP)
EP = NG * GROUP
NT = NG * TPG
W = 128
WR = W - 2
HALF = GROUP // 2
NH = 2 * NG
CHUNK = 512
NC = -(-(N + W) // CHUNK)
NP = NC * CHUNK
NW = NP // W
EMB_STEP = P // NB
NE = NH // EMB_STEP
EMB_AHEAD = 2
EMB_GROUPS = EMB_STEP // 2
HEAD = -(-NE // 2) * 2
LN_EPS = 1e-5
SQ3 = 3.0 ** 0.5
OUT_SCALE = 1.0 / ((2 * MUL) ** 0.5 * 16.0)
assert NH % EMB_STEP == 0 and NG % 2 == 0


def along(ap, axis, n):
    shape = list(ap.shape)
    return ap.unsqueeze(axis).broadcast_to(shape[:axis] + [n] + shape[axis:])


def run_steps(eng, steps, lag, head, step, slots=2):
    assert head % slots == 0
    for n in range(head):
        step(n, n % slots, n // slots)
    loops = (steps - head) // slots
    with eng.Fori(0, loops) as i:
        for s in range(slots):
            step(i * slots + (head + s), s, i + head // slots)
    for n in range(head + slots * loops, steps + lag):
        step(n, n % slots, n // slots)


def last(steps, slots, s):
    return (steps + slots - 1 - s) // slots


def live(n, steps):
    return not isinstance(n, int) or 0 <= n < steps


def gnn_kernel(nc, a, out):
    with ExitStack() as ctx:
        def sb(name, shape, dt=F32):
            return ctx.enter_context(nc.sbuf_tensor(name, shape, dt))

        def sem(name):
            return ctx.enter_context(nc.semaphore(name))

        def pair(name):
            return [sem(f"{name}{s}") for s in range(2)]

        def dram(name, shape, dt=F32):
            return nc.dram_tensor(name, shape, dt).ap()

        x_table = dram("x_table", [NP, F])
        src_table = dram("src_table", [NP, F])
        dst_table = dram("dst_table", [NP, F])
        emb_d = [dram(f"emb_d{k}", [NH * NB, HALF], BF16) for k in range(3)]
        rel_d = dram("rel_d", [NG, GROUP], BF16)
        base_i_d = dram("base_i_d", [NG, 1], I32)
        base_f_d = dram("base_f_d", [NG, 1])
        cnt_d = dram("cnt_d", [1, NP])
        cnt_inv_d = dram("cnt_inv_d", [1, NP])
        span_d = dram("span_d", [NG, 1])
        b2_parts_d = dram("b2_parts_d", [1, 3 * F], BF16)

        ps = ctx.enter_context(nc.psum_tensor("ps", [P, 8, 512], F32))

        acc = sb("acc", [P, 2, NP])
        x1n = sb("x1n", [P, NC * 4, F])
        x1T = sb("x1T", [P, NP])
        rhat = sb("rhat", [P, NT, 3])
        rel = sb("rel", [P, NT])
        dcol = sb("dcol", [P, NT])
        base_sb = sb("base_sb", [1, NG], I32)
        gen_i = sb("gen_i", [1, 1], I32)
        w_up = sb("w_up", [P, F])
        w0 = sb("w0", [2 * NB, P])
        w1 = sb("w1", [P, P])
        w0_part = sb("w0_part", [2 * NB, 3, P], BF16)
        w0_all = sb("w0_all", [P, P], BF16)
        w2 = sb("w2", [P, 2, F])
        b0 = sb("b0", [P, 1])
        b1 = sb("b1", [P, 1])
        b2_row = sb("b2_row", [1, F])
        b2_part = sb("b2_part", [1, 3, F], BF16)
        b2p = sb("b2p", [3, 4, F], BF16)
        ones_bf = sb("ones_bf", [P, P], BF16)
        w_out = sb("w_out", [P, 2, 2 * MUL])
        m_w1 = sb("m_w1", [P, 2, F])
        mb1 = sb("mb1", [P, F])
        m_w2 = sb("m_w2", [P, F])
        mb2 = sb("mb2", [1, F])
        u_w1 = sb("u_w1", [P, 2, F])
        ub1 = sb("ub1", [P, 1])
        u_w2 = sb("u_w2", [P, F])
        ub2 = sb("ub2", [P, F])
        gamma = sb("gamma", [P, F])
        beta = sb("beta", [P, F])
        ones = sb("ones", [P, P])
        ident = sb("ident", [P, P])
        iota_i = sb("iota_i", [P, W], I32)
        iota_n = sb("iota_n", [P, W])
        part_i = sb("part_i", [P, 2], I32)
        iota_p = sb("iota_p", [P, 1])
        center = sb("center", [P, 1])
        eps = sb("eps", [P, 1])
        zero = sb("zero", [P, 1])
        gen_col = sb("gen_col", [P, 2])
        ids = [sb(f"ids{s}", [P, 2 * TPG], I32) for s in range(2)]
        gx = [sb(f"gx{s}", [P, TPG, F]) for s in range(2)]
        mid = [sb(f"mid{s}", [P, TPG, 2 * F]) for s in range(2)]
        onehot = [sb(f"onehot{s}", [P, TPG, W]) for s in range(2)]
        onehot_b = [sb(f"onehot_b{s}", [P, TPG, W], BF16) for s in range(2)]
        relw = sb("relw", [P, TPG])
        emb_in = [sb(f"emb_in{s}", [P, HALF], BF16) for s in range(2)]
        hid = [sb(f"hid{s}", [P, 2, HALF]) for s in range(2)]
        prod = sb("prod", [P, TPG, 3, MUL])
        dot = sb("dot", [P, TPG, MUL])
        onehot_t = [sb(f"onehot_t{s}", [P, GROUP]) for s in range(2)]
        rel_in = [sb(f"rel_in{s}", [1, GROUP], BF16) for s in range(2)]
        bwin = [sb(f"bwin{s}", [P, F]) for s in range(2)]
        hrelu = [sb(f"hrelu{s}", [P, TPG, F]) for s in range(2)]
        stats = [sb(f"stats{s}", [P, 4, 6]) for s in range(2)]
        mean_var = [sb(f"mean_var{s}", [P, 4, 2]) for s in range(2)]
        std = [sb(f"std{s}", [P, 4]) for s in range(2)]
        stats_b = [sb(f"stats_b{s}", [P, 4, 6]) for s in range(2)]
        mean_var_b = [sb(f"mean_var_b{s}", [P, 4, 2]) for s in range(2)]
        std_b = [sb(f"std_b{s}", [P, 4]) for s in range(2)]
        shift = [sb(f"shift{s}", [P, 4]) for s in range(2)]
        shift_b = [sb(f"shift_b{s}", [P, 4]) for s in range(2)]
        cnt_cols = sb("cnt_cols", [P, NP // P])

        def flat(t):
            return t[:].rearrange("p a b -> p (a b)")

        def quad(ap):
            return ap.rearrange("p (q f) -> p q f", f=F)

        x1n_flat = x1n[:].rearrange("p a b -> p (a b)")
        evec_sq = x1n_flat[:, 0:3 * NT].rearrange("p (t c) -> p t c", c=3)
        norm = x1n_flat[:, 3 * NT:4 * NT]
        inv = x1n_flat[:, 4 * NT:5 * NT]
        dcol_i = x1n_flat[:, 5 * NT:6 * NT].bitcast(I32)
        drow_i = x1T[0:NG, 0:GROUP].bitcast(I32)
        drow = x1T[0:NG, GROUP:2 * GROUP]
        rel_row = x1T[0:NG, 2 * GROUP:3 * GROUP]
        rel_row_b = x1T[0:NG, 3 * GROUP:3 * GROUP + GROUP // 2].bitcast(BF16)
        base_all = x1T[:, 3584:3584 + NG]
        span_all = x1T[:, 3712:3712 + NG]
        small = x1T[:, 3840:3856]
        small_i = x1T[:, 3856:3858].bitcast(I32)
        w0_rest = x1T[0:2 * NB, 3872:3872 + P]
        lengths = x1n_flat[0:NG, 6 * NT:6 * NT + GROUP]
        far = x1T[0:NG, 0:GROUP]
        expand = x1T[0:NG, 4000:4000 + NE * P + NB]
        emb_sq = [flat(hrelu[s])[:, 0:HALF] for s in range(2)]
        emb_rest = [flat(hrelu[s])[:, HALF:2 * HALF] for s in range(2)]
        emb_part = [[onehot_t[s][:, k * HALF // 2:(k + 1) * HALF // 2].bitcast(BF16)
                     for k in range(3)] for s in range(2)]
        mid_flat = [flat(mid[s]) for s in range(2)]
        xt_in = [quad(mid_flat[s // 2][:, (s % 2) * 512:(s % 2) * 512 + 512]) for s in range(4)]
        xt_stage = [quad(mid_flat[s // 2][:, 1024 + (s % 2) * 512:1536 + (s % 2) * 512])
                    for s in range(4)]
        msum = [flat(gx[s]).rearrange("p (c n) -> p c n", c=2) for s in range(2)]
        xin = [hrelu[s][:, 0:4, :] for s in range(2)]
        y = [hrelu[s][:, 4:8, :] for s in range(2)]
        x1s = [quad(mid_flat[s][:, 0:512]) for s in range(2)]
        x1Ts = [mid_flat[s][:, 512:1024] for s in range(2)]
        tab = [mid[s][:, 4:8, :] for s in range(2)]
        gb = [mid[s][:, :, 0:F] for s in range(2)]
        sums = [mid[s][:, :, F:2 * F] for s in range(2)]
        cnt_inv = [flat(gx[s])[:, 0:512] for s in range(2)]
        agg_t = [flat(gx[s])[:, 512:1024] for s in range(2)]
        h_u = [flat(hrelu[s])[:, 0:512] for s in range(2)]
        t_sum = [quad(mid_flat[s][:, 0:512]) for s in range(2)]
        z = [quad(mid_flat[s][:, 512:1024]) for s in range(2)]
        res = [quad(mid_flat[s][:, 1024:1536]) for s in range(2)]

        weights_in = sem("weights_in")
        cleared = sem("cleared")
        pool_consts = sem("pool_consts")
        consts = sem("consts")
        up_in, late_in = sem("up_in"), sem("late_in")
        xt_loaded = [sem(f"xt_loaded{s}") for s in range(4)]
        xt_stored = [sem(f"xt_stored{s}") for s in range(4)]
        xt_mm, xt_staged = sem("xt_mm"), sem("xt_staged")
        drow_in, dcol_in, evec_in = sem("drow_in"), sem("dcol_in"), sem("evec_in")
        dprep, ranges_ready, ranges_out, ranges_in = (
            sem("dprep"), sem("ranges_ready"), sem("ranges_out"), sem("ranges_in"))
        gen_ready, rel_ready, rel_out = sem("gen_ready"), sem("rel_ready"), sem("rel_out")
        norm_sq, norm_ready, vprep = sem("norm_sq"), sem("norm_ready"), sem("vprep")
        w0_split, w0_placed = sem("w0_split"), sem("w0_placed")
        b2_split, b2_out, b2_in = sem("b2_split"), sem("b2_out"), sem("b2_in")
        lengths_in, emb_stored = sem("lengths_in"), pair("emb_stored")
        r_prep, r_ready, emb_mm, emb_sqd, emb_ready, emb_cast, emb_split = (
            sem("r_prep"), sem("r_ready"), sem("emb_mm"), sem("emb_sqd"), sem("emb_ready"),
            sem("emb_cast"), sem("emb_split"))
        ids_loaded, emb_loaded, gathered = pair("ids_loaded"), pair("emb_loaded"), pair("gathered")
        h1_mm, h1_act, h2_mm, h2_act, w_mm = (
            sem("h1_mm"), sem("h1_act"), sem("h2_mm"), sem("h2_act"), sem("w_mm"))
        vstep, mid_ready, seg_done, acc_add, acc_all = (
            sem("vstep"), sem("mid_ready"), sem("seg_done"), sem("acc_add"), sem("acc_all"))
        relw_step, win_ready, win_done = sem("relw_step"), sem("win_ready"), sem("win_done")
        msum_ready, po_mm, y_ready, xin_loaded = (
            sem("msum_ready"), sem("po_mm"), sem("y_ready"), pair("xin_loaded"))
        bn_done, mv_ready, std_ready, rstd_ready, x1_ready = (
            sem("bn_done"), sem("mv_ready"), sem("std_ready"), sem("rstd_ready"), sem("x1_ready"))
        x1_kept, x1t_mm, x1t_copied, x1t_kept = (
            sem("x1_kept"), sem("x1t_mm"), sem("x1t_copied"), sem("x1t_kept"))
        tab_mm, tab_a, tab_b, tab_stored = (
            sem("tab_mm"), sem("tab_a"), sem("tab_b"), pair("tab_stored"))
        acc_cleared, var_a, var_b = sem("acc_cleared"), sem("var_a"), sem("var_b")
        zero_set = sem("zero_set")
        ids2_loaded, rel_loaded, pre_loaded, gathered2 = (
            pair("ids2_loaded"), pair("rel_loaded"), pair("pre_loaded"), pair("gathered2"))
        rel_spread, onehot_built = sem("rel_spread"), sem("onehot_built")
        gathered_b = pair("gathered_b")
        we_loaded = sem("we_loaded")
        oht_ready, pre_mm, sum_step, sums_ready, relu_done = (
            sem("oht_ready"), sem("pre_mm"), sem("sum_step"), sem("sums_ready"), sem("relu_done"))
        seg2_done, acc2_add, acc2_all = sem("seg2_done"), sem("acc2_add"), sem("acc2_all")
        relw2_step, win2_ready, win2_done = sem("relw2_step"), sem("win2_ready"), sem("win2_done")
        cnt_out, cnt_back, inv_out, inv_loaded = (
            sem("cnt_out"), sem("cnt_back"), sem("inv_out"), pair("inv_loaded"))
        cnt_max, cnt_ready, pa_mm, agg_ready, ph_mm, hu_ready, pu_mm = (
            sem("cnt_max"), sem("cnt_ready"), sem("pa_mm"), sem("agg_ready"), sem("ph_mm"),
            sem("hu_ready"), sem("pu_mm"))
        beta_ready = sem("beta_ready")
        t_ready, bna, stda, rstda, z_ready = (
            sem("t_ready"), sem("bna"), sem("stda"), sem("rstda"), sem("z_ready"))
        zg, zb, zx = sem("zg"), sem("zb"), sem("zx")
        bnb, stdb, rstdb, res_ready = sem("bnb"), sem("stdb"), sem("rstdb"), sem("res_ready")
        out_stored = pair("out_stored")

        passed = sem("passed")

        def hold(eng):
            eng.sem_inc(passed, 1)

        block = ctx.enter_context(nc.Block())

        N_WEIGHTS, N_LATE, N_COMBOS = 15, 12, 8
        combos = [(e, w) for e in range(3) for w in range(3)][:N_COMBOS]
        x_rows = a["x_rows"].rearrange("(q p) f -> p q f", p=P)
        x_table_rows = x_table.rearrange("(q p) f -> p q f", p=P)
        src_rows = src_table.rearrange("(q p) f -> p q f", p=P)
        dst_rows = dst_table.rearrange("(q p) f -> p q f", p=P)
        out_rows = out.rearrange("(q p) f -> p q f", p=P)

        @block.sync
        def _(sp):
            sp.wait_ge(cleared, 1)
            for c in range(4):
                sp.dma_start(w_up[32 * c:32 * c + 32, 32 * c:32 * c + 32],
                             a["w_up0" if c == 0 else "w_up1"]).then_inc(up_in, 16)

            def load_xt(n, s, r):
                if live(n - 4, NC):
                    sp.wait_ge(xt_mm, n - 3)
                sp.dma_start(xt_in[s], quad(a["x_t"][:, bass.ds(n * CHUNK, CHUNK)])).then_inc(
                    xt_loaded[s], 16)
                if isinstance(n, int) and n == 3:
                    sp.dma_start(drow_i, a["dst_row"]).then_inc(drow_in, 16)
                    sp.dma_start(lengths, a["lengths"]).then_inc(lengths_in, 16)
                    sp.dma_start(rhat[:], a["evec"]).then_inc(evec_in, 16)
                    sp.dma_start(dcol_i, a["dst_col"]).then_inc(dcol_in, 16)
                    for k in range(2):
                        sp.dma_start(ids[k][:], a["ids"][k * P:k * P + P, :]).then_inc(
                            ids_loaded[k], 16)
            run_steps(sp, NC, 0, 4, load_xt, slots=4)

            sp.wait_ge(ranges_ready, 1)
            sp.dma_start(base_f_d, small[0:NG, 0:1]).then_inc(ranges_out, 16)
            sp.dma_start(span_d, small[0:NG, 2:3]).then_inc(ranges_out, 16)
            sp.dma_start(base_i_d, small_i[0:NG, 0:1]).then_inc(ranges_out, 16)
            sp.wait_ge(ranges_out, 48)
            sp.dma_start(base_all, base_f_d.rearrange("g h -> (g h)").unsqueeze(0).broadcast_to(
                [P, NG])).then_inc(ranges_in, 16)
            sp.dma_start(span_all, span_d.rearrange("g h -> (g h)").unsqueeze(0).broadcast_to(
                [P, NG])).then_inc(ranges_in, 16)
            sp.dma_start(base_sb[:], base_i_d.rearrange("g h -> (g h)").unsqueeze(0)).then_inc(
                ranges_in, 16)

            sp.wait_ge(w0_split, 5)
            for b, (_, k) in enumerate(combos):
                sp.dma_start(w0_all[2 * NB * b:2 * NB * b + 2 * NB, :], w0_part[:, k, :]).then_inc(
                    w0_placed, 16)
            sp.wait_ge(b2_split, 5)
            sp.dma_start(b2_parts_d, b2_part[:].rearrange("o k f -> o (k f)")).then_inc(b2_out, 16)
            sp.wait_ge(b2_out, 16)
            parts = b2_parts_d.rearrange("o (k f) -> (o k) f", k=3)
            for q in range(4):
                sp.dma_start(b2p[:, q, :], parts).then_inc(b2_in, 16)
            sp.wait_ge(rel_ready, 1)
            sp.dma_start(rel_d, rel_row_b).then_inc(rel_out, 16)

            def load_edges(n, s, r):
                if isinstance(n, int) and n % EMB_GROUPS == 0:
                    sp.wait_ge(emb_stored[n // EMB_GROUPS], 48)
                if live(n - 2, NG):
                    sp.wait_ge(gathered[s], 128 * r)
                    sp.dma_start(ids[s][:], a["ids"][bass.ds(n * P, P), :]).then_inc(
                        ids_loaded[s], 16)
                    sp.wait_ge(h1_mm, n - 1)
                row = 0
                for e in range(3):
                    times = sum(c[0] == e for c in combos)
                    sp.dma_start(
                        emb_in[s][row:row + 2 * NB * times, :],
                        along(emb_d[e][bass.ds(n * 2 * NB, 2 * NB), :], 0, times)).then_inc(
                            emb_loaded[s], 16)
                    row += 2 * NB * times
                if isinstance(n, int) and n == 2 * EMB_GROUPS - 1:
                    for k in range(2):
                        sp.wait_ge(emb_stored[k], 48 * last(NE, 2, k))
            run_steps(sp, NG, 0, 2 * EMB_GROUPS, load_edges)

            def nodes(n, s, r):
                if live(n, NC):
                    if live(n - 2, NC):
                        sp.wait_ge(y_ready, 2 * n - 2)
                    sp.dma_start(xin[s], x_rows[:, bass.ds(n * 4, 4), :]).then_inc(
                        xin_loaded[s], 16)
                if live(n - 3, NC):
                    sp.wait_ge(tab_a, n - 2)
                    sp.wait_ge(tab_b, n - 2)
                    rows = bass.ds((n - 3) * 4, 4)
                    sp.dma_start(src_rows[:, rows, :], tab[1 - s][:, :, 0:F]).then_inc(
                        tab_stored[1 - s], 16)
                    sp.dma_start(dst_rows[:, rows, :], tab[1 - s][:, :, F:2 * F]).then_inc(
                        tab_stored[1 - s], 16)
            sp.wait_ge(acc_all, 1)
            run_steps(sp, NC, 3, 4, nodes)
            for s in range(2):
                sp.wait_ge(tab_stored[s], 32 * last(NC, 2, s))
                sp.dma_start(bwin[s][WR:P, :], a["m_w1"][2 * F:2 * F + 2, :]).then_inc(
                    we_loaded, 16)
            sp.wait_ge(rel_out, 16)

            def load_edges2(n, s, r):
                if live(n - 2, NG):
                    sp.wait_ge(gathered2[s], 128 * r)
                sp.dma_start(ids[s][:], a["ids"][bass.ds(n * P, P), :]).then_inc(
                    ids2_loaded[s], 16)
                if live(n - 2, NG):
                    sp.wait_ge(rel_spread, n - 1)
                sp.dma_start(rel_in[s][:], rel_d[bass.ds(n, 1), :]).then_inc(rel_loaded[s], 16)
                base = sp.value_load(base_sb[0:1, bass.ds(n, 1)], min_val=0, max_val=NP - W)
                if live(n - 2, NG):
                    sp.wait_ge(pre_mm, n - 1)
                sp.dma_start(onehot_t[s][WR:P, :], a["attr2"][bass.ds(n * 2, 2), :]).then_inc(
                    pre_loaded[s], 16)
                sp.dma_start(bwin[s][0:WR, :], dst_table[bass.ds(base, WR), :]).then_inc(
                    pre_loaded[s], 16)
            run_steps(sp, NG, 0, 2, load_edges2)

            sp.wait_ge(acc2_all, 1)
            sp.dma_start(cnt_d, acc[0:1, 1, :]).then_inc(cnt_out, 16)
            sp.wait_ge(cnt_out, 16)
            sp.dma_start(cnt_cols[:], cnt_d.rearrange("o (p k) -> (o p) k", p=P)).then_inc(
                cnt_back, 16)
            sp.wait_ge(cnt_ready, 1)
            sp.dma_start(cnt_inv_d.rearrange("o (p k) -> (o p) k", p=P), cnt_cols[:]).then_inc(
                inv_out, 16)
            sp.wait_ge(inv_out, 16)

            def last_loads(n, s, r):
                if live(n, NC):
                    if live(n - 2, NC):
                        sp.wait_ge(agg_ready, n - 1)
                    sp.dma_start(cnt_inv[s], cnt_inv_d[:, bass.ds(n * CHUNK, CHUNK)].broadcast_to(
                        [P, CHUNK])).then_inc(inv_loaded[s], 16)
                if live(n - 3, NC):
                    sp.wait_ge(res_ready, 4 * n - 8)
                    sp.dma_start(out_rows[:, bass.ds((n - 3) * 4, 4), :], res[1 - s]).then_inc(
                        out_stored[1 - s], 16)
            run_steps(sp, NC, 3, 4, last_loads)
            for s in range(2):
                sp.wait_ge(out_stored[s], 16 * last(NC, 2, s))

        @block.gpsimd
        def _(pool):
            pool.memset(ident[:], 0.0).then_inc(pool_consts, 1)
            pool.iota(iota_i[:], pattern=[[1, W]], base=0, channel_multiplier=0).then_inc(
                pool_consts, 1)
            pool.iota(part_i[:], pattern=[[0, 2]], base=0, channel_multiplier=1).then_inc(
                pool_consts, 1)
            def load(dst, src):
                pool.dma_start(dst, src).then_inc(weights_in, 16)

            pool.wait_ge(cleared, 5)
            load(b2_row[:], a["mlp_b2"].unsqueeze(0))
            load(w0[0:NB, 0:HID], a["mlp_w0"])
            load(w0[NB:2 * NB, HID:P], a["mlp_w0"])
            for h in range(2):
                rows = slice(h * HID, h * HID + HID)
                load(w1[rows, rows], a["mlp_w1"])
                load(w2[rows, h, :], a["mlp_w2"])
                load(b0[rows, :], a["mlp_b0"].unsqueeze(1))
                load(b1[rows, :], a["mlp_b1"].unsqueeze(1))
            load(w_out[0:64, 0, 0:32], a["w_out0"])
            load(w_out[64:128, 0, 32:64], a["w_out1"])
            load(w_out[0:64, 1, 0:32], a["w_out1"])
            load(w_out[64:128, 1, 32:64], a["w_out1"])
            columns = NE * P + NB
            pool.wait_ge(zero_set, 2)
            pool.affine_select(out=expand, in_=expand, compare_op=ALU.is_ge, fill=0.0, base=-NB,
                               pattern=[[1, columns]], channel_multiplier=-2 * NB).then_inc(
                                   pool_consts, 1)
            pool.wait_ge(pool_consts, 4)
            pool.affine_select(out=expand, in_=expand, compare_op=ALU.is_ge, fill=0.0,
                               base=2 * NB - 1, pattern=[[-1, columns]],
                               channel_multiplier=2 * NB).then_inc(pool_consts, 1)
            pool.affine_select(out=ident[:], in_=ident[:], compare_op=ALU.not_equal, fill=1.0,
                               base=0, pattern=[[-1, P]], channel_multiplier=1).then_inc(
                                   pool_consts, 1)
            pool.memset(acc[:], 0.0).then_inc(acc_cleared, 1)

            for s in range(4):
                pool.wait_ge(xt_stored[s], 16 * last(NC, 4, s))

            def gather(n, s, r):
                pool.wait_ge(ids_loaded[s], 16 * r + 16)
                if live(n - 2, NG):
                    pool.wait_ge(mid_ready, n - 1)
                    hold(pool)
                for t in range(TPG):
                    pool.indirect_dma_start(
                        out=gx[s][:, t, :], out_offset=None, in_=x_table,
                        in_offset=bass.IndirectOffsetOnAxis(ap=ids[s][:, t:t + 1], axis=0),
                    ).then_inc(gathered[s], 16)
            run_steps(pool, NG, 0, 2, gather)

            pool.wait_ge(late_in, 16 * N_LATE)
            def keep(n, s, r):
                pool.wait_ge(x1_ready, 4 * n + 4)
                pool.tensor_tensor(x1n[:, bass.ds(n * 4, 4), :], x1s[s], along(ub2[:], 1, 4),
                                   ALU.add).then_inc(x1_kept, 1)
                pool.wait_ge(x1t_copied, n + 1)
                pool.tensor_copy(x1T[:, bass.ds(n * CHUNK, CHUNK)], x1Ts[s]).then_inc(x1t_kept, 1)
            run_steps(pool, NC, 0, 2, keep)

            pool.wait_ge(x1_kept, NC)
            pool.wait_ge(x1t_kept, NC)
            for s in range(2):
                pool.wait_ge(tab_stored[s], 32 * last(NC, 2, s))

            def gathers2(general):
                def gather2(n, s, r):
                    pool.wait_ge(ids2_loaded[s], 16 * r + 16)
                    if live(n - 2, NG):
                        pool.wait_ge(sums_ready, n - 1)
                        hold(pool)
                    if general:
                        for t in range(TPG):
                            pool.indirect_dma_start(
                                out=gb[s][:, t, :], out_offset=None, in_=dst_table,
                                in_offset=bass.IndirectOffsetOnAxis(
                                    ap=ids[s][:, TPG + t:TPG + t + 1], axis=0),
                            ).then_inc(gathered_b[s], 16)
                        pool.wait_ge(gathered_b[s], 128 * r + 128)
                        hold(pool)
                    for t in range(TPG):
                        pool.indirect_dma_start(
                            out=gx[s][:, t, :], out_offset=None, in_=src_table,
                            in_offset=bass.IndirectOffsetOnAxis(ap=ids[s][:, t:t + 1], axis=0),
                        ).then_inc(gathered2[s], 16)
                run_steps(pool, NG, 0, 2, gather2)

            general = pool.value_load(gen_i[0:1, 0:1], min_val=0, max_val=1)
            with pool.If(general == 1):
                gathers2(True)
            with pool.Else():
                gathers2(False)

            pool.wait_ge(beta_ready, 1)

            def finish(n, s, r):
                pool.wait_ge(z_ready, 4 * n + 4)
                pool.tensor_tensor(z[s], z[s], along(gamma[:], 1, 4), ALU.mult).then_inc(zg, 1)
                pool.wait_ge(zg, n + 1)
                pool.tensor_tensor(z[s], z[s], along(beta[:], 1, 4), ALU.add).then_inc(zb, 1)
                pool.wait_ge(zb, n + 1)
                pool.tensor_tensor(z[s], z[s], x1n[:, bass.ds(n * 4, 4), :], ALU.add).then_inc(
                    zx, 1)
            run_steps(pool, NC, 0, 2, finish)

        @block.scalar
        def _(act):
            def stage_xt(n, s, r):
                act.wait_ge(xt_mm, n + 1)
                if live(n - 4, NC):
                    act.wait_ge(xt_stored[s], 16 * r)
                act.activation(xt_stage[s], quad(ps[:, s, :]), ACT.Copy,
                               scale=1.0 / MUL ** 0.5).then_inc(xt_staged, 1)
                act.wait_ge(xt_staged, n + 1)
                act.dma_start(x_table_rows[:, bass.ds(n * 4, 4), :], xt_stage[s]).then_inc(
                    xt_stored[s], 16)
            run_steps(act, NC, 0, 4, stage_xt, slots=4)

            act.wait_ge(consts, 1)

            def embed(k, s):
                act.wait_ge(emb_mm, k + 1)
                act.activation(emb_sq[s], ps[:, 0, :], ACT.Square, bias=center[:, 0:1],
                               scale=float(NB - 1)).then_inc(emb_sqd, 1)
                act.wait_ge(emb_sqd, k + 1)
                if k >= 2:
                    act.wait_ge(emb_split, 4 * k - 4)
                act.activation(emb_rest[s], emb_sq[s], ACT.Exp, scale=-0.5).then_inc(emb_ready, 1)

            def store(k, s):
                act.wait_ge(emb_split, 4 * k + 4)
                for part in range(3):
                    act.dma_start(emb_d[part][bass.ds(k * P, P), :],
                                  emb_part[s][part]).then_inc(emb_stored[s], 16)

            for k in range(EMB_AHEAD):
                embed(k, k)

            act.wait_ge(norm_sq, 1)
            act.activation(norm, norm, ACT.Sqrt).then_inc(norm_ready, 1)

            for k in range(EMB_AHEAD):
                store(k, k)

            act.preload_act_table(ACT.Silu)

            def mlp(n, s, r):
                if live(n - 1, NG):
                    act.wait_ge(h2_mm, n)
                    if live(n - 3, NG):
                        act.wait_ge(w_mm, n - 2)
                    act.activation(hid[1 - s][:, 1, :], ps[:, 1, :], ACT.Silu,
                                   bias=b1[:, 0:1]).then_inc(h2_act, 1)
                if live(n, NG):
                    act.wait_ge(h1_mm, n + 1)
                    if live(n - 2, NG):
                        act.wait_ge(h2_mm, n - 1)
                    act.activation(hid[s][:, 0, :], ps[:, 0, :], ACT.Silu,
                                   bias=b0[:, 0:1]).then_inc(h1_act, 1)
                if isinstance(n, int) and n + EMB_AHEAD < NE:
                    embed(n + EMB_AHEAD, s)
                if isinstance(n, int) and EMB_AHEAD <= n < NE:
                    store(n, s)
                if isinstance(n, int) and n == 1:
                    def load(dst, src):
                        act.dma_start(dst, src).then_inc(late_in, 16)

                    def rows(x):
                        return x.unsqueeze(0).broadcast_to([P, F])

                    for h in range(2):
                        load(m_w1[:, h, :], a["m_w1"][h * F:h * F + F, :])
                        load(u_w1[:, h, :], a["u_w1"][h * F:h * F + F, :])
                    load(mb1[:], rows(a["mb1"]))
                    load(m_w2[:], a["m_w2"])
                    load(mb2[:], a["mb2"].unsqueeze(0))
                    load(ub1[:], a["ub1"].unsqueeze(1))
                    load(u_w2[:], a["u_w2"])
                    load(ub2[:], rows(a["ub2"]))
                    load(gamma[:], rows(a["gamma"]))
                    load(beta[:], rows(a["beta"]))
            act.wait_ge(weights_in, 16 * N_WEIGHTS)
            run_steps(act, NG, 1, HEAD, mlp)

            act.preload_act_table(ACT.Sqrt)
            act.wait_ge(acc_all, 1)

            def nodes(n, s, r):
                if live(n, NC):
                    if live(n - 2, NC):
                        act.wait_ge(po_mm, n - 1)
                    act.copy(msum[s], acc[:, :, bass.ds(n * CHUNK, CHUNK)]).then_inc(msum_ready, 1)
                if live(n - 2, NC):
                    act.wait_ge(x1t_mm, n - 1)
                    if live(n - 4, NC):
                        act.wait_ge(tab_mm, n - 3)
                        act.wait_ge(x1t_kept, n - 3)
                    act.copy(x1Ts[s], ps[:, 2 + s, :]).then_inc(x1t_copied, 1)
                if live(n - 1, NC):
                    act.wait_ge(mv_ready, 4 * n)
                    act.activation(std[1 - s][:], mean_var[1 - s][:, :, 1], ACT.Sqrt,
                                   bias=eps[:, 0:1]).then_inc(std_ready, 1)
                if live(n - 3, NC):
                    act.wait_ge(tab_mm, n - 2)
                    if live(n - 5, NC):
                        act.wait_ge(tab_stored[1 - s], 32 * (r + s - 2))
                    act.copy(tab[1 - s][:, :, 0:F], quad(ps[:, 4 + 2 * (1 - s), :])).then_inc(
                        tab_a, 1)
            run_steps(act, NC, 3, 6, nodes)

            act.wait_ge(zero_set, 1)
            act.copy(acc[:].rearrange("p c n -> p (c n)"),
                     zero[:, 0:1].broadcast_to([P, 2 * NP])).then_inc(acc_cleared, 1)

            def relu(n, s, r):
                act.wait_ge(onehot_built, n + 1)
                if live(n - 2, NG):
                    act.wait_ge(seg2_done, n - 1)
                act.copy(onehot_b[s][:], onehot[s][:])
                act.wait_ge(sums_ready, n + 1)
                act.activation(hrelu[s][:], sums[s], ACT.Relu).then_inc(relu_done, 1)
            run_steps(act, NG, 0, 2, relu)

            act.preload_act_table(ACT.Sqrt)

            def normalize(dst, src, rstd, shifts, done):
                for q in range(4):
                    act.activation(dst[:, q, :], src[:, q, :], ACT.Identity,
                                   bias=shifts[:, q:q + 1], scale=rstd[:, q:q + 1]).then_inc(
                                       done, 1)

            def update(n, s, r):
                if live(n - 1, NC):
                    o = 1 - s
                    act.wait_ge(ph_mm, n)
                    if live(n - 3, NC):
                        act.wait_ge(pu_mm, n - 2)
                    act.activation(h_u[o], ps[:, 2 + o, :], ACT.Relu, bias=ub1[:, 0:1]).then_inc(
                        hu_ready, 1)
                    act.wait_ge(var_a, 4 * n)
                    act.activation(std[o][:], mean_var[o][:, :, 1], ACT.Sqrt,
                                   bias=eps[:, 0:1]).then_inc(stda, 1)
                if live(n - 2, NC):
                    act.wait_ge(var_b, 4 * n - 4)
                    act.activation(std_b[s][:], mean_var_b[s][:, :, 1], ACT.Sqrt,
                                   bias=eps[:, 0:1]).then_inc(stdb, 1)
                if live(n - 1, NC):
                    act.wait_ge(rstda, 2 * n)
                    if live(n - 3, NC):
                        act.wait_ge(bnb, 4 * n - 8)
                        act.wait_ge(res_ready, 4 * n - 8)
                    normalize(z[1 - s], t_sum[1 - s], std[1 - s], shift[1 - s], z_ready)
                if live(n - 2, NC):
                    act.wait_ge(rstdb, 2 * n - 2)
                    if live(n - 4, NC):
                        act.wait_ge(out_stored[s], 16 * r - 16)
                    normalize(res[s], z[s], std_b[s], shift_b[s], res_ready)
            run_steps(act, NC, 2, 4, update)

        @block.tensor
        def _(pe):
            pe.wait_ge(up_in, 64)

            def project(n, s, r):
                pe.wait_ge(xt_loaded[s], 16 * r + 16)
                if live(n - 4, NC):
                    pe.wait_ge(xt_staged, n - 3)
                for q in range(4):
                    mm = pe.matmul(ps[:, s, q * F:q * F + F], xt_in[s][:, q, :], w_up[:],
                                   start=True, stop=True)
                mm.then_inc(xt_mm, 1)
            run_steps(pe, NC, 0, 4, project, slots=4)

            def spread(k):
                if k > 0:
                    pe.wait_ge(emb_sqd, k)
                for h in range(2):
                    mm = pe.matmul(ps[:, 0, :], expand[:, k * P + NB * (1 - h):k * P + P + NB *
                                                       (1 - h)],
                                   lengths[:, h * HALF:h * HALF + HALF], start=(h == 0),
                                   stop=(h == 1))
                mm.then_inc(emb_mm, 1)

            pe.wait_ge(pool_consts, 5)
            pe.wait_ge(r_ready, 1)
            pe.wait_ge(xt_staged, NC)
            for k in range(EMB_AHEAD):
                spread(k)

            pe.wait_ge(w0_placed, 16 * N_COMBOS)
            pe.wait_ge(consts, 2)
            pe.wait_ge(b2_in, 64)

            def first_layer(n, s, r):
                pe.wait_ge(emb_loaded[s], 48 * r + 48)
                if live(n - 1, NG):
                    pe.wait_ge(h1_act, n)
                if isinstance(n, int):
                    pe.wait_ge(emb_sqd, min(n + EMB_AHEAD, NE))
                pe.matmul(ps[:, 0, :], w0_all[:], emb_in[s][:], start=True, stop=True).then_inc(
                    h1_mm, 1)

            def second_layer(m, s):
                if live(m - 2, NG):
                    pe.wait_ge(mid_ready, m - 1)
                for h in range(2):
                    pe.matmul(ps[:, 2 + 2 * s + h, :], ones_bf[0:3, :],
                              b2p[:].rearrange("k q f -> k (q f)"), start=True, stop=False)
                pe.wait_ge(h1_act, m + 1)
                if live(m - 1, NG):
                    pe.wait_ge(h2_act, m)
                pe.matmul(ps[:, 1, :], w1[:], hid[s][:, 0, :], start=True, stop=True).then_inc(
                    h2_mm, 1)

            def third_layer(m, s):
                pe.wait_ge(h2_act, m + 1)
                for h in range(2):
                    for t in range(4):
                        mm = pe.matmul(ps[:, 2 + 2 * s + h, t * F:t * F + F],
                                       hid[s][:, 1, t * P:t * P + P], w2[:, h, :],
                                       start=False, stop=(t == 3))
                mm.then_inc(w_mm, 1)

            def layer1(general):
                def step(n, s, r):
                    if live(n - 1, NG):
                        second_layer(n - 1, 1 - s)
                    if live(n, NG):
                        first_layer(n, s, r)
                    if live(n - 1, NG):
                        third_layer(n - 1, 1 - s)
                    if isinstance(n, int) and n + EMB_AHEAD < NE:
                        pe.wait_ge(h1_act, n + 1)
                        spread(n + EMB_AHEAD)
                    if live(n - 2, NG):
                        pe.wait_ge(mid_ready, n - 1)
                        if general:
                            hold(pe)
                            with pe.Fori(0, NW) as w:
                                pe.wait_ge(win_ready, (n - 2) * NW + w + 1)
                                for c in range(2):
                                    for t in range(TPG):
                                        mm = pe.matmul(
                                            ps[:, 6, c * W:c * W + W],
                                            mid[s][:, t, c * F:c * F + F],
                                            onehot[s][:, t, :], start=(t == 0),
                                            stop=(t == TPG - 1))
                                mm.then_inc(win_done, 1)
                            return
                        if live(n - 4, NG):
                            pe.wait_ge(acc_add, n - 3)
                        for c in range(2):
                            for t in range(TPG):
                                mm = pe.matmul(ps[:, 6 + s, c * W:c * W + W],
                                               mid[s][:, t, c * F:c * F + F],
                                               onehot[s][:, t, :], start=(t == 0),
                                               stop=(t == TPG - 1))
                        mm.then_inc(seg_done, 1)
                run_steps(pe, NG, 2, HEAD, step)

            pe.wait_ge(gen_ready, 1)
            general = pe.value_load(gen_i[0:1, 0:1], min_val=0, max_val=1)
            with pe.If(general == 1):
                layer1(True)
            with pe.Else():
                layer1(False)

            pe.wait_ge(late_in, 16 * N_LATE)
            pe.wait_ge(pool_consts, 6)

            def nodes(n, s, r):
                if live(n, NC):
                    pe.wait_ge(msum_ready, n + 1)
                    if live(n - 2, NC):
                        pe.wait_ge(y_ready, 2 * n - 2)
                    for q in range(4):
                        for c in range(2):
                            mm = pe.matmul(ps[:, s, q * F + c * 64:q * F + c * 64 + 64],
                                           msum[s][:, c, q * P:q * P + P], w_out[:, c, :],
                                           start=True, stop=True)
                    mm.then_inc(po_mm, 1)
                if live(n - 1, NC):
                    pe.wait_ge(x1_ready, 4 * n)
                    if live(n - 3, NC):
                        pe.wait_ge(x1t_copied, n - 2)
                    for q in range(4):
                        mm = pe.transpose(ps[:, 2 + (1 - s), q * P:q * P + P], x1s[1 - s][:, q, :],
                                          ident[:])
                    mm.then_inc(x1t_mm, 1)
                if live(n - 2, NC):
                    pe.wait_ge(x1t_copied, n - 1)
                    if live(n - 4, NC):
                        pe.wait_ge(tab_a, n - 3)
                        pe.wait_ge(tab_b, n - 3)
                    for h in range(2):
                        for q in range(4):
                            mm = pe.matmul(ps[:, 4 + 2 * s + h, q * F:q * F + F],
                                           x1Ts[s][:, q * P:q * P + P], m_w1[:, h, :],
                                           start=True, stop=True)
                    mm.then_inc(tab_mm, 1)
            run_steps(pe, NC, 2, 4, nodes)

            pe.wait_ge(we_loaded, 32)

            def layer2(general):
                def step(n, s, r):
                    if live(n, NG):
                        pe.wait_ge(rel_loaded[s], 16 * r + 16)
                        if live(n - 1, NG):
                            pe.wait_ge(oht_ready, n)
                        for h in range(2):
                            mm = pe.matmul(ps[:, 6 + h, :], ones_bf[0:1, :],
                                           rel_in[s][:, h * HALF:h * HALF + HALF], start=True,
                                           stop=True)
                        mm.then_inc(rel_spread, 1)
                    if live(n - 1, NG):
                        o = 1 - s
                        pe.wait_ge(oht_ready, n)
                        pe.wait_ge(pre_loaded[o], 32 * (r + s))
                        if live(n - 3, NG):
                            pe.wait_ge(sums_ready, n - 2)
                        for t in range(TPG):
                            col = (t % 4) * F
                            mm = pe.matmul(ps[:, 2 * o + t // 4, col:col + F],
                                           onehot_t[o][:, t * P:t * P + P], bwin[o][:],
                                           start=True, stop=True)
                        mm.then_inc(pre_mm, 1)
                    if live(n - 2, NG):
                        pe.wait_ge(relu_done, n - 1)
                        if general:
                            hold(pe)
                            with pe.Fori(0, NW) as w:
                                pe.wait_ge(win2_ready, (n - 2) * NW + w + 1)
                                for c in range(2):
                                    for t in range(TPG):
                                        mm = pe.matmul(
                                            ps[:, 4, c * W:c * W + W],
                                            hrelu[s][:, t, :] if c == 0 else ones[:],
                                            onehot[s][:, t, :], start=(t == 0),
                                            stop=(t == TPG - 1))
                                mm.then_inc(win2_done, 1)
                            pe.sem_inc(seg2_done, 1)
                            return
                        if live(n - 4, NG):
                            pe.wait_ge(acc2_add, n - 3)
                        for c in range(2):
                            for t in range(TPG):
                                mm = pe.matmul(
                                    ps[:, 4 + s, c * W:c * W + W],
                                    hrelu[s][:, t, :] if c == 0 else ones_bf[:],
                                    onehot[s][:, t, :] if c == 0 else onehot_b[s][:, t, :],
                                    start=(t == 0), stop=(t == TPG - 1))
                        mm.then_inc(seg2_done, 1)
                run_steps(pe, NG, 2, 4, step)

            general = pe.value_load(gen_i[0:1, 0:1], min_val=0, max_val=1)
            with pe.If(general == 1):
                layer2(True)
            with pe.Else():
                layer2(False)

            pe.wait_ge(acc2_all, 1)
            pe.wait_ge(x1t_kept, NC)

            def update(n, s, r):
                cols = bass.ds(n * CHUNK, CHUNK)
                if live(n, NC):
                    if live(n - 2, NC):
                        pe.wait_ge(agg_ready, n - 1)
                    pe.matmul(ps[:, s, :], m_w2[:], acc[:, 0, cols], start=True, stop=False)
                    pe.matmul(ps[:, s, :], mb2[:], acc[0:1, 1, cols], start=False,
                              stop=True).then_inc(pa_mm, 1)
                if live(n - 1, NC):
                    pe.wait_ge(hu_ready, n)
                    if live(n - 3, NC):
                        pe.wait_ge(t_ready, n - 2)
                    for q in range(4):
                        mm = pe.matmul(ps[:, 4 + (1 - s), q * F:q * F + F],
                                       h_u[1 - s][:, q * P:q * P + P], u_w2[:], start=True,
                                       stop=True)
                    mm.then_inc(pu_mm, 1)
                if live(n, NC):
                    if live(n - 2, NC):
                        pe.wait_ge(hu_ready, n - 1)
                    pe.matmul(ps[:, 2 + s, :], u_w1[:, 0, :], x1T[:, cols], start=True, stop=False)
                    pe.wait_ge(agg_ready, n + 1)
                    pe.matmul(ps[:, 2 + s, :], u_w1[:, 1, :], agg_t[s], start=False,
                              stop=True).then_inc(ph_mm, 1)
            run_steps(pe, NC, 2, 4, update)

        @block.vector
        def _(dve):
            for t in (w_up, w0, w1, w2, w_out):
                dve.memset(t[:], 0.0).then_inc(cleared, 1)
            dve.memset(zero[:], 0.0).then_inc(zero_set, 1)
            dve.memset(expand, 1.0).then_inc(zero_set, 1)
            dve.memset(ones[:], 1.0)
            dve.memset(ones_bf[:], 1.0)
            dve.memset(eps[:], LN_EPS)
            dve.wait_ge(pool_consts, 3)
            dve.tensor_copy(iota_n[:], iota_i[:])
            dve.tensor_copy(iota_p[:], part_i[:, 0:1])
            dve.tensor_scalar(part_i[:, 1:2], part_i[:, 0:1], NB - 1, None,
                              ALU.bitwise_and).then_inc(dprep, 1)
            dve.wait_ge(dprep, 1)
            dve.tensor_copy(center[:], part_i[:, 1:2]).then_inc(dprep, 1)
            dve.wait_ge(dprep, 2)
            dve.tensor_scalar(center[:], center[:], -1.0, None, ALU.mult).then_inc(consts, 1)

            dve.wait_ge(drow_in, 16)
            dve.tensor_copy(drow, drow_i).then_inc(dprep, 1)
            dve.wait_ge(dprep, 3)
            dve.tensor_reduce(small[0:NG, 0:1], drow, AX, ALU.min).then_inc(dprep, 1)
            dve.tensor_reduce(small[0:NG, 1:2], drow, AX, ALU.max).then_inc(dprep, 1)
            dve.wait_ge(dprep, 5)
            dve.tensor_copy(small_i[0:NG, 0:1], small[0:NG, 0:1])
            dve.tensor_tensor(small[0:NG, 2:3], small[0:NG, 1:2], small[0:NG, 0:1],
                              ALU.subtract).then_inc(ranges_ready, 1)
            dve.tensor_scalar(rel_row, drow, small[0:NG, 0:1], None, ALU.subtract).then_inc(
                dprep, 1)

            dve.wait_ge(lengths_in, 16)
            dve.tensor_scalar(far, lengths, 1.0, 1000.0, ALU.is_gt, ALU.mult).then_inc(r_prep, 1)
            dve.wait_ge(r_prep, 1)
            dve.scalar_tensor_tensor(lengths, lengths, 1.0, far, ALU.min, ALU.add).then_inc(
                r_prep, 1)
            dve.wait_ge(r_prep, 2)
            dve.tensor_scalar(lengths, lengths, 0.0, None, ALU.max).then_inc(r_ready, 1)

            dve.wait_ge(weights_in, 16 * N_WEIGHTS)
            dve.tensor_scalar(w0_rest, w0[:], float(NB) ** 0.5, None, ALU.mult).then_inc(vprep, 1)
            dve.tensor_scalar(w_out[:], w_out[:], OUT_SCALE, None, ALU.mult).then_inc(vprep, 1)
            dve.wait_ge(vprep, 2)
            dve.tensor_copy(w0_part[:, 0, :], w0_rest).then_inc(w0_split, 1)
            dve.tensor_copy(b2_part[:, 0, :], b2_row[:]).then_inc(b2_split, 1)
            for k in range(2):
                dve.wait_ge(w0_split, 2 * k + 1)
                dve.tensor_tensor(w0_rest, w0_rest, w0_part[:, k, :], ALU.subtract).then_inc(
                    w0_split, 1)
                dve.wait_ge(b2_split, 2 * k + 1)
                dve.tensor_tensor(b2_row[:], b2_row[:], b2_part[:, k, :], ALU.subtract).then_inc(
                    b2_split, 1)
                dve.wait_ge(w0_split, 2 * k + 2)
                dve.tensor_copy(w0_part[:, k + 1, :], w0_rest).then_inc(w0_split, 1)
                dve.wait_ge(b2_split, 2 * k + 2)
                dve.tensor_copy(b2_part[:, k + 1, :], b2_row[:]).then_inc(b2_split, 1)
            for k, (rows, c) in enumerate(((slice(64, 96), 0), (slice(0, 32), 1),
                                           (slice(64, 96), 1))):
                scaled = dve.tensor_scalar(w_out[rows, c, :], w_out[rows, c, :], SQ3, None,
                                           ALU.mult)
            scaled.then_inc(consts, 1)

            def split(n, s, r):
                dve.wait_ge(emb_ready, n + 1)
                if live(n - 2, NE):
                    dve.wait_ge(emb_stored[s], 48 * r)
                dve.tensor_copy(emb_part[s][0], emb_rest[s]).then_inc(emb_cast, 1)
                dve.wait_ge(emb_cast, 2 * n + 1)
                dve.tensor_tensor(emb_rest[s], emb_rest[s], emb_part[s][0],
                                  ALU.subtract).then_inc(emb_split, 1)
                dve.wait_ge(emb_split, 4 * n + 1)
                dve.tensor_copy(emb_part[s][1], emb_rest[s]).then_inc(emb_cast, 1)
                dve.wait_ge(emb_cast, 2 * n + 2)
                dve.tensor_tensor(emb_part[s][2], emb_rest[s], emb_part[s][1],
                                  ALU.subtract).then_inc(emb_split, 3)

            split(0, 0, 0)

            dve.wait_ge(ranges_in, 48)
            dve.tensor_reduce(small[:, 8:9], span_all, AX, ALU.max).then_inc(dprep, 1)
            dve.wait_ge(dprep, 7)
            dve.tensor_scalar(gen_col[:, 0:1], small[:, 8:9], float(WR), None,
                              ALU.is_ge).then_inc(dprep, 1)
            dve.wait_ge(dprep, 8)
            dve.tensor_copy(gen_i[:], gen_col[0:1, 0:1]).then_inc(gen_ready, 1)
            dve.tensor_scalar(gen_col[:, 1:2], gen_col[:, 0:1], -1.0, 1.0, ALU.mult,
                              ALU.add).then_inc(dprep, 1)
            dve.wait_ge(dprep, 9)
            dve.tensor_scalar(rel_row_b, rel_row, gen_col[0:NG, 1:2], gen_col[0:NG, 0:1],
                              ALU.mult, ALU.subtract).then_inc(rel_ready, 1)
            dve.wait_ge(dcol_in, 16)
            dve.tensor_copy(dcol[:], dcol_i).then_inc(dprep, 1)
            dve.wait_ge(dprep, 10)
            dve.tensor_tensor(rel[:].rearrange("p (g t) -> p g t", t=TPG),
                              dcol[:].rearrange("p (g t) -> p g t", t=TPG),
                              along(base_all, 2, TPG), ALU.subtract).then_inc(dprep, 1)
            split(1, 1, 0)

            dve.wait_ge(evec_in, 16)
            dve.tensor_tensor(evec_sq, rhat[:], rhat[:], ALU.mult).then_inc(vprep, 1)
            dve.wait_ge(vprep, 3)
            dve.tensor_reduce(norm, evec_sq, AX, ALU.add).then_inc(norm_sq, 1)
            dve.wait_ge(norm_ready, 1)
            dve.tensor_scalar(norm, norm, 1e-12, None, ALU.add).then_inc(vprep, 1)
            dve.wait_ge(vprep, 4)
            dve.reciprocal(inv, norm).then_inc(vprep, 1)
            dve.wait_ge(vprep, 5)
            dve.tensor_tensor(rhat[:], rhat[:], along(inv, 2, 3), ALU.mult).then_inc(vprep, 1)
            dve.wait_ge(vprep, 6)
            dve.wait_ge(dprep, 11)

            def build_onehot(n, s):
                return dve.tensor_tensor(onehot[s][:], along(iota_n[:], 1, TPG),
                                         along(rel[:, bass.ds(n * TPG, TPG)], 2, W), ALU.is_equal)

            def all_windows(n, s, bank, step_sem, ready_sem, done_sem, add_sem):
                dve.tensor_copy(relw[:], dcol[:, bass.ds(n * TPG, TPG)]).then_inc(step_sem, 1)
                with dve.Fori(0, NW) as w:
                    dve.wait_ge(step_sem, n * (NW + 1) + w + 1)
                    dve.tensor_tensor(onehot[s][:], along(iota_n[:], 1, TPG),
                                      along(relw[:], 2, W), ALU.is_equal).then_inc(ready_sem, 1)
                    dve.wait_ge(ready_sem, n * NW + w + 1)
                    dve.tensor_scalar(relw[:], relw[:], -float(W), None, ALU.add).then_inc(
                        step_sem, 1)
                    dve.wait_ge(done_sem, n * NW + w + 1)
                    win = acc[:, :, bass.ds(w * W, W)]
                    dve.tensor_tensor(win, win, ps[:, bank, 0:2 * W].rearrange(
                        "p (c n) -> p c n", c=2), ALU.add).then_inc(add_sem, 1)
                dve.wait_ge(add_sem, n * NW + NW)
                dve.wait_ge(step_sem, (n + 1) * (NW + 1))

            def add_window(n, bank, add_sem):
                base = dve.value_load(base_sb[0:1, bass.ds(n, 1)], min_val=0, max_val=NP - W)
                if live(n - 1, NG):
                    dve.wait_ge(add_sem, n)
                win = acc[:, :, bass.ds(base, W)]
                dve.tensor_tensor(win, win, ps[:, bank, 0:2 * W].rearrange(
                    "p (c n) -> p c n", c=2), ALU.add).then_inc(add_sem, 1)

            VS = 6

            def messages(n, s, r, general):
                if live(n - 2, NG) and not general:
                    dve.wait_ge(seg_done, n - 1)
                if not general:
                    build_onehot(n, s)
                m = mid[s][:]
                vec = m[:, :, 2 * MUL:].rearrange("p t (c u k) -> p t c u k", c=3, u=2)
                w = ps[:, 2 + 2 * s:4 + 2 * s, :].rearrange("p b (t f) -> p (b t) f", t=4)
                xs, xv = gx[s][:, :, 0:MUL], gx[s][:, :, MUL:].rearrange(
                    "p t (c k) -> p t c k", c=3)
                unit = along(rhat[:, bass.ds(n * TPG, TPG), :], 3, MUL)
                dve.wait_ge(gathered[s], 128 * r + 128)
                dve.tensor_tensor(prod[:], xv, unit, ALU.mult).then_inc(vstep, 1)
                dve.wait_ge(w_mm, n + 1)
                dve.tensor_tensor(m[:, :, 0:2 * MUL].rearrange("p t (u k) -> p t u k", u=2),
                                  w[:, :, 0:2 * MUL].rearrange("p t (u k) -> p t u k", u=2),
                                  along(xs, 2, 2), ALU.mult).then_inc(vstep, 1)
                dve.wait_ge(vstep, n * VS + 1)
                dve.tensor_tensor(dot[:], prod[:, :, 0, :], prod[:, :, 1, :], ALU.add).then_inc(
                    vstep, 1)
                dve.wait_ge(vstep, n * VS + 2)
                dve.tensor_tensor(vec[:, :, :, 0, :], along(m[:, :, MUL:2 * MUL], 2, 3), unit,
                                  ALU.mult).then_inc(vstep, 1)
                dve.wait_ge(vstep, n * VS + 3)
                dve.tensor_tensor(dot[:], dot[:], prod[:, :, 2, :], ALU.add).then_inc(vstep, 1)
                dve.tensor_tensor(vec[:, :, :, 1, :], along(w[:, :, 2 * MUL:3 * MUL], 2, 3), xv,
                                  ALU.mult).then_inc(vstep, 1)
                dve.wait_ge(vstep, n * VS + 5)
                dve.tensor_tensor(m[:, :, MUL:2 * MUL], w[:, :, 3 * MUL:], dot[:],
                                  ALU.mult).then_inc(mid_ready, 1)

            def layer1(general):
                def step(n, s, r):
                    if live(n, NG):
                        messages(n, s, r, general)
                        if general:
                            all_windows(n, s, 6, relw_step, win_ready, win_done, acc_add)
                    if live(n - 1, NG) and not general:
                        dve.wait_ge(seg_done, n)
                        add_window(n - 1, 6 + (1 - s), acc_add)
                    if isinstance(n, int) and n + EMB_AHEAD < NE:
                        split(n + EMB_AHEAD, s, r + EMB_AHEAD // 2)
                run_steps(dve, NG, 1, HEAD, step)

            dve.wait_ge(acc_cleared, 1)
            general = dve.value_load(gen_i[0:1, 0:1], min_val=0, max_val=1)
            with dve.If(general == 1):
                layer1(True)
            with dve.Else():
                layer1(False)
            dve.engine_nop().then_inc(acc_all, 1)

            dve.wait_ge(late_in, 16 * N_LATE)
            dve.tensor_tensor(beta[:], beta[:], ub2[:], ALU.subtract).then_inc(beta_ready, 1)

            def norm_stats(src, st, mv, bn_sem, mv_sem, n):
                for q in range(4):
                    dve.bn_stats(st[:, q, :], src[:, q, :]).then_inc(bn_sem, 1)
                dve.wait_ge(bn_sem, 4 * n + 4)
                hold(dve)
                for q in range(4):
                    dve.bn_aggr(mv[:, q, :], st[:, q, :]).then_inc(mv_sem, 1)

            def nodes(n, s, r):
                if live(n, NC):
                    dve.wait_ge(po_mm, n + 1)
                    dve.wait_ge(xin_loaded[s], 16 * r + 16)
                    po = quad(ps[:, s, :])
                    dve.tensor_tensor(y[s][:, :, 0:MUL], po[:, :, 0:MUL], xin[s][:, :, 0:MUL],
                                      ALU.add).then_inc(y_ready, 1)
                    dve.tensor_tensor(
                        y[s][:, :, MUL:].rearrange("p q (k c) -> p q c k", c=3),
                        po[:, :, MUL:].rearrange("p q (c k) -> p q c k", c=3),
                        xin[s][:, :, MUL:].rearrange("p q (k c) -> p q c k", c=3),
                        ALU.add).then_inc(y_ready, 1)
                    dve.wait_ge(y_ready, 2 * n + 2)
                    norm_stats(y[s], stats[s], mean_var[s], bn_done, mv_ready, n)
                if live(n - 2, NC):
                    dve.wait_ge(tab_mm, n - 1)
                    if live(n - 4, NC):
                        dve.wait_ge(tab_stored[s], 32 * r - 32)
                    dve.tensor_tensor(tab[s][:, :, F:2 * F], quad(ps[:, 5 + 2 * s, :]),
                                      along(mb1[:], 1, 4), ALU.add).then_inc(tab_b, 1)
                if live(n, NC):
                    dve.wait_ge(std_ready, n + 1)
                    dve.reciprocal(std[s][:], std[s][:]).then_inc(rstd_ready, 1)
                    dve.wait_ge(rstd_ready, n + 1)
                    if live(n - 2, NC):
                        dve.wait_ge(x1t_mm, n - 1)
                        dve.wait_ge(x1_kept, n - 1)
                    for q in range(4):
                        dve.tensor_scalar(x1s[s][:, q, :], y[s][:, q, :], mean_var[s][:, q, 0:1],
                                          std[s][:, q:q + 1], ALU.subtract, ALU.mult).then_inc(
                                              x1_ready, 1)
            run_steps(dve, NC, 2, 4, nodes)

            def layer2(general):
                def step(n, s, r):
                    o = 1 - s
                    if live(n, NG):
                        dve.wait_ge(rel_spread, n + 1)
                        if live(n - 2, NG):
                            dve.wait_ge(pre_mm, n - 1)
                        dve.tensor_scalar(
                            onehot_t[s][0:WR, :], ps[0:WR, 6:8, :].rearrange("p b e -> p (b e)"),
                            iota_p[0:WR, 0:1], None, ALU.is_equal).then_inc(oht_ready, 1)
                    if live(n - 1, NG):
                        if live(n - 3, NG):
                            dve.wait_ge(seg2_done, n - 2)
                        build_onehot(n - 1, o).then_inc(onehot_built, 1)
                        dve.wait_ge(gathered2[o], 128 * (r + s))
                        dve.wait_ge(pre_mm, n)
                        if live(n - 3, NG):
                            dve.wait_ge(relu_done, n - 2)
                        pre = ps[:, 2 * o:2 * o + 2, :].rearrange("p b (t f) -> p (b t) f", t=4)
                        add = dve.tensor_tensor(sums[o], pre, gx[o][:], ALU.add)
                        if general:
                            add.then_inc(sum_step, 1)
                            dve.wait_ge(sum_step, n)
                            add = dve.tensor_tensor(sums[o], sums[o], gb[o], ALU.add)
                        add.then_inc(sums_ready, 1)
                        if general:
                            dve.wait_ge(relu_done, n)
                            all_windows(n - 1, o, 4, relw2_step, win2_ready, win2_done, acc2_add)
                    if live(n - 2, NG) and not general:
                        dve.wait_ge(seg2_done, n - 1)
                        add_window(n - 2, 4 + s, acc2_add)
                run_steps(dve, NG, 2, 4, step)

            dve.wait_ge(acc_cleared, 2)
            with dve.If(general == 1):
                layer2(True)
            with dve.Else():
                layer2(False)
            dve.engine_nop().then_inc(acc2_all, 1)
            dve.wait_ge(acc2_all, 1)

            dve.wait_ge(cnt_back, 16)
            dve.tensor_scalar(cnt_cols[:], cnt_cols[:], 1.0, None, ALU.max).then_inc(cnt_max, 1)
            dve.wait_ge(cnt_max, 1)
            dve.reciprocal(cnt_cols[:], cnt_cols[:]).then_inc(cnt_ready, 1)

            def scale_shift(rstd, shifts, mv, done, n):
                dve.reciprocal(rstd[:], rstd[:]).then_inc(done, 1)
                dve.wait_ge(done, 2 * n + 1)
                dve.scalar_tensor_tensor(shifts[:], mv[:, :, 0], -1.0, rstd[:], ALU.mult,
                                         ALU.mult).then_inc(done, 1)

            def update(n, s, r):
                o = 1 - s
                if live(n, NC):
                    dve.wait_ge(pa_mm, n + 1)
                    dve.wait_ge(inv_loaded[s], 16 * r + 16)
                    if live(n - 2, NC):
                        dve.wait_ge(ph_mm, n - 1)
                    dve.tensor_tensor(agg_t[s], ps[:, s, :], cnt_inv[s], ALU.mult).then_inc(
                        agg_ready, 1)
                if live(n - 1, NC):
                    dve.wait_ge(pu_mm, n)
                    if live(n - 3, NC):
                        dve.wait_ge(z_ready, 4 * n - 8)
                    dve.tensor_tensor(t_sum[o], quad(ps[:, 4 + o, :]),
                                      x1n[:, bass.ds((n - 1) * 4, 4), :], ALU.add).then_inc(
                                          t_ready, 1)
                    dve.wait_ge(t_ready, n)
                    norm_stats(t_sum[o], stats[o], mean_var[o], bna, var_a, n - 1)
                if live(n - 2, NC):
                    dve.wait_ge(zx, n - 1)
                    norm_stats(z[s], stats_b[s], mean_var_b[s], bnb, var_b, n - 2)
                if live(n - 1, NC):
                    dve.wait_ge(stda, n)
                    scale_shift(std[o], shift[o], mean_var[o], rstda, n - 1)
                if live(n - 2, NC):
                    dve.wait_ge(stdb, n - 1)
                    scale_shift(std_b[s], shift_b[s], mean_var_b[s], rstdb, n - 2)
            run_steps(dve, NC, 2, 4, update)
    return nc


def kernel(**inputs):
    import numpy as np
    import concourse.bacc as bacc
    from concourse.bass_utils import run_bass_kernel_spmd

    given = {k: np.ascontiguousarray(v) for k, v in inputs.items()}

    def pad(x, n, value=0):
        fill = np.full((n - x.shape[0],) + x.shape[1:], value, x.dtype)
        return np.concatenate([x, fill])

    x = pad(given["x"], NP)
    order = np.concatenate([np.arange(MUL)] + [MUL + 3 * np.arange(MUL) + c for c in range(3)])
    src, dst = pad(given["src"], EP), pad(given["dst"], EP, N)

    def by_tile(v):
        return v.reshape(NT, P, *v.shape[1:]).swapaxes(0, 1)

    def ids(v):
        return v.reshape(NG, TPG, P).transpose(0, 2, 1)

    arrays = {
        "x_t": x[:, order].T,
        "x_rows": x,
        "ids": np.concatenate([ids(src), ids(dst)], axis=2).reshape(NG * P, 2 * TPG),
        "dst_row": dst.reshape(NG, GROUP),
        "dst_col": by_tile(dst),
        "evec": by_tile(pad(given["edge_attr_3"], EP)),
        "lengths": pad(given["edge_weight"], EP).reshape(NG, GROUP),
        "attr2": pad(given["edge_attr_2"], EP).reshape(NG, GROUP, 2).transpose(0, 2, 1).reshape(
            2 * NG, GROUP),
    }
    for name, key in (("w_up0", "L0_gnn_W_up0"), ("w_up1", "L0_gnn_W_up1"),
                      ("mlp_w0", "L0_gnn_mlp_w0"), ("mlp_b0", "L0_gnn_mlp_b0"),
                      ("mlp_w1", "L0_gnn_mlp_w1"), ("mlp_b1", "L0_gnn_mlp_b1"),
                      ("mlp_w2", "L0_gnn_mlp_w2"), ("mlp_b2", "L0_gnn_mlp_b2"),
                      ("w_out0", "L0_gnn_W_out0"), ("w_out1", "L0_gnn_W_out1"),
                      ("m_w1", "L1_gnn_mW1"), ("mb1", "L1_gnn_mb1"), ("m_w2", "L1_gnn_mW2"),
                      ("mb2", "L1_gnn_mb2"), ("u_w1", "L1_gnn_uW1"), ("ub1", "L1_gnn_ub1"),
                      ("u_w2", "L1_gnn_uW2"), ("ub2", "L1_gnn_ub2"), ("gamma", "L1_gnn_gamma"),
                      ("beta", "L1_gnn_beta")):
        arrays[name] = given[key]
    arrays = {f"in_{k}": np.ascontiguousarray(v) for k, v in arrays.items()}

    nc = bacc.Bacc("TRN2", target_bir_lowering=False, num_devices=1)
    a = {k[3:]: nc.dram_tensor(k, v.shape, mybir.dt.from_np(v.dtype), kind="ExternalInput").ap()
         for k, v in arrays.items()}
    out = nc.dram_tensor("out_rows", [NP, F], F32, kind="ExternalOutput").ap()
    gnn_kernel(nc, a, out)
    r = run_bass_kernel_spmd(nc, [arrays], core_ids=[0])
    return r.results[0]["out_rows"][:N]
```

```python
from contextlib import ExitStack

import concourse.bass as bass
from concourse import mybir

F32 = mybir.dt.float32
BF16 = mybir.dt.bfloat16
I32 = mybir.dt.int32
ALU = mybir.AluOpType
ACT = mybir.ActivationFunctionType
AX = mybir.AxisListType.X

P = 128
N = 6250
E = 106250
F = 128
MUL = 32
NB = 8
HID = 64
TPG = 8
GROUP = TPG * P
NG = -(-E // GROUP)
EP = NG * GROUP
NT = NG * TPG
W = 128
NA = 3
WR = W - NA
HALF = GROUP // 2
NH = 2 * NG
CHUNK = 512
NC = -(-(N + W) // CHUNK)
NP = NC * CHUNK
LAST_TILES = -(-(N - (NC - 1) * CHUNK) // P)
NW = NP // W
EMB_STEP = P // NB
NE = NH // EMB_STEP
EMB_GROUPS = EMB_STEP // 2
EMB_AHEAD = 2
HEAD = 2 * (NE - EMB_AHEAD + 1)
BODY = NG // NC
SIDE_LAG = 3
EARLY = NG // BODY - SIDE_LAG
LN_EPS = 1e-5
SQ3 = 3.0 ** 0.5
OUT_SCALE = 1.0 / ((2 * MUL) ** 0.5 * 16.0)
assert NH % EMB_STEP == 0 and NG % 2 == 0
assert BODY == 8 and NG % BODY == 0 and HEAD == SIDE_LAG * BODY


def along(ap, axis, n):
    shape = list(ap.shape)
    return ap.unsqueeze(axis).broadcast_to(shape[:axis] + [n] + shape[axis:])


def run_steps(eng, steps, lag, head, step, slots=2):
    assert head % slots == 0
    head = min(head, steps // slots * slots)
    for n in range(head):
        step(n, n % slots, n // slots)
    loops = (steps - head) // slots
    if loops:
        with eng.Fori(0, loops) as i:
            for s in range(slots):
                step(i * slots + (head + s), s, i + head // slots)
    for n in range(head + slots * loops, steps + lag):
        step(n, n % slots, n // slots)


def run_passes(eng, lag, head, step):
    half = BODY // 2
    for n in range(head):
        step(n, n % 2, n // 2)
    if SIDE_LAG * BODY > head:
        with eng.Fori(0, SIDE_LAG - head // BODY) as i:
            for s in range(BODY):
                step(i * BODY + (head + s), s % 2, i * half + (head + s) // 2)
    with eng.Fori(0, EARLY) as c:
        for s in range(BODY):
            step(c * BODY + (SIDE_LAG * BODY + s), s % 2, c * half + (SIDE_LAG * half + s // 2),
                 (c, s))
    for n in range(NG, NG + lag):
        step(n, n % 2, n // 2)


def last(steps, slots, s):
    return (steps + slots - 1 - s) // slots


def emb_beside(n):
    if isinstance(n, int) and 2 <= n < HEAD and n % 2 == 0:
        return n // 2 + EMB_AHEAD - 1
    return None


def live(n, steps):
    return not isinstance(n, int) or 0 <= n < steps


def tiles_of(n, steps):
    return LAST_TILES if isinstance(n, int) and n == steps - 1 else 4


def gnn_kernel(nc, a, out):
    with ExitStack() as ctx:
        def sb(name, shape, dt=F32):
            return ctx.enter_context(nc.sbuf_tensor(name, shape, dt))

        def sem(name):
            return ctx.enter_context(nc.semaphore(name))

        def pair(name):
            return [sem(f"{name}{s}") for s in range(2)]

        def dram(name, shape, dt=F32):
            return nc.dram_tensor(name, shape, dt).ap()

        x_table = dram("x_table", [NP, F])
        src_table = dram("src_table", [NP, F])
        dst_table = dram("dst_table", [NP, F])
        emb_d = [dram(f"emb_d{k}", [NH * NB, HALF], BF16) for k in range(3)]
        rel_d = dram("rel_d", [NG, GROUP], BF16)
        base_i_d = dram("base_i_d", [NG, 1], I32)
        base_f_d = dram("base_f_d", [NG, 1])
        cnt_d = dram("cnt_d", [1, NP])
        cnt_inv_d = dram("cnt_inv_d", [1, NP])
        span_d = dram("span_d", [NG, 1])
        cnt_some_d = dram("cnt_some_d", [1, NP], BF16)
        b2_parts_d = dram("b2_parts_d", [1, 3 * F], BF16)
        v_parts_d = dram("v_parts_d", [1, 6 * F], BF16)

        ps = ctx.enter_context(nc.psum_tensor("ps", [P, 8, 512], F32))

        acc = sb("acc", [P, 2, NP])
        x1n = sb("x1n", [P, NC * 4, F])
        x1T = sb("x1T", [P, NP])
        rhat = sb("rhat", [P, NT, 3])
        rel = sb("rel", [P, NT])
        dcol = sb("dcol", [P, NT])
        base_sb = sb("base_sb", [1, NG], I32)
        gen_i = sb("gen_i", [1, 1], I32)
        w_up = sb("w_up", [P, F])
        w0 = sb("w0", [2 * NB, P])
        w1 = sb("w1", [P, P])
        w0_part = sb("w0_part", [2 * NB, 3, P], BF16)
        w0_all = sb("w0_all", [P, P], BF16)
        w2 = sb("w2", [P, 2, F])
        b0 = sb("b0", [P, 1])
        b1 = sb("b1", [P, 1])
        b2_row = sb("b2_row", [1, F])
        b2_part = sb("b2_part", [1, 3, F], BF16)
        b2p = sb("b2p", [3, 4, F], BF16)
        ones_bf = sb("ones_bf", [P, P], BF16)
        w_out = sb("w_out", [P, 2, 2 * MUL])
        m_w1 = sb("m_w1", [P, 2, F])
        m_w2 = sb("m_w2", [P, F])
        mb2 = sb("mb2", [P, 1])
        mu_w = sb("mu_w", [P, F])
        v_rows = sb("v_rows", [3, 2 * F], BF16)
        u_w1 = sb("u_w1", [P, 2, F])
        ub1 = sb("ub1", [P, 1])
        u_w2 = sb("u_w2", [P, F])
        ub2 = sb("ub2", [P, F])
        gamma = sb("gamma", [P, F])
        beta = sb("beta", [P, F])
        ones = sb("ones", [P, P])
        ident = sb("ident", [P, P])
        iota_i = sb("iota_i", [P, W], I32)
        iota_n = sb("iota_n", [P, W])
        part_i = sb("part_i", [P, 2], I32)
        iota_p = sb("iota_p", [P, 1])
        center = sb("center", [P, 1])
        eps = sb("eps", [P, 1])
        zero = sb("zero", [P, 1])
        gen_col = sb("gen_col", [P, 2])
        ids = [sb(f"ids{s}", [P, 2 * TPG], I32) for s in range(2)]
        gx = [sb(f"gx{s}", [P, TPG, F]) for s in range(2)]
        mid = [sb(f"mid{s}", [P, TPG, 2 * F]) for s in range(2)]
        onehot = [sb(f"onehot{s}", [P, TPG, W]) for s in range(2)]
        onehot_b = [sb(f"onehot_b{s}", [P, TPG, W], BF16) for s in range(2)]
        relw = sb("relw", [P, TPG])
        emb_in = [sb(f"emb_in{s}", [P, HALF], BF16) for s in range(2)]
        hid = [sb(f"hid{s}", [P, 2, HALF]) for s in range(2)]
        prod = sb("prod", [P, TPG, 3, MUL])
        dot = sb("dot", [P, TPG, MUL])
        onehot_t = [sb(f"onehot_t{s}", [P, GROUP]) for s in range(2)]
        rel_in = [sb(f"rel_in{s}", [1, GROUP], BF16) for s in range(2)]
        bwin = [sb(f"bwin{s}", [P, F]) for s in range(2)]
        hrelu = [sb(f"hrelu{s}", [P, TPG, F]) for s in range(2)]
        stats = [sb(f"stats{s}", [P, 4, 6]) for s in range(2)]
        mean_var = [sb(f"mean_var{s}", [P, 4, 2]) for s in range(2)]
        std = [sb(f"std{s}", [P, 4]) for s in range(2)]
        stats_b = [sb(f"stats_b{s}", [P, 4, 6]) for s in range(2)]
        mean_var_b = [sb(f"mean_var_b{s}", [P, 4, 2]) for s in range(2)]
        std_b = [sb(f"std_b{s}", [P, 4]) for s in range(2)]
        shift = [sb(f"shift{s}", [P, 4]) for s in range(2)]
        shift_b = [sb(f"shift_b{s}", [P, 4]) for s in range(2)]
        cnt_cols = sb("cnt_cols", [P, NP // P])
        some_cols = sb("some_cols", [P, NP // P], BF16)

        def flat(t):
            return t[:].rearrange("p a b -> p (a b)")

        def quad(ap):
            return ap.rearrange("p (q f) -> p q f", f=F)

        x1n_flat = x1n[:].rearrange("p a b -> p (a b)")
        evec_sq = x1n_flat[:, 0:3 * NT].rearrange("p (t c) -> p t c", c=3)
        norm = x1n_flat[:, 3 * NT:4 * NT]
        inv = x1n_flat[:, 4 * NT:5 * NT]
        dcol_i = x1n_flat[:, 5 * NT:6 * NT].bitcast(I32)
        drow_i = x1T[0:NG, 0:GROUP].bitcast(I32)
        drow = x1T[0:NG, GROUP:2 * GROUP]
        rel_row = x1T[0:NG, 2 * GROUP:3 * GROUP]
        rel_row_b = x1T[0:NG, 3 * GROUP:3 * GROUP + GROUP // 2].bitcast(BF16)
        base_all = x1T[:, 3584:3584 + NG]
        span_all = x1T[:, 3712:3712 + NG]
        small = x1T[:, 3840:3856]
        small_i = x1T[:, 3856:3858].bitcast(I32)
        w0_rest = x1T[0:2 * NB, 3872:3872 + P]
        lengths = x1n_flat[0:NG, 6 * NT:6 * NT + GROUP]
        far = x1T[0:NG, 0:GROUP]
        expand = x1T[0:NG, 4000:4000 + NE * P + NB]
        m_w2T = x1T[:, 5700:5700 + P]
        v_row = x1T[0:1, 5840:5840 + 2 * F]
        v_part = flat(hid[0])[0:1, 0:3 * F].bitcast(BF16).rearrange("o (k f) -> o k f", f=2 * F)
        emb_sq = [flat(hrelu[s])[:, 0:HALF] for s in range(2)]
        emb_rest = [flat(hrelu[s])[:, HALF:2 * HALF] for s in range(2)]
        emb_part = [[onehot_t[s][:, k * HALF // 2:(k + 1) * HALF // 2].bitcast(BF16)
                     for k in range(3)] for s in range(2)]
        mid_flat = [flat(mid[s]) for s in range(2)]
        xt_in = [quad(mid_flat[s // 2][:, (s % 2) * 512:(s % 2) * 512 + 512]) for s in range(4)]
        xt_stage = [quad(mid_flat[s // 2][:, 1024 + (s % 2) * 512:1536 + (s % 2) * 512])
                    for s in range(4)]
        side_sum = flat(hrelu[0]).rearrange("p (c n) -> p c n", c=2)
        side_y, side_x = hrelu[1][:, 0:4, :], hrelu[1][:, 4:8, :]
        side_x1 = quad(onehot_t[1][:, 0:512])
        side_x1T = onehot_t[1][:, 512:1024]
        side_tab = onehot_t[0][:].rearrange("p (q f) -> p q f", q=4)
        msum = [flat(gx[s]).rearrange("p (c n) -> p c n", c=2) for s in range(2)]
        xin = [hrelu[s][:, 0:4, :] for s in range(2)]
        y = [hrelu[s][:, 4:8, :] for s in range(2)]
        x1s = [quad(mid_flat[s][:, 0:512]) for s in range(2)]
        x1Ts = [mid_flat[s][:, 512:1024] for s in range(2)]
        tab = [mid[s][:, 4:8, :] for s in range(2)]
        gb = [mid[s][:, :, 0:F] for s in range(2)]
        sums = [mid[s][:, :, F:2 * F] for s in range(2)]
        side2_h, side2_t = flat(hid[0])[:, 0:512], quad(flat(hid[0])[:, 512:1024])
        side2_agg, side2_inv = flat(hid[1])[:, 0:512], flat(hid[1])[:, 512:1024]
        side2_z = quad(prod[:].rearrange("p t c k -> p (t c k)")[:, 0:512])
        side2_some = emb_in[0][0:3, :]
        side2_res = mid[0][:, 0:4, 0:F]
        cnt_inv = [flat(gx[s])[:, 0:512] for s in range(2)]
        agg = [flat(gx[s])[:, 512:1024] for s in range(2)]
        prod_flat = prod[:].rearrange("p t c k -> p (t c k)")
        cnt_some = [prod_flat[0:3, s * CHUNK // 2:(s + 1) * CHUNK // 2].bitcast(BF16)
                    for s in range(2)]
        h_u = [flat(hrelu[s])[:, 0:512] for s in range(2)]
        t_sum = [quad(mid_flat[s][:, 0:512]) for s in range(2)]
        z = [quad(mid_flat[s][:, 512:1024]) for s in range(2)]
        res = [quad(mid_flat[s][:, 1024:1536]) for s in range(2)]

        w0_in, weights_in = sem("w0_in"), sem("weights_in")
        w_out_scaled, cleared = sem("w_out_scaled"), sem("cleared")
        pool_consts = sem("pool_consts")
        consts = sem("consts")
        up_in, late_in = sem("up_in"), sem("late_in")
        xt_loaded = [sem(f"xt_loaded{s}") for s in range(4)]
        xt_stored = [sem(f"xt_stored{s}") for s in range(4)]
        xt_mm, xt_staged = sem("xt_mm"), sem("xt_staged")
        drow_in, dcol_in, evec_in = sem("drow_in"), sem("dcol_in"), sem("evec_in")
        dprep, ranges_ready, ranges_out, ranges_in = (
            sem("dprep"), sem("ranges_ready"), sem("ranges_out"), sem("ranges_in"))
        gen_ready, rel_ready, rel_out = sem("gen_ready"), sem("rel_ready"), sem("rel_out")
        norm_sq, norm_ready, vprep = sem("norm_sq"), sem("norm_ready"), sem("vprep")
        w0_split, w0_placed = sem("w0_split"), sem("w0_placed")
        bias_split, bias_out, bias_in = sem("bias_split"), sem("bias_out"), sem("bias_in")
        lengths_in, emb_stored = sem("lengths_in"), pair("emb_stored")
        r_ready, emb_mm, emb_sqd, emb_ready, emb_cast, emb_split = (
            sem("r_ready"), sem("emb_mm"), sem("emb_sqd"), sem("emb_ready"),
            sem("emb_cast"), sem("emb_split"))
        ids_loaded, emb_loaded, gathered = pair("ids_loaded"), pair("emb_loaded"), pair("gathered")
        h1_mm, h1_act, h2_mm, h2_act, w_mm = (
            sem("h1_mm"), sem("h1_act"), sem("h2_mm"), sem("h2_act"), sem("w_mm"))
        vstep, mid_ready, seg_done, acc_add, acc_all = (
            sem("vstep"), sem("mid_ready"), sem("seg_done"), sem("acc_add"), sem("acc_all"))
        relw_step, win_ready, win_done = sem("relw_step"), sem("win_ready"), sem("win_done")
        msum_ready, po_mm, y_ready, xin_loaded = (
            sem("msum_ready"), sem("po_mm"), sem("y_ready"), pair("xin_loaded"))
        bn_done, mv_ready, std_ready, rstd_ready, x1_ready = (
            sem("bn_done"), sem("mv_ready"), sem("std_ready"), sem("rstd_ready"), sem("x1_ready"))
        x1_kept, x1t_mm, x1t_copied, x1t_kept = (
            sem("x1_kept"), sem("x1t_mm"), sem("x1t_copied"), sem("x1t_kept"))
        tab_mm, tab_ready, tab_stored = sem("tab_mm"), sem("tab_ready"), pair("tab_stored")
        acc_cleared, var_a, var_b = sem("acc_cleared"), sem("var_a"), sem("var_b")
        fold_mm, fold_copied = sem("fold_mm"), sem("fold_copied")
        zero_set = sem("zero_set")
        side_summed, side_mm, side_copied, side_x_in = (
            sem("side_summed"), sem("side_mm"), sem("side_copied"), sem("side_x_in"))
        side_added, side_bn, side_var, side_std, side_rstd = (
            sem("side_added"), sem("side_bn"), sem("side_var"), sem("side_std"),
            sem("side_rstd"))
        side_ready, side_kept, side_stored = (
            sem("side_ready"), sem("side_kept"), sem("side_stored"))
        range_step = sem("range_step")
        side2_cnt, side2_means, side2_zstep, side2_stored = (
            sem("side2_cnt"), sem("side2_means"), sem("side2_zstep"), sem("side2_stored"))
        ids2_loaded, rel_loaded, pre_loaded, gathered2 = (
            pair("ids2_loaded"), pair("rel_loaded"), pair("pre_loaded"), pair("gathered2"))
        rel_spread, onehot_built = sem("rel_spread"), sem("onehot_built")
        gathered_b = pair("gathered_b")
        we_loaded = sem("we_loaded")
        oht_ready, pre_mm, sum_step, sums_ready, relu_done = (
            sem("oht_ready"), sem("pre_mm"), sem("sum_step"), sem("sums_ready"), sem("relu_done"))
        seg2_done, acc2_add, acc2_all = sem("seg2_done"), sem("acc2_add"), sem("acc2_all")
        relw2_step, win2_ready, win2_done = sem("relw2_step"), sem("win2_ready"), sem("win2_done")
        cnt_in, inbias_out, inv_loaded, some_loaded = (
            sem("cnt_in"), sem("inbias_out"), pair("inv_loaded"), pair("some_loaded"))
        cnt_ready, agg_ready, ph_mm, hu_ready, pu_mm = (
            sem("cnt_ready"), sem("agg_ready"), sem("ph_mm"),
            sem("hu_ready"), sem("pu_mm"))
        first_ready, bias_ready = sem("first_ready"), sem("bias_ready")
        t_ready, bna, stda, rstda, z_ready = (
            sem("t_ready"), sem("bna"), sem("stda"), sem("rstda"), sem("z_ready"))
        zg, zx = sem("zg"), sem("zx")
        bnb, stdb, rstdb, res_ready = sem("bnb"), sem("stdb"), sem("rstdb"), sem("res_ready")
        out_stored = pair("out_stored")

        passed = sem("passed")

        def hold(eng):
            eng.sem_inc(passed, 1)

        block = ctx.enter_context(nc.Block())

        ACT_TILES = 2
        N_WEIGHTS, N_LATE, N_COMBOS = 12, 11, 8
        combos = [(e, w) for e in range(3) for w in range(3)][:N_COMBOS]
        x_rows = a["x_rows"].rearrange("(q p) f -> p q f", p=P)
        x_table_rows = x_table.rearrange("(q p) f -> p q f", p=P)
        src_rows = src_table.rearrange("(q p) f -> p q f", p=P)
        dst_rows = dst_table.rearrange("(q p) f -> p q f", p=P)
        out_rows = out.rearrange("(q p) f -> p q f", p=P)

        @block.sync
        def _(sp):
            def load_xt(n, s, r):
                if live(n - 4, NC):
                    sp.wait_ge(xt_mm, n - 3)
                sp.dma_start(xt_in[s], quad(a["x_t"][:, bass.ds(n * CHUNK, CHUNK)])).then_inc(
                    xt_loaded[s], 16)
                if isinstance(n, int) and n == 1:
                    sp.wait_ge(cleared, 1)
                    for c in range(4):
                        sp.dma_start(w_up[32 * c:32 * c + 32, 32 * c:32 * c + 32],
                                     a["w_up0" if c == 0 else "w_up1"]).then_inc(up_in, 16)
                if isinstance(n, int) and n == 0:
                    sp.dma_start(drow_i, a["dst_row"]).then_inc(drow_in, 16)
                if isinstance(n, int) and n == 3:
                    sp.dma_start(lengths, a["lengths"]).then_inc(lengths_in, 16)
                if isinstance(n, int) and n == 7:
                    for k in range(2):
                        sp.dma_start(ids[k][:], a["ids"][k * P:k * P + P, :]).then_inc(
                            ids_loaded[k], 16)
            run_steps(sp, NC, 0, 8, load_xt, slots=4)
            sp.dma_start(rhat[:], a["evec"]).then_inc(evec_in, 16)

            def store_emb(k):
                sp.wait_ge(emb_split, 4 * k + 4)
                for part in range(3):
                    sp.dma_start(emb_d[part][k * P:k * P + P, :],
                                 emb_part[k % 2][part]).then_inc(emb_stored[k % 2], 16)
            store_emb(0)
            sp.dma_start(dcol_i, a["dst_col"]).then_inc(dcol_in, 16)

            sp.wait_ge(w0_split, 5)
            for b, (_, k) in enumerate(combos):
                sp.dma_start(w0_all[2 * NB * b:2 * NB * b + 2 * NB, :], w0_part[:, k, :]).then_inc(
                    w0_placed, 16)
            def rows(x):
                return x.unsqueeze(0).broadcast_to([P, F])

            late_loads = [
                (m_w2[:], a["m_w2"]), (u_w1[:, 1, :], a["u_w1"][F:2 * F, :]),
                (mb2[:], a["mb2"].unsqueeze(1)), (u_w1[:, 0, :], a["u_w1"][0:F, :]),
                (m_w1[:, 0, :], a["m_w1"][0:F, :]), (m_w1[:, 1, :], a["m_w1"][F:2 * F, :]),
                (ub1[:], a["ub1"].unsqueeze(1)), (u_w2[:], a["u_w2"]), (ub2[:], rows(a["ub2"])),
                (gamma[:], rows(a["gamma"])), (beta[:], rows(a["beta"]))]
            assert len(late_loads) == N_LATE < HEAD - 3

            def load_edges(n, s, r):
                if isinstance(n, int) and n % EMB_GROUPS == 0:
                    k = n // EMB_GROUPS
                    sp.wait_ge(emb_stored[k % 2], 48 * last(max(n // 2, 1), 2, k % 2))
                if live(n - 2, NG):
                    sp.wait_ge(gathered[s], 128 * r)
                    sp.dma_start(ids[s][:], a["ids"][bass.ds(n * P, P), :]).then_inc(
                        ids_loaded[s], 16)
                    sp.wait_ge(h1_mm, n - 1)
                row = 0
                for e in range(3):
                    times = sum(c[0] == e for c in combos)
                    sp.dma_start(
                        emb_in[s][row:row + 2 * NB * times, :],
                        along(emb_d[e][bass.ds(n * 2 * NB, 2 * NB), :], 0, times)).then_inc(
                            emb_loaded[s], 16)
                    row += 2 * NB * times
                if isinstance(n, int) and n == 1:
                    sp.wait_ge(rel_ready, 1)
                    sp.dma_start(rel_d, rel_row_b).then_inc(rel_out, 16)
                if isinstance(n, int) and n < N_LATE:
                    sp.dma_start(*late_loads[n]).then_inc(late_in, 16)
                if isinstance(n, int) and n % 2 == 1 and 1 <= n // 2 < NE:
                    store_emb(n // 2)
                if isinstance(n, int) and n == HEAD + 1:
                    for k in range(2):
                        sp.wait_ge(emb_stored[k], 48 * last(NE, 2, k))
            run_steps(sp, NG, 0, HEAD + 2, load_edges)

            def node_phase(first):
                steps = NC - first

                def nodes(n, s, r):
                    if live(n, steps):
                        if live(n - 2, steps):
                            sp.wait_ge(y_ready, 2 * n - 2)
                        sp.dma_start(xin[s], x_rows[:, bass.ds((n + first) * 4, 4), :]).then_inc(
                            xin_loaded[s], 16)
                    if live(n - 5, steps):
                        sp.wait_ge(tab_ready, n - 4)
                        rows = bass.ds((n + first - 5) * 4, 4)
                        sp.dma_start(src_rows[:, rows, :], tab[1 - s][:, :, 0:F]).then_inc(
                            tab_stored[1 - s], 16)
                        sp.dma_start(dst_rows[:, rows, :], tab[1 - s][:, :, F:2 * F]).then_inc(
                            tab_stored[1 - s], 16)
                run_steps(sp, steps, 5, 6, nodes)
                for s in range(2):
                    sp.wait_ge(tab_stored[s], 32 * last(steps, 2, s))

            for s in range(2):
                sp.wait_ge(gathered[s], 128 * last(NG, 2, s))
                sp.dma_start(ids[s][:], a["ids"][s * P:s * P + P, :]).then_inc(
                    ids2_loaded[s], 16)
            sp.wait_ge(acc_all, 1)
            for s in range(2):
                sp.dma_start(bwin[s][WR:P - 1, :], a["m_w1"][2 * F:2 * F + 2, :]).then_inc(
                    we_loaded, 16)
                sp.dma_start(bwin[s][P - 1:P, :], a["mb1"].unsqueeze(0)).then_inc(we_loaded, 16)
            general = sp.value_load(gen_i[0:1, 0:1], min_val=0, max_val=1)
            with sp.If(general == 1):
                node_phase(0)
            with sp.Else():
                node_phase(EARLY)
                sp.wait_ge(side_stored, 32 * EARLY + 1)
            sp.wait_ge(rel_out, 16)

            def load_edges2(n, s, r):
                if live(n - 2, NG):
                    sp.wait_ge(gathered2[s], 128 * r)
                    sp.dma_start(ids[s][:], a["ids"][bass.ds(n * P, P), :]).then_inc(
                        ids2_loaded[s], 16)
                if live(n - 2, NG):
                    sp.wait_ge(rel_spread, n - 1)
                sp.dma_start(rel_in[s][:], rel_d[bass.ds(n, 1), :]).then_inc(rel_loaded[s], 16)
                base = sp.value_load(base_sb[0:1, bass.ds(n, 1)], min_val=0, max_val=NP - W)
                if live(n - 2, NG):
                    sp.wait_ge(pre_mm, n - 1)
                sp.dma_start(onehot_t[s][WR:P, :], a["attr_rows"][bass.ds(n, 1), :, :]).then_inc(
                    pre_loaded[s], 16)
                sp.dma_start(bwin[s][0:WR, :], dst_table[bass.ds(base, WR), :]).then_inc(
                    pre_loaded[s], 16)
            run_steps(sp, NG, 0, 2, load_edges2)

            sp.wait_ge(acc2_all, 1)
            sp.dma_start(cnt_cols[:], acc[0:1, 1, :]).then_inc(cnt_in, 16)
            sp.wait_ge(cnt_ready, 3)
            sp.dma_start(cnt_inv_d.rearrange("o (p k) -> (o p) k", p=P), cnt_cols[:]).then_inc(
                inbias_out, 16)
            sp.dma_start(cnt_some_d.rearrange("o (p k) -> (o p) k", p=P), some_cols[:]).then_inc(
                inbias_out, 16)
            sp.wait_ge(inbias_out, 32)

            def last_phase(first):
                steps = NC - first

                def last_loads(n, s, r):
                    if live(n, steps) and not (isinstance(n, int) and n == 0):
                        cols = bass.ds((n + first) * CHUNK, CHUNK)
                        if live(n - 2, steps):
                            sp.wait_ge(agg_ready, n - 1)
                        sp.dma_start(cnt_inv[s], cnt_inv_d[:, cols].broadcast_to(
                            [P, CHUNK])).then_inc(inv_loaded[s], 16)
                        if live(n - 2, steps):
                            sp.wait_ge(ph_mm, n - 1)
                            hold(sp)
                        sp.dma_start(cnt_some[s], cnt_some_d[:, cols].broadcast_to(
                            [3, CHUNK])).then_inc(some_loaded[s], 16)
                    if live(n - 5, steps):
                        sp.wait_ge(res_ready, 4 * n - 16)
                        tiles = tiles_of(n - 5, steps)
                        sp.dma_start(out_rows[:, bass.ds((n + first - 5) * 4, tiles), :],
                                     res[1 - s][:, 0:tiles, :]).then_inc(out_stored[1 - s], 16)
                run_steps(sp, steps, 5, 6, last_loads)
                for s in range(2):
                    sp.wait_ge(out_stored[s], 16 * last(steps, 2, s))

            general = sp.value_load(gen_i[0:1, 0:1], min_val=0, max_val=1)
            with sp.If(general == 1):
                last_phase(0)
            with sp.Else():
                last_phase(EARLY)
                sp.wait_ge(side2_stored, 16 * EARLY + 1)

        @block.gpsimd
        def _(pool):
            pool.memset(ident[:], 0.0).then_inc(pool_consts, 1)
            pool.iota(iota_i[:], pattern=[[1, W]], base=0, channel_multiplier=0).then_inc(
                pool_consts, 1)
            pool.iota(part_i[:], pattern=[[0, 2]], base=0, channel_multiplier=1).then_inc(
                pool_consts, 1)
            columns = NE * P + NB
            pool.wait_ge(zero_set, 2)
            pool.affine_select(out=expand, in_=expand, compare_op=ALU.is_ge, fill=0.0, base=-NB,
                               pattern=[[1, columns]], channel_multiplier=-2 * NB).then_inc(
                                   pool_consts, 1)
            pool.wait_ge(pool_consts, 4)
            pool.affine_select(out=expand, in_=expand, compare_op=ALU.is_ge, fill=0.0,
                               base=2 * NB - 1, pattern=[[-1, columns]],
                               channel_multiplier=2 * NB).then_inc(pool_consts, 1)
            pool.affine_select(out=ident[:], in_=ident[:], compare_op=ALU.not_equal, fill=1.0,
                               base=0, pattern=[[-1, P]], channel_multiplier=1).then_inc(
                                   pool_consts, 1)

            def load(dst, src):
                pool.dma_start(dst, src).then_inc(weights_in, 16)

            pool.wait_ge(cleared, 5)
            for h in range(2):
                rows = slice(h * HID, h * HID + HID)
                load(w1[rows, rows], a["mlp_w1"])
                load(w2[rows, h, :], a["mlp_w2"])
                load(b0[rows, :], a["mlp_b0"].unsqueeze(1))
                load(b1[rows, :], a["mlp_b1"].unsqueeze(1))
            load(w_out[0:64, 0, 0:32], a["w_out0"])
            load(w_out[64:128, 0, 32:64], a["w_out1"])
            load(w_out[0:64, 1, 0:32], a["w_out1"])
            load(w_out[64:128, 1, 32:64], a["w_out1"])
            pool.memset(acc[:, 1, :], 0.0).then_inc(acc_cleared, 1)

            pool.wait_ge(weights_in, 16 * N_WEIGHTS)
            pool.wait_ge(acc_cleared, 2)
            pool.tensor_scalar(w_out[:], w_out[:], OUT_SCALE, None, ALU.mult).then_inc(
                w_out_scaled, 1)
            for k, (rows, c) in enumerate(((slice(64, 96), 0), (slice(0, 32), 1),
                                           (slice(64, 96), 1))):
                pool.wait_ge(w_out_scaled, k + 1)
                pool.tensor_scalar(w_out[rows, c, :], w_out[rows, c, :], SQ3, None,
                                   ALU.mult).then_inc(w_out_scaled, 1)
            pool.wait_ge(w_out_scaled, 4)

            for s in range(4):
                pool.wait_ge(xt_stored[s], 16 * last(NC, 4, s))

            def gather(n, s, r):
                pool.wait_ge(ids_loaded[s], 16 * r + 16)
                if live(n - 2, NG):
                    pool.wait_ge(mid_ready, n - 1)
                    hold(pool)
                for t in range(TPG):
                    pool.indirect_dma_start(
                        out=gx[s][:, t, :], out_offset=None, in_=x_table,
                        in_offset=bass.IndirectOffsetOnAxis(ap=ids[s][:, t:t + 1], axis=0),
                    ).then_inc(gathered[s], 16)
            run_steps(pool, NG, 0, 2, gather)

            pool.wait_ge(late_in, 16 * N_LATE)

            def keep_phase(first):
                steps = NC - first

                def keep(n, s, r):
                    pool.wait_ge(x1_ready, 4 * n + 4)
                    pool.tensor_tensor(x1n[:, bass.ds((n + first) * 4, 4), :], x1s[s],
                                       along(beta[:], 1, 4), ALU.add).then_inc(x1_kept, 1)
                    pool.wait_ge(x1t_copied, n + 1)
                    pool.tensor_copy(x1T[:, bass.ds((n + first) * CHUNK, CHUNK)],
                                     x1Ts[s]).then_inc(x1t_kept, 1)
                run_steps(pool, steps, 0, 2, keep)
                pool.wait_ge(x1_kept, steps)
                pool.wait_ge(x1t_kept, steps)
                for s in range(2):
                    pool.wait_ge(tab_stored[s], 32 * last(steps, 2, s))

            def last_phase(first):
                steps = NC - first
                pool.wait_ge(acc2_all, 1)
                pool.wait_ge(first_ready, 4)

                def finish(n, s, r):
                    if live(n, steps):
                        if not isinstance(n, int) or n > 0:
                            pool.wait_ge(inv_loaded[s], 16 * (r + s))
                        if live(n - 2, steps):
                            pool.wait_ge(ph_mm, n - 1)
                        cols = bass.ds((n + first) * CHUNK, CHUNK)
                        pool.tensor_tensor(agg[s], acc[:, 0, cols], cnt_inv[s],
                                           ALU.mult).then_inc(agg_ready, 1)
                    if live(n - 2, steps):
                        pool.wait_ge(z_ready, 4 * n - 4)
                        tiles = tiles_of(n - 2, steps)
                        z_rows = z[s][:, 0:tiles, :]
                        pool.tensor_tensor(z_rows, z_rows, along(gamma[:], 1, tiles),
                                           ALU.mult).then_inc(zg, 1)
                        pool.wait_ge(zg, n - 1)
                        pool.tensor_tensor(
                            z_rows, z_rows, x1n[:, bass.ds((n + first - 2) * 4, tiles), :],
                            ALU.add).then_inc(zx, 1)
                run_steps(pool, steps, 2, 4, finish)

            def gathers2(general):
                def gather2(n, s, r):
                    pool.wait_ge(ids2_loaded[s], 16 * r + 16)
                    if live(n - 2, NG):
                        pool.wait_ge(sums_ready, n - 1)
                        hold(pool)
                    if general:
                        for t in range(TPG):
                            pool.indirect_dma_start(
                                out=gb[s][:, t, :], out_offset=None, in_=dst_table,
                                in_offset=bass.IndirectOffsetOnAxis(
                                    ap=ids[s][:, TPG + t:TPG + t + 1], axis=0),
                            ).then_inc(gathered_b[s], 16)
                        pool.wait_ge(gathered_b[s], 128 * r + 128)
                        hold(pool)
                    for t in range(TPG):
                        pool.indirect_dma_start(
                            out=gx[s][:, t, :], out_offset=None, in_=src_table,
                            in_offset=bass.IndirectOffsetOnAxis(ap=ids[s][:, t:t + 1], axis=0),
                        ).then_inc(gathered2[s], 16)
                run_steps(pool, NG, 0, 2, gather2)

            general = pool.value_load(gen_i[0:1, 0:1], min_val=0, max_val=1)
            with pool.If(general == 1):
                keep_phase(0)
                gathers2(True)
                last_phase(0)
            with pool.Else():
                keep_phase(EARLY)
                pool.wait_ge(side_stored, 32 * EARLY + 1)
                gathers2(False)
                last_phase(EARLY)

        @block.scalar
        def _(act):
            act.dma_start(b2_row[:], a["mlp_b2"].unsqueeze(0)).then_inc(w0_in, 16)
            act.wait_ge(cleared, 2)
            act.dma_start(w0[0:NB, 0:HID], a["mlp_w0"]).then_inc(w0_in, 16)
            act.dma_start(w0[NB:2 * NB, HID:P], a["mlp_w0"]).then_inc(w0_in, 16)
            act.wait_ge(zero_set, 1)
            act.copy(acc[:, 0, :], zero[:, 0:1].broadcast_to([P, NP])).then_inc(acc_cleared, 1)

            act.wait_ge(consts, 1)

            def embed(k, s):
                act.wait_ge(emb_mm, k + 1)
                act.activation(emb_sq[s], ps[:, 4 + k if k < EMB_AHEAD else 0, :], ACT.Square,
                               bias=center[:, 0:1], scale=float(NB - 1)).then_inc(emb_sqd, 1)
                act.wait_ge(emb_sqd, k + 1)
                if k >= 2:
                    act.wait_ge(emb_split, 4 * k - 4)
                act.activation(emb_rest[s], emb_sq[s], ACT.Exp, scale=-0.5).then_inc(emb_ready, 1)

            def stage_xt(n, s, r):
                act.wait_ge(xt_mm, n + 1)
                if live(n - 4, NC):
                    act.wait_ge(xt_stored[s], 16 * r)
                act.activation(xt_stage[s], quad(ps[:, s, :]), ACT.Copy,
                               scale=1.0 / MUL ** 0.5).then_inc(xt_staged, 1)
                act.wait_ge(xt_staged, n + 1)
                act.dma_start(x_table_rows[:, bass.ds(n * 4, 4), :], xt_stage[s]).then_inc(
                    xt_stored[s], 16)
                if isinstance(n, int) and n == 4:
                    act.wait_ge(ranges_ready, 1)
                    act.dma_start(base_f_d, small[0:NG, 0:1]).then_inc(ranges_out, 16)
                    act.dma_start(span_d, small[0:NG, 2:3]).then_inc(ranges_out, 16)
                    act.dma_start(base_i_d, small_i[0:NG, 0:1]).then_inc(ranges_out, 16)
                if isinstance(n, int) and n == 7:
                    act.wait_ge(ranges_out, 48)
                    for dst, src in ((base_all, base_f_d), (span_all, span_d)):
                        act.dma_start(dst, src.rearrange("g h -> (g h)").unsqueeze(0).broadcast_to(
                            [P, NG])).then_inc(ranges_in, 16)
                    act.dma_start(base_sb[:], base_i_d.rearrange("g h -> (g h)").unsqueeze(
                        0)).then_inc(ranges_in, 16)
                if isinstance(n, int) and n == 6:
                    act.wait_ge(bias_split, 5)
                    act.dma_start(b2_parts_d, b2_part[:].rearrange("o k f -> o (k f)")).then_inc(
                        bias_out, 16)
                if isinstance(n, int) and n == 7:
                    embed(0, 0)
            run_steps(act, NC, 0, 8, stage_xt, slots=4)

            embed(1, 1)
            act.preload_act_table(ACT.Sqrt)
            act.wait_ge(bias_out, 16)
            parts = b2_parts_d.rearrange("o (k f) -> (o k) f", k=3)
            for q in range(4):
                act.dma_start(b2p[:, q, :], parts).then_inc(bias_in, 16)

            act.wait_ge(norm_sq, 1)
            act.activation(norm, norm, ACT.Sqrt).then_inc(norm_ready, 1)

            act.preload_act_table(ACT.Silu)

            def side(c, part):
                if part == 0:
                    act.wait_ge(acc_add, (c + SIDE_LAG) * BODY - 3)
                    act.wait_ge(emb_split, 4 * NE)
                    act.copy(side_sum, acc[:, :, bass.ds(c * CHUNK, CHUNK)]).then_inc(
                        side_summed, 1)
                    act.dma_start(side_x, x_rows[:, bass.ds(c * 4, 4), :]).then_inc(side_x_in, 16)
                    act.wait_ge(side_mm, c * 4 + 1)
                    out_s = quad(ps[:, 0, :])
                    act.copy(side_y[:, :, 0:MUL], out_s[:, :, 0:MUL])
                    act.copy(side_y[:, :, MUL:].rearrange("p q (k c) -> p q c k", c=3),
                             out_s[:, :, MUL:].rearrange("p q (c k) -> p q c k", c=3)).then_inc(
                                 side_copied, 1)
                if part == 3:
                    act.wait_ge(side_var, c * 4 + 4)
                    act.activation(std[0][:], mean_var[0][:, :, 1], ACT.Sqrt,
                                   bias=eps[:, 0:1]).then_inc(side_std, 1)
                if part == 5:
                    act.wait_ge(side_mm, c * 4 + 2)
                    act.copy(x1T[:, bass.ds(c * CHUNK, CHUNK)], ps[:, 0, :])
                    act.copy(side_x1T, ps[:, 0, :]).then_inc(side_copied, 1)
                if part == 6:
                    act.wait_ge(emb_stored[0], 48 * last(NE, 2, 0))
                    act.wait_ge(side_stored, c * 32 + 1)
                if part in (6, 7):
                    h = part - 6
                    act.wait_ge(side_mm, c * 4 + 3 + h)
                    act.copy(side_tab[:, :, h * F:h * F + F], quad(ps[:, 0, :])).then_inc(
                        side_copied, 1)
                    act.wait_ge(side_copied, c * 4 + 3 + h)
                    table = (src_rows, dst_rows)[h]
                    act.dma_start(table[:, bass.ds(c * 4, 4), :],
                                  side_tab[:, :, h * F:h * F + F]).then_inc(side_stored, 16)

            def mlp(n, s, r, beside=None):
                if live(n - 1, NG):
                    act.wait_ge(h2_mm, n)
                    if live(n - 3, NG):
                        act.wait_ge(w_mm, n - 2)
                    act.activation(hid[1 - s][:, 1, :], ps[:, 1, :], ACT.Silu,
                                   bias=b1[:, 0:1]).then_inc(h2_act, 1)
                if live(n, NG):
                    act.wait_ge(h1_mm, n + 1)
                    if live(n - 2, NG):
                        act.wait_ge(h2_mm, n - 1)
                    act.activation(hid[s][:, 0, :], ps[:, 0, :], ACT.Silu,
                                   bias=b0[:, 0:1]).then_inc(h1_act, 1)
                if emb_beside(n):
                    embed(emb_beside(n), emb_beside(n) % 2)
                if isinstance(n, int) and n == HEAD - 3:
                    act.wait_ge(fold_mm, 1)
                    act.copy(m_w2T, ps[:, 0, 0:P]).then_inc(fold_copied, 1)
                if isinstance(n, int) and n == HEAD - 1:
                    act.wait_ge(fold_mm, 2)
                    act.copy(mu_w[:], ps[:, 0, 0:F])
                    act.copy(v_row[:, 0:F], ps[0:1, 0, F:2 * F]).then_inc(fold_copied, 1)
                if beside:
                    side(*beside)
            act.wait_ge(weights_in, 16 * N_WEIGHTS)

            def node_phase(first):
                steps = NC - first
                act.preload_act_table(ACT.Sqrt)
                act.wait_ge(acc_all, 1)

                def nodes(n, s, r):
                    o = 1 - s
                    if live(n, steps):
                        if live(n - 2, steps):
                            act.wait_ge(po_mm, n - 1)
                        act.copy(msum[s], acc[:, :, bass.ds((n + first) * CHUNK, CHUNK)]).then_inc(
                            msum_ready, 1)
                    if live(n - 4, steps):
                        act.wait_ge(x1t_mm, n - 3)
                        if live(n - 6, steps):
                            act.wait_ge(tab_mm, n - 5)
                            act.wait_ge(x1t_kept, n - 5)
                        act.copy(x1Ts[s], ps[:, 2 + s, :]).then_inc(x1t_copied, 1)
                    if live(n - 5, steps):
                        act.wait_ge(tab_mm, n - 4)
                        if live(n - 7, steps):
                            act.wait_ge(tab_stored[o], 32 * (r + s - 3))
                        act.copy(tab[o].rearrange("p q (h f) -> p h q f", h=2),
                                 ps[:, 4 + 2 * o:6 + 2 * o, :].rearrange(
                                     "p h (q f) -> p h q f", f=F)).then_inc(tab_ready, 1)
                    if live(n - 2, steps):
                        act.wait_ge(mv_ready, 4 * n - 4)
                        act.activation(std[s][:], mean_var[s][:, :, 1], ACT.Sqrt,
                                       bias=eps[:, 0:1]).then_inc(std_ready, 1)
                run_steps(act, steps, 5, 8, nodes)

            act.sem_inc(side_stored, 1)
            act.wait_ge(gen_ready, 1)
            general = act.value_load(gen_i[0:1, 0:1], min_val=0, max_val=1)
            with act.If(general == 1):
                run_steps(act, NG, 1, HEAD, mlp)
                node_phase(0)
            with act.Else():
                run_passes(act, 1, HEAD, mlp)
                node_phase(EARLY)

            act.copy(acc[:].rearrange("p c n -> p (c n)"),
                     zero[:, 0:1].broadcast_to([P, 2 * NP])).then_inc(acc_cleared, 1)
            act.wait_ge(bias_split, 10)
            act.dma_start(v_parts_d, v_part.rearrange("o k f -> o (k f)")).then_inc(bias_out, 16)
            act.wait_ge(bias_out, 32)
            act.dma_start(v_rows[:], v_parts_d.rearrange("o (k f) -> (o k) f", k=3)).then_inc(
                bias_in, 16)

            def side2(c, part):
                if part == 1:
                    act.wait_ge(side_mm, EARLY * 4 + c * 2 + 1)
                    act.activation(side2_h, ps[:, 6, :], ACT.Relu, bias=ub1[:, 0:1]).then_inc(
                        side_copied, 1)
                if part == 2:
                    act.wait_ge(side_mm, EARLY * 4 + c * 2 + 2)
                    act.copy(side2_t, quad(ps[:, 6, :])).then_inc(side_copied, 1)
                if part == 4:
                    act.wait_ge(side_var, (EARLY + c * 2) * 4 + 4)
                    act.activation(std[0][:], mean_var[0][:, :, 1], ACT.Sqrt,
                                   bias=eps[:, 0:1]).then_inc(side_std, 1)
                if part == 6:
                    act.wait_ge(side_var, (EARLY + c * 2) * 4 + 8)
                    act.activation(std_b[0][:], mean_var_b[0][:, :, 1], ACT.Sqrt,
                                   bias=eps[:, 0:1]).then_inc(side_std, 1)
                if part == 7:
                    act.wait_ge(side_ready, EARLY * 4 + c * 4 + 4)
                    act.dma_start(out_rows[:, bass.ds(c * 4, 4), :], side2_res).then_inc(
                        side2_stored, 16)

            def relu(n, s, r, beside=None):
                if live(n, NG):
                    act.wait_ge(onehot_built, n + 1)
                    if live(n - 2, NG):
                        act.wait_ge(seg2_done, n - 1)
                    act.copy(onehot_b[s][:], onehot[s][:])
                    act.wait_ge(sums_ready, n + 1)
                    act.activation(hrelu[s][:], sums[s], ACT.Relu).then_inc(relu_done, 1)
                if beside:
                    side2(*beside)

            def normalize(dst, src, rstd, shifts, done, tiles):
                for q in tiles:
                    act.activation(dst[:, q, :], src[:, q, :], ACT.Identity,
                                   bias=shifts[:, q:q + 1], scale=rstd[:, q:q + 1]).then_inc(
                                       done, 1)

            def last_phase(first):
                steps = NC - first

                def update(n, s, r):
                    o = 1 - s
                    if live(n - 1, steps):
                        act.wait_ge(ph_mm, n)
                        if live(n - 3, steps):
                            act.wait_ge(pu_mm, n - 2)
                        act.activation(h_u[o], ps[:, 2 + o, :], ACT.Relu,
                                       bias=ub1[:, 0:1]).then_inc(hu_ready, 1)
                    if live(n - 2, steps):
                        act.wait_ge(var_a, 4 * n - 4)
                        act.activation(std[s][:], mean_var[s][:, :, 1], ACT.Sqrt,
                                       bias=eps[:, 0:1]).then_inc(stda, 1)
                    if live(n - 4, steps):
                        act.wait_ge(rstdb, 2 * n - 6)
                        if live(n - 6, steps):
                            act.wait_ge(out_stored[s], 16 * r - 32)
                        normalize(res[s], z[s], std_b[s], shift_b[s], res_ready, range(ACT_TILES))
                    if live(n - 2, steps):
                        act.wait_ge(rstda, 2 * n - 2)
                        if live(n - 4, steps):
                            act.wait_ge(res_ready, 4 * n - 12)
                        normalize(z[s], t_sum[s], std[s], shift[s], z_ready, range(4))
                    if live(n - 3, steps):
                        act.wait_ge(var_b, 4 * n - 8)
                        act.activation(std_b[o][:], mean_var_b[o][:, :, 1], ACT.Sqrt,
                                       bias=eps[:, 0:1]).then_inc(stdb, 1)
                run_steps(act, steps, 4, 6, update)

            act.sem_inc(side2_stored, 1)
            with act.If(general == 1):
                run_steps(act, NG, 0, 2, relu)
                last_phase(0)
            with act.Else():
                run_passes(act, 0, BODY, relu)
                last_phase(EARLY)

        @block.tensor
        def _(pe):
            pe.wait_ge(up_in, 64)

            def spread(k):
                if k > EMB_AHEAD:
                    pe.wait_ge(emb_sqd, k)
                bank = 4 + k if k < EMB_AHEAD else 0
                for h in range(2):
                    first = k * P + NB * (1 - h)
                    mm = pe.matmul(ps[:, bank, :], expand[:, first:first + P],
                                   lengths[:, h * HALF:h * HALF + HALF], start=(h == 0),
                                   stop=(h == 1))
                mm.then_inc(emb_mm, 1)

            def project(n, s, r):
                pe.wait_ge(xt_loaded[s], 16 * r + 16)
                if live(n - 4, NC):
                    pe.wait_ge(xt_staged, n - 3)
                for q in range(4):
                    mm = pe.matmul(ps[:, s, q * F:q * F + F], xt_in[s][:, q, :], w_up[:],
                                   start=True, stop=True)
                mm.then_inc(xt_mm, 1)
                if isinstance(n, int) and n == 5:
                    pe.wait_ge(pool_consts, 5)
                    pe.wait_ge(r_ready, 3)
                    spread(0)
            run_steps(pe, NC, 0, 8, project, slots=4)

            spread(1)

            pe.wait_ge(w0_placed, 16 * N_COMBOS)
            pe.wait_ge(consts, 1)
            pe.wait_ge(weights_in, 16 * N_WEIGHTS)
            pe.wait_ge(bias_in, 64)

            def first_layer(n, s, r):
                pe.wait_ge(emb_loaded[s], 48 * r + 48)
                if live(n - 1, NG):
                    pe.wait_ge(h1_act, n)
                if isinstance(n, int):
                    pe.wait_ge(emb_sqd, max(n - 1, 0) // 2 + EMB_AHEAD)
                pe.matmul(ps[:, 0, :], w0_all[:], emb_in[s][:], start=True, stop=True).then_inc(
                    h1_mm, 1)

            def second_layer(m, s):
                if live(m - 2, NG):
                    pe.wait_ge(mid_ready, m - 1)
                for h in range(2):
                    pe.matmul(ps[:, 2 + 2 * s + h, :], ones_bf[0:3, :],
                              b2p[:].rearrange("k q f -> k (q f)"), start=True, stop=False)
                pe.wait_ge(h1_act, m + 1)
                if live(m - 1, NG):
                    pe.wait_ge(h2_act, m)
                pe.matmul(ps[:, 1, :], w1[:], hid[s][:, 0, :], start=True, stop=True).then_inc(
                    h2_mm, 1)

            def third_layer(m, s):
                pe.wait_ge(h2_act, m + 1)
                for h in range(2):
                    for t in range(4):
                        mm = pe.matmul(ps[:, 2 + 2 * s + h, t * F:t * F + F],
                                       hid[s][:, 1, t * P:t * P + P], w2[:, h, :],
                                       start=False, stop=(t == 3))
                mm.then_inc(w_mm, 1)

            def side(c, part):
                bank = quad(ps[:, 0, :])
                group = (c + SIDE_LAG) * BODY + part
                if part in (0, 5, 6, 7):
                    pe.wait_ge(h1_act, group + 1)
                if part == 0:
                    pe.wait_ge(side_summed, c + 1)
                    for q in range(4):
                        for h in range(2):
                            mm = pe.matmul(bank[:, q, h * 64:h * 64 + 64],
                                           side_sum[:, h, q * P:q * P + P], w_out[:, h, :],
                                           start=True, stop=True)
                if part == 5:
                    pe.wait_ge(side_ready, c * 4 + 4)
                    for q in range(4):
                        mm = pe.transpose(bank[:, q, :], side_x1[:, q, :], ident[:])
                if part in (6, 7):
                    for q in range(4):
                        mm = pe.matmul(bank[:, q, :], side_x1T[:, q * P:q * P + P],
                                       m_w1[:, part - 6, :], start=True, stop=True)
                if part in (0, 5, 6, 7):
                    mm.then_inc(side_mm, 1)

            def layer1(general):
                def step(n, s, r, beside=None):
                    if live(n - 1, NG):
                        second_layer(n - 1, 1 - s)
                    if live(n, NG):
                        if beside and beside[1] in (1, 6, 7):
                            pe.wait_ge(side_copied, beside[0] * 4 + (1, 6, 7).index(
                                beside[1]) + 1)
                        first_layer(n, s, r)
                    if live(n - 1, NG):
                        third_layer(n - 1, 1 - s)
                    if emb_beside(n):
                        pe.wait_ge(h1_act, n + 1)
                        spread(emb_beside(n))
                    if beside:
                        side(*beside)
                    if isinstance(n, int) and n == HEAD - 3:
                        pe.wait_ge(late_in, 16 * N_LATE)
                        pe.wait_ge(pool_consts, 6)
                        pe.wait_ge(h1_act, n + 1)
                        pe.transpose(ps[:, 0, 0:P], m_w2[:], ident[:]).then_inc(fold_mm, 1)
                        pe.wait_ge(fold_copied, 1)
                    if isinstance(n, int) and n == HEAD - 1:
                        pe.wait_ge(h1_act, n + 1)
                        pe.matmul(ps[:, 0, 0:F], m_w2T, u_w1[:, 1, :], start=True, stop=True)
                        pe.matmul(ps[0:1, 0, F:2 * F], mb2[:], u_w1[:, 1, :], start=True,
                                  stop=True).then_inc(fold_mm, 1)
                        pe.wait_ge(fold_copied, 2)
                    if live(n - 2, NG):
                        pe.wait_ge(mid_ready, n - 1)
                        if general:
                            hold(pe)
                            with pe.Fori(0, NW) as w:
                                pe.wait_ge(win_ready, (n - 2) * NW + w + 1)
                                for c in range(2):
                                    for t in range(TPG):
                                        mm = pe.matmul(
                                            ps[:, 6, c * W:c * W + W],
                                            mid[s][:, t, c * F:c * F + F],
                                            onehot[s][:, t, :], start=(t == 0),
                                            stop=(t == TPG - 1))
                                mm.then_inc(win_done, 1)
                            return
                        if live(n - 4, NG):
                            pe.wait_ge(acc_add, n - 3)
                        for c in range(2):
                            for t in range(TPG):
                                mm = pe.matmul(ps[:, 6 + s, c * W:c * W + W],
                                               mid[s][:, t, c * F:c * F + F],
                                               onehot[s][:, t, :], start=(t == 0),
                                               stop=(t == TPG - 1))
                        mm.then_inc(seg_done, 1)
                    if beside and beside[1] == BODY - 1:
                        pe.wait_ge(side_copied, beside[0] * 4 + 4)
                if general:
                    run_steps(pe, NG, 2, HEAD, step)
                else:
                    run_passes(pe, 2, HEAD, step)

            def node_phase(first):
                steps = NC - first

                def nodes(n, s, r):
                    o = 1 - s
                    if live(n, steps):
                        pe.wait_ge(msum_ready, n + 1)
                        if live(n - 2, steps):
                            pe.wait_ge(y_ready, 2 * n - 2)
                        for q in range(4):
                            for c in range(2):
                                mm = pe.matmul(ps[:, s, q * F + c * 64:q * F + c * 64 + 64],
                                               msum[s][:, c, q * P:q * P + P], w_out[:, c, :],
                                               start=True, stop=True)
                        mm.then_inc(po_mm, 1)
                    if live(n - 2, steps):
                        pe.wait_ge(x1_ready, 4 * n - 4)
                        if live(n - 4, steps):
                            pe.wait_ge(x1t_copied, n - 3)
                        for q in range(4):
                            mm = pe.transpose(ps[:, 2 + s, q * P:q * P + P], x1s[s][:, q, :],
                                              ident[:])
                        mm.then_inc(x1t_mm, 1)
                    if live(n - 3, steps):
                        pe.wait_ge(x1t_copied, n - 2)
                        if live(n - 5, steps):
                            pe.wait_ge(tab_ready, n - 4)
                        for h in range(2):
                            for q in range(4):
                                mm = pe.matmul(ps[:, 4 + 2 * o + h, q * F:q * F + F],
                                               x1Ts[o][:, q * P:q * P + P], m_w1[:, h, :],
                                               start=True, stop=True)
                        mm.then_inc(tab_mm, 1)
                run_steps(pe, steps, 3, 6, nodes)

            pe.wait_ge(w_out_scaled, 4)
            pe.wait_ge(gen_ready, 1)
            general = pe.value_load(gen_i[0:1, 0:1], min_val=0, max_val=1)
            with pe.If(general == 1):
                layer1(True)
                node_phase(0)
            with pe.Else():
                layer1(False)
                node_phase(EARLY)

            pe.wait_ge(we_loaded, 64)

            def side2(c, part):
                if part == 2:
                    cols = bass.ds(c * CHUNK, CHUNK)
                    pe.matmul(ps[:, 6, :], u_w1[:, 0, :], x1T[:, cols], start=True, stop=False)
                    pe.wait_ge(side2_cnt, c * 3 + 2)
                    pe.matmul(ps[:, 6, :], v_rows[:, 0:F], side2_some, start=False, stop=False)
                    pe.wait_ge(side2_means, c + 1)
                    pe.matmul(ps[:, 6, :], mu_w[:], side2_agg, start=False, stop=True).then_inc(
                        side_mm, 1)
                if part == 3:
                    pe.wait_ge(side_copied, EARLY * 4 + c * 2 + 1)
                    pe.matmul(ps[:, 6, :], ones_bf[0:3, :], along(v_rows[:, F:2 * F], 1, 4),
                              start=True, stop=False)
                    for q in range(4):
                        mm = pe.matmul(ps[:, 6, q * F:q * F + F], side2_h[:, q * P:q * P + P],
                                       u_w2[:], start=False, stop=(q == 3))
                    mm.then_inc(side_mm, 1)

            def layer2(general):
                def step(n, s, r, beside=None):
                    if beside and beside[1] in (3, 4):
                        pe.wait_ge(side_copied, EARLY * 4 + beside[0] * 2 + (beside[1] - 2))
                    if live(n, NG):
                        pe.wait_ge(rel_loaded[s], 16 * r + 16)
                        if live(n - 1, NG):
                            pe.wait_ge(oht_ready, n)
                        for h in range(2):
                            mm = pe.matmul(ps[:, 6 + h, :], ones_bf[0:1, :],
                                           rel_in[s][:, h * HALF:h * HALF + HALF], start=True,
                                           stop=True)
                        mm.then_inc(rel_spread, 1)
                    if live(n - 1, NG):
                        o = 1 - s
                        pe.wait_ge(oht_ready, n)
                        pe.wait_ge(pre_loaded[o], 32 * (r + s))
                        if live(n - 3, NG):
                            pe.wait_ge(sums_ready, n - 2)
                        for t in range(TPG):
                            col = (t % 4) * F
                            mm = pe.matmul(ps[:, 2 * o + t // 4, col:col + F],
                                           onehot_t[o][:, t * P:t * P + P], bwin[o][:],
                                           start=True, stop=True)
                        mm.then_inc(pre_mm, 1)
                    if beside and beside[1] in (2, 3):
                        pe.wait_ge(oht_ready, n + 1)
                        side2(*beside)
                    if live(n - 2, NG):
                        pe.wait_ge(relu_done, n - 1)
                        if general:
                            hold(pe)
                            with pe.Fori(0, NW) as w:
                                pe.wait_ge(win2_ready, (n - 2) * NW + w + 1)
                                for c in range(2):
                                    for t in range(TPG):
                                        mm = pe.matmul(
                                            ps[:, 4, c * W:c * W + W],
                                            hrelu[s][:, t, :] if c == 0 else ones[:],
                                            onehot[s][:, t, :], start=(t == 0),
                                            stop=(t == TPG - 1))
                                mm.then_inc(win2_done, 1)
                            pe.sem_inc(seg2_done, 1)
                            return
                        if live(n - 4, NG):
                            pe.wait_ge(acc2_add, n - 3)
                        for c in range(2):
                            for t in range(TPG):
                                mm = pe.matmul(
                                    ps[:, 4 + s, c * W:c * W + W],
                                    hrelu[s][:, t, :] if c == 0 else ones_bf[:],
                                    onehot[s][:, t, :] if c == 0 else onehot_b[s][:, t, :],
                                    start=(t == 0), stop=(t == TPG - 1))
                        mm.then_inc(seg2_done, 1)
                if general:
                    run_steps(pe, NG, 2, 4, step)
                else:
                    run_passes(pe, 2, BODY, step)

            def last_phase(first):
                steps = NC - first
                pe.wait_ge(acc2_all, 1)

                def update(n, s, r):
                    o = 1 - s
                    if live(n - 1, steps):
                        pe.wait_ge(hu_ready, n)
                        if live(n - 3, steps):
                            pe.wait_ge(t_ready, n - 2)
                        pe.matmul(ps[:, 4 + o, :], ones_bf[0:3, :],
                                  along(v_rows[:, F:2 * F], 1, 4), start=True, stop=False)
                        for q in range(4):
                            mm = pe.matmul(ps[:, 4 + o, q * F:q * F + F],
                                           h_u[o][:, q * P:q * P + P], u_w2[:], start=False,
                                           stop=(q == 3))
                        mm.then_inc(pu_mm, 1)
                    if live(n, steps):
                        if live(n - 2, steps):
                            pe.wait_ge(hu_ready, n - 1)
                        cols = bass.ds((n + first) * CHUNK, CHUNK)
                        pe.matmul(ps[:, 2 + s, :], u_w1[:, 0, :], x1T[:, cols],
                                  start=True, stop=False)
                        if isinstance(n, int) and n == 0:
                            pe.wait_ge(first_ready, 2)
                        else:
                            pe.wait_ge(some_loaded[s], 16 * (r + s))
                        pe.matmul(ps[:, 2 + s, :], v_rows[:, 0:F], cnt_some[s], start=False,
                                  stop=False)
                        pe.wait_ge(agg_ready, n + 1)
                        pe.matmul(ps[:, 2 + s, :], mu_w[:], agg[s], start=False,
                                  stop=True).then_inc(ph_mm, 1)
                run_steps(pe, steps, 1, 4, update)

            pe.wait_ge(bias_in, 80)
            general = pe.value_load(gen_i[0:1, 0:1], min_val=0, max_val=1)
            with pe.If(general == 1):
                layer2(True)
                last_phase(0)
            with pe.Else():
                layer2(False)
                last_phase(EARLY)

        @block.vector
        def _(dve):
            for t in (w_up, w0, w1, w2, w_out):
                dve.memset(t[:], 0.0).then_inc(cleared, 1)
            dve.memset(zero[:], 0.0).then_inc(zero_set, 1)
            dve.memset(expand, 1.0).then_inc(zero_set, 1)
            dve.memset(ones[:], 1.0)
            dve.memset(ones_bf[:], 1.0)
            dve.memset(eps[:], LN_EPS)
            dve.wait_ge(pool_consts, 3)
            dve.tensor_copy(iota_n[:], iota_i[:])
            dve.tensor_copy(iota_p[:], part_i[:, 0:1])
            dve.tensor_scalar(part_i[:, 1:2], part_i[:, 0:1], NB - 1, None,
                              ALU.bitwise_and).then_inc(dprep, 1)
            dve.wait_ge(dprep, 1)
            dve.tensor_copy(center[:], part_i[:, 1:2]).then_inc(dprep, 1)
            dve.wait_ge(dprep, 2)
            dve.tensor_scalar(center[:], center[:], -1.0, None, ALU.mult).then_inc(consts, 1)

            dve.wait_ge(drow_in, 16)
            dve.tensor_copy(drow, drow_i).then_inc(dprep, 1)
            dve.wait_ge(dprep, 3)
            dve.tensor_reduce(small[0:NG, 0:1], drow, AX, ALU.min).then_inc(dprep, 1)
            dve.tensor_reduce(small[0:NG, 1:2], drow, AX, ALU.max).then_inc(dprep, 1)
            dve.wait_ge(dprep, 5)
            dve.tensor_copy(small_i[0:NG, 0:1], small[0:NG, 0:1])
            base, high, span, due, late = (small[0:NG, k:k + 1] for k in range(5))
            dve.tensor_tensor(span, high, base, ALU.subtract).then_inc(range_step, 1)
            dve.tensor_scalar(due, iota_p[0:NG, :], float(CHUNK // BODY),
                              -float(CHUNK // BODY * ((SIDE_LAG - 1) * BODY - 3)), ALU.mult,
                              ALU.add).then_inc(range_step, 1)
            dve.wait_ge(range_step, 2)
            dve.tensor_scalar(late, due, float(CHUNK * EARLY), base, ALU.min,
                              ALU.subtract).then_inc(range_step, 1)
            dve.wait_ge(range_step, 3)
            dve.tensor_scalar(late, late, 0.0, float(WR), ALU.is_gt, ALU.mult).then_inc(
                range_step, 1)
            dve.wait_ge(range_step, 4)
            dve.tensor_tensor(span, span, late, ALU.max).then_inc(ranges_ready, 1)
            dve.tensor_scalar(rel_row, drow, small[0:NG, 0:1], None, ALU.subtract).then_inc(
                dprep, 1)

            dve.wait_ge(lengths_in, 16)
            dve.tensor_scalar(far, lengths, 1.0, 1000.0, ALU.is_gt, ALU.mult).then_inc(r_ready, 1)
            dve.wait_ge(r_ready, 1)
            dve.scalar_tensor_tensor(lengths, lengths, 1.0, far, ALU.min, ALU.add).then_inc(
                r_ready, 1)
            dve.wait_ge(r_ready, 2)
            dve.tensor_scalar(lengths, lengths, 0.0, None, ALU.max).then_inc(r_ready, 1)

            dve.wait_ge(w0_in, 48)
            dve.tensor_scalar(w0_rest, w0[:], float(NB) ** 0.5, None, ALU.mult).then_inc(vprep, 1)
            dve.wait_ge(vprep, 1)
            dve.tensor_copy(w0_part[:, 0, :], w0_rest).then_inc(w0_split, 1)
            dve.tensor_copy(b2_part[:, 0, :], b2_row[:]).then_inc(bias_split, 1)
            for k in range(2):
                dve.wait_ge(w0_split, 2 * k + 1)
                dve.tensor_tensor(w0_rest, w0_rest, w0_part[:, k, :], ALU.subtract).then_inc(
                    w0_split, 1)
                dve.wait_ge(bias_split, 2 * k + 1)
                dve.tensor_tensor(b2_row[:], b2_row[:], b2_part[:, k, :], ALU.subtract).then_inc(
                    bias_split, 1)
                dve.wait_ge(w0_split, 2 * k + 2)
                dve.tensor_copy(w0_part[:, k + 1, :], w0_rest).then_inc(w0_split, 1)
                dve.wait_ge(bias_split, 2 * k + 2)
                dve.tensor_copy(b2_part[:, k + 1, :], b2_row[:]).then_inc(bias_split, 1)

            def split(n):
                s, r = n % 2, n // 2
                dve.wait_ge(emb_ready, n + 1)
                if live(n - 2, NE):
                    dve.wait_ge(emb_stored[s], 48 * r)
                dve.tensor_copy(emb_part[s][0], emb_rest[s]).then_inc(emb_cast, 1)
                dve.wait_ge(emb_cast, 2 * n + 1)
                dve.tensor_tensor(emb_rest[s], emb_rest[s], emb_part[s][0],
                                  ALU.subtract).then_inc(emb_split, 1)
                dve.wait_ge(emb_split, 4 * n + 1)
                dve.tensor_copy(emb_part[s][1], emb_rest[s]).then_inc(emb_cast, 1)
                dve.wait_ge(emb_cast, 2 * n + 2)
                dve.tensor_tensor(emb_part[s][2], emb_rest[s], emb_part[s][1],
                                  ALU.subtract).then_inc(emb_split, 3)

            split(0)
            dve.wait_ge(ranges_in, 48)
            dve.tensor_reduce(small[:, 8:9], span_all, AX, ALU.max).then_inc(dprep, 1)
            dve.wait_ge(dprep, 7)
            dve.tensor_scalar(gen_col[:, 0:1], small[:, 8:9], float(WR), None,
                              ALU.is_ge).then_inc(dprep, 1)
            dve.wait_ge(dprep, 8)
            dve.tensor_copy(gen_i[:], gen_col[0:1, 0:1]).then_inc(gen_ready, 1)
            dve.tensor_scalar(gen_col[:, 1:2], gen_col[:, 0:1], -1.0, 1.0, ALU.mult,
                              ALU.add).then_inc(dprep, 1)
            dve.wait_ge(dprep, 9)
            dve.tensor_scalar(rel_row_b, rel_row, gen_col[0:NG, 1:2], gen_col[0:NG, 0:1],
                              ALU.mult, ALU.subtract).then_inc(rel_ready, 1)
            dve.wait_ge(evec_in, 16)
            dve.tensor_tensor(evec_sq, rhat[:], rhat[:], ALU.mult).then_inc(vprep, 1)
            dve.wait_ge(vprep, 2)
            dve.tensor_reduce(norm, evec_sq, AX, ALU.add).then_inc(norm_sq, 1)

            dve.wait_ge(dcol_in, 16)
            dve.tensor_copy(dcol[:], dcol_i).then_inc(dprep, 1)
            dve.wait_ge(dprep, 10)
            dve.tensor_tensor(rel[:].rearrange("p (g t) -> p g t", t=TPG),
                              dcol[:].rearrange("p (g t) -> p g t", t=TPG),
                              along(base_all, 2, TPG), ALU.subtract).then_inc(dprep, 1)
            dve.wait_ge(norm_ready, 1)
            dve.tensor_scalar(norm, norm, 1e-12, None, ALU.add).then_inc(vprep, 1)
            dve.wait_ge(vprep, 3)
            dve.reciprocal(inv, norm).then_inc(vprep, 1)
            dve.wait_ge(vprep, 4)
            dve.tensor_tensor(rhat[:], rhat[:], along(inv, 2, 3), ALU.mult).then_inc(vprep, 1)
            dve.wait_ge(vprep, 5)
            dve.wait_ge(dprep, 11)

            def build_onehot(n, s):
                return dve.tensor_tensor(onehot[s][:], along(iota_n[:], 1, TPG),
                                         along(rel[:, bass.ds(n * TPG, TPG)], 2, W), ALU.is_equal)

            def all_windows(n, s, bank, step_sem, ready_sem, done_sem, add_sem):
                dve.tensor_copy(relw[:], dcol[:, bass.ds(n * TPG, TPG)]).then_inc(step_sem, 1)
                with dve.Fori(0, NW) as w:
                    dve.wait_ge(step_sem, n * (NW + 1) + w + 1)
                    dve.tensor_tensor(onehot[s][:], along(iota_n[:], 1, TPG),
                                      along(relw[:], 2, W), ALU.is_equal).then_inc(ready_sem, 1)
                    dve.wait_ge(ready_sem, n * NW + w + 1)
                    dve.tensor_scalar(relw[:], relw[:], -float(W), None, ALU.add).then_inc(
                        step_sem, 1)
                    dve.wait_ge(done_sem, n * NW + w + 1)
                    win = acc[:, :, bass.ds(w * W, W)]
                    dve.tensor_tensor(win, win, ps[:, bank, 0:2 * W].rearrange(
                        "p (c n) -> p c n", c=2), ALU.add).then_inc(add_sem, 1)
                dve.wait_ge(add_sem, n * NW + NW)
                dve.wait_ge(step_sem, (n + 1) * (NW + 1))

            def add_window(n, bank, add_sem):
                base = dve.value_load(base_sb[0:1, bass.ds(n, 1)], min_val=0, max_val=NP - W)
                if live(n - 1, NG):
                    dve.wait_ge(add_sem, n)
                win = acc[:, :, bass.ds(base, W)]
                dve.tensor_tensor(win, win, ps[:, bank, 0:2 * W].rearrange(
                    "p (c n) -> p c n", c=2), ALU.add).then_inc(add_sem, 1)

            VS = 6

            def messages(n, s, r, general):
                if live(n - 2, NG) and not general:
                    dve.wait_ge(seg_done, n - 1)
                if not general:
                    build_onehot(n, s)
                m = mid[s][:]
                vec = m[:, :, 2 * MUL:].rearrange("p t (c u k) -> p t c u k", c=3, u=2)
                w = ps[:, 2 + 2 * s:4 + 2 * s, :].rearrange("p b (t f) -> p (b t) f", t=4)
                xs, xv = gx[s][:, :, 0:MUL], gx[s][:, :, MUL:].rearrange(
                    "p t (c k) -> p t c k", c=3)
                unit = along(rhat[:, bass.ds(n * TPG, TPG), :], 3, MUL)
                dve.wait_ge(gathered[s], 128 * r + 128)
                dve.tensor_tensor(prod[:], xv, unit, ALU.mult).then_inc(vstep, 1)
                dve.wait_ge(w_mm, n + 1)
                dve.tensor_tensor(m[:, :, 0:2 * MUL].rearrange("p t (u k) -> p t u k", u=2),
                                  w[:, :, 0:2 * MUL].rearrange("p t (u k) -> p t u k", u=2),
                                  along(xs, 2, 2), ALU.mult).then_inc(vstep, 1)
                dve.wait_ge(vstep, n * VS + 1)
                dve.tensor_tensor(dot[:], prod[:, :, 0, :], prod[:, :, 1, :], ALU.add).then_inc(
                    vstep, 1)
                dve.wait_ge(vstep, n * VS + 2)
                dve.tensor_tensor(vec[:, :, :, 0, :], along(m[:, :, MUL:2 * MUL], 2, 3), unit,
                                  ALU.mult).then_inc(vstep, 1)
                dve.wait_ge(vstep, n * VS + 3)
                dve.tensor_tensor(dot[:], dot[:], prod[:, :, 2, :], ALU.add).then_inc(vstep, 1)
                dve.tensor_tensor(vec[:, :, :, 1, :], along(w[:, :, 2 * MUL:3 * MUL], 2, 3), xv,
                                  ALU.mult).then_inc(vstep, 1)
                dve.wait_ge(vstep, n * VS + 5)
                dve.tensor_tensor(m[:, :, MUL:2 * MUL], w[:, :, 3 * MUL:], dot[:],
                                  ALU.mult).then_inc(mid_ready, 1)

            def norm_stats(src, st, mv, bn_sem, mv_sem, n):
                for q in range(4):
                    dve.bn_stats(st[:, q, :], src[:, q, :]).then_inc(bn_sem, 1)
                dve.wait_ge(bn_sem, 4 * n + 4)
                hold(dve)
                for q in range(4):
                    dve.bn_aggr(mv[:, q, :], st[:, q, :]).then_inc(mv_sem, 1)

            def side(c, part):
                if part == 1:
                    dve.wait_ge(side_copied, c * 4 + 1)
                    dve.wait_ge(side_x_in, c * 16 + 16)
                    dve.tensor_tensor(side_y, side_y, side_x, ALU.add).then_inc(side_added, 1)
                    dve.wait_ge(side_added, c + 1)
                    norm_stats(side_y, stats[0], mean_var[0], side_bn, side_var, c)
                if part == 3:
                    dve.wait_ge(side_std, c + 1)
                    dve.reciprocal(std[0][:], std[0][:]).then_inc(side_rstd, 1)
                    dve.wait_ge(side_rstd, c + 1)
                    dve.wait_ge(emb_stored[1], 48 * last(NE, 2, 1))
                    for q in range(4):
                        dve.tensor_scalar(side_x1[:, q, :], side_y[:, q, :],
                                          mean_var[0][:, q, 0:1], std[0][:, q:q + 1],
                                          ALU.subtract, ALU.mult).then_inc(side_ready, 1)
                    dve.wait_ge(side_ready, c * 4 + 4)
                    dve.wait_ge(late_in, 16 * N_LATE)
                    dve.tensor_tensor(x1n[:, bass.ds(c * 4, 4), :], side_x1,
                                      along(beta[:], 1, 4), ALU.add).then_inc(side_kept, 1)

            def layer1(general):
                def step(n, s, r, beside=None):
                    if live(n, NG):
                        messages(n, s, r, general)
                        if general:
                            all_windows(n, s, 6, relw_step, win_ready, win_done, acc_add)
                    if live(n - 1, NG) and not general:
                        dve.wait_ge(seg_done, n)
                        add_window(n - 1, 6 + (1 - s), acc_add)
                    if isinstance(n, int) and n == 0:
                        split(1)
                    if emb_beside(n):
                        split(emb_beside(n))
                    if beside:
                        side(*beside)
                if general:
                    run_steps(dve, NG, 1, HEAD, step)
                else:
                    run_passes(dve, 1, HEAD, step)

            dve.wait_ge(acc_cleared, 2)
            general = dve.value_load(gen_i[0:1, 0:1], min_val=0, max_val=1)

            def node_phase(first):
                steps = NC - first
                dve.engine_nop().then_inc(acc_all, 1)
                dve.wait_ge(fold_copied, 2)
                dve.wait_ge(late_in, 16 * N_LATE)
                dve.tensor_tensor(v_row[:, F:2 * F], ub2[0:1, :], beta[0:1, :],
                                  ALU.subtract).then_inc(bias_ready, 1)
                dve.wait_ge(bias_ready, 1)
                dve.tensor_copy(v_part[:, 0, :], v_row).then_inc(bias_split, 1)
                for k in range(2):
                    dve.wait_ge(bias_split, 5 + 2 * k + 1)
                    dve.tensor_tensor(v_row, v_row, v_part[:, k, :], ALU.subtract).then_inc(
                        bias_split, 1)
                    dve.wait_ge(bias_split, 5 + 2 * k + 2)
                    dve.tensor_copy(v_part[:, k + 1, :], v_row).then_inc(bias_split, 1)

                def nodes(n, s, r):
                    if live(n, steps):
                        dve.wait_ge(po_mm, n + 1)
                        dve.wait_ge(xin_loaded[s], 16 * r + 16)
                        if live(n - 2, steps):
                            dve.wait_ge(x1_ready, 4 * n - 4)
                        po = quad(ps[:, s, :])
                        dve.tensor_tensor(y[s][:, :, 0:MUL], po[:, :, 0:MUL], xin[s][:, :, 0:MUL],
                                          ALU.add).then_inc(y_ready, 1)
                        dve.tensor_tensor(
                            y[s][:, :, MUL:].rearrange("p q (k c) -> p q c k", c=3),
                            po[:, :, MUL:].rearrange("p q (c k) -> p q c k", c=3),
                            xin[s][:, :, MUL:].rearrange("p q (k c) -> p q c k", c=3),
                            ALU.add).then_inc(y_ready, 1)
                        dve.wait_ge(y_ready, 2 * n + 2)
                        norm_stats(y[s], stats[s], mean_var[s], bn_done, mv_ready, n)
                    if live(n - 1, steps):
                        o = 1 - s
                        dve.wait_ge(std_ready, n)
                        dve.reciprocal(std[o][:], std[o][:]).then_inc(rstd_ready, 1)
                        dve.wait_ge(rstd_ready, n)
                        if live(n - 3, steps):
                            dve.wait_ge(x1t_mm, n - 2)
                            dve.wait_ge(x1_kept, n - 2)
                        for q in range(4):
                            dve.tensor_scalar(x1s[o][:, q, :], y[o][:, q, :],
                                              mean_var[o][:, q, 0:1], std[o][:, q:q + 1],
                                              ALU.subtract, ALU.mult).then_inc(x1_ready, 1)
                run_steps(dve, steps, 1, 4, nodes)

            with dve.If(general == 1):
                layer1(True)
                node_phase(0)
            with dve.Else():
                layer1(False)
                dve.wait_ge(side_kept, EARLY)
                node_phase(EARLY)

            def side2(c, part):
                if part == 0:
                    dve.wait_ge(acc2_add, (c + SIDE_LAG) * BODY - 1)
                    cnt = acc[:, 1, bass.ds(c * CHUNK, CHUNK)]
                    dve.wait_ge(bias_out, 32)
                    dve.tensor_scalar(side2_inv, cnt, 1.0, None, ALU.max).then_inc(side2_cnt, 1)
                    dve.tensor_scalar(side2_some, cnt[0:3, :], 1.0, None, ALU.min).then_inc(
                        side2_cnt, 1)
                    dve.wait_ge(side2_cnt, c * 3 + 2)
                    dve.reciprocal(side2_inv, side2_inv).then_inc(side2_cnt, 1)
                if part == 1:
                    dve.wait_ge(side2_cnt, c * 3 + 3)
                    dve.tensor_tensor(side2_agg, acc[:, 0, bass.ds(c * CHUNK, CHUNK)], side2_inv,
                                      ALU.mult).then_inc(side2_means, 1)
                x1_rows = x1n[:, bass.ds(c * 4, 4), :]
                if part == 4:
                    dve.wait_ge(side_copied, EARLY * 4 + c * 2 + 2)
                    dve.tensor_tensor(side2_t, side2_t, x1_rows, ALU.add).then_inc(side_added, 1)
                    dve.wait_ge(side_added, EARLY + c + 1)
                    norm_stats(side2_t, stats[0], mean_var[0], side_bn, side_var,
                               c * 2 + EARLY)
                if part == 6:
                    dve.wait_ge(side_std, EARLY + c * 2 + 1)
                    dve.reciprocal(std[0][:], std[0][:]).then_inc(side2_zstep, 1)
                    dve.wait_ge(side2_zstep, c * 7 + 1)
                    for q in range(4):
                        dve.tensor_scalar(side2_z[:, q, :], side2_t[:, q, :],
                                          mean_var[0][:, q, 0:1], std[0][:, q:q + 1],
                                          ALU.subtract, ALU.mult).then_inc(side2_zstep, 1)
                    dve.wait_ge(side2_zstep, c * 7 + 5)
                    dve.tensor_tensor(side2_z, side2_z, along(gamma[:], 1, 4),
                                      ALU.mult).then_inc(side2_zstep, 1)
                    dve.wait_ge(side2_zstep, c * 7 + 6)
                    dve.tensor_tensor(side2_z, side2_z, x1_rows, ALU.add).then_inc(side2_zstep, 1)
                    dve.wait_ge(side2_zstep, c * 7 + 7)
                    norm_stats(side2_z, stats_b[0], mean_var_b[0], side_bn, side_var,
                               c * 2 + (EARLY + 1))
                if part == 7:
                    dve.wait_ge(side_std, EARLY + c * 2 + 2)
                    dve.reciprocal(std_b[0][:], std_b[0][:]).then_inc(side_rstd, 1)
                    dve.wait_ge(side_rstd, EARLY + c + 1)
                    dve.wait_ge(side2_stored, c * 16 + 1)
                    for q in range(4):
                        dve.tensor_scalar(side2_res[:, q, :], side2_z[:, q, :],
                                          mean_var_b[0][:, q, 0:1], std_b[0][:, q:q + 1],
                                          ALU.subtract, ALU.mult).then_inc(side_ready, 1)

            def layer2(general):
                def step(n, s, r, beside=None):
                    o = 1 - s
                    if live(n, NG):
                        dve.wait_ge(rel_spread, n + 1)
                        if live(n - 2, NG):
                            dve.wait_ge(pre_mm, n - 1)
                        dve.tensor_scalar(
                            onehot_t[s][0:WR, :], ps[0:WR, 6:8, :].rearrange("p b e -> p (b e)"),
                            iota_p[0:WR, 0:1], None, ALU.is_equal).then_inc(oht_ready, 1)
                    if live(n - 1, NG):
                        if live(n - 3, NG):
                            dve.wait_ge(seg2_done, n - 2)
                        build_onehot(n - 1, o).then_inc(onehot_built, 1)
                        dve.wait_ge(gathered2[o], 128 * (r + s))
                        dve.wait_ge(pre_mm, n)
                        if live(n - 3, NG):
                            dve.wait_ge(relu_done, n - 2)
                        pre = ps[:, 2 * o:2 * o + 2, :].rearrange("p b (t f) -> p (b t) f", t=4)
                        add = dve.tensor_tensor(sums[o], pre, gx[o][:], ALU.add)
                        if general:
                            add.then_inc(sum_step, 1)
                            dve.wait_ge(sum_step, n)
                            add = dve.tensor_tensor(sums[o], sums[o], gb[o], ALU.add)
                        add.then_inc(sums_ready, 1)
                        if general:
                            dve.wait_ge(relu_done, n)
                            all_windows(n - 1, o, 4, relw2_step, win2_ready, win2_done, acc2_add)
                    if live(n - 2, NG) and not general:
                        dve.wait_ge(seg2_done, n - 1)
                        add_window(n - 2, 4 + s, acc2_add)
                    if beside:
                        side2(*beside)
                if general:
                    run_steps(dve, NG, 2, 4, step)
                else:
                    run_passes(dve, 2, BODY, step)

            def scale_shift(rstd, shifts, mv, done, n):
                dve.reciprocal(rstd[:], rstd[:]).then_inc(done, 1)
                dve.wait_ge(done, 2 * n + 1)
                dve.scalar_tensor_tensor(shifts[:], mv[:, :, 0], -1.0, rstd[:], ALU.mult,
                                         ALU.mult).then_inc(done, 1)

            def last_phase(first):
                steps = NC - first
                dve.engine_nop().then_inc(acc2_all, 1)
                dve.wait_ge(acc2_all, 1)

                counts = acc[:, 1, first * CHUNK:first * CHUNK + CHUNK]
                dve.tensor_scalar(cnt_inv[0], counts, 1.0, None, ALU.max).then_inc(first_ready, 1)
                dve.tensor_scalar(cnt_some[0], counts[0:3, :], 1.0, None, ALU.min).then_inc(
                    first_ready, 1)
                dve.wait_ge(first_ready, 1)
                dve.reciprocal(cnt_inv[0][:, 0:CHUNK // 2], cnt_inv[0][:, 0:CHUNK // 2]).then_inc(
                    first_ready, 1)
                dve.wait_ge(cnt_in, 16)
                dve.tensor_scalar(some_cols[:], cnt_cols[:], 1.0, None, ALU.min).then_inc(
                    cnt_ready, 1)
                dve.wait_ge(cnt_ready, 1)
                dve.tensor_scalar(cnt_cols[:], cnt_cols[:], 1.0, None, ALU.max).then_inc(
                    cnt_ready, 1)
                dve.wait_ge(cnt_ready, 2)
                dve.reciprocal(cnt_cols[:], cnt_cols[:]).then_inc(cnt_ready, 1)
                dve.reciprocal(cnt_inv[0][:, CHUNK // 2:], cnt_inv[0][:, CHUNK // 2:]).then_inc(
                    first_ready, 1)

                def update(n, s, r):
                    o = 1 - s
                    if live(n - 2, steps):
                        dve.wait_ge(pu_mm, n - 1)
                        if live(n - 4, steps):
                            dve.wait_ge(z_ready, 4 * n - 12)
                        tiles = tiles_of(n - 2, steps)
                        dve.tensor_tensor(t_sum[s][:, 0:tiles, :],
                                          quad(ps[:, 4 + s, :])[:, 0:tiles, :],
                                          x1n[:, bass.ds((n + first - 2) * 4, tiles), :],
                                          ALU.add).then_inc(t_ready, 1)
                        dve.wait_ge(t_ready, n - 1)
                        norm_stats(t_sum[s], stats[s], mean_var[s], bna, var_a, n - 2)
                    if live(n - 4, steps):
                        dve.wait_ge(stdb, n - 3)
                        scale_shift(std_b[s], shift_b[s], mean_var_b[s], rstdb, n - 4)
                    if live(n - 2, steps):
                        dve.wait_ge(stda, n - 1)
                        scale_shift(std[s], shift[s], mean_var[s], rstda, n - 2)
                    if live(n - 4, steps):
                        if live(n - 6, steps):
                            dve.wait_ge(out_stored[s], 16 * r - 32)
                        for q in range(ACT_TILES, 4):
                            dve.tensor_scalar(res[s][:, q, :], z[s][:, q, :],
                                              mean_var_b[s][:, q, 0:1], std_b[s][:, q:q + 1],
                                              ALU.subtract, ALU.mult).then_inc(res_ready, 1)
                    if live(n - 3, steps):
                        dve.wait_ge(zx, n - 2)
                        norm_stats(z[o], stats_b[o], mean_var_b[o], bnb, var_b, n - 3)
                run_steps(dve, steps, 4, 6, update)

            dve.wait_ge(acc_cleared, 3)
            with dve.If(general == 1):
                layer2(True)
                last_phase(0)
            with dve.Else():
                layer2(False)
                dve.wait_ge(side2_stored, 16 * EARLY + 1)
                last_phase(EARLY)
    return nc


def kernel(**inputs):
    import numpy as np
    import concourse.bacc as bacc
    from concourse.bass_utils import run_bass_kernel_spmd

    given = {k: np.ascontiguousarray(v) for k, v in inputs.items()}

    def pad(x, n, value=0):
        fill = np.full((n - x.shape[0],) + x.shape[1:], value, x.dtype)
        return np.concatenate([x, fill])

    x = pad(given["x"], NP)
    order = np.concatenate([np.arange(MUL)] + [MUL + 3 * np.arange(MUL) + c for c in range(3)])
    src, dst = pad(given["src"], EP), pad(given["dst"], EP, N)

    def by_tile(v):
        return v.reshape(NT, P, *v.shape[1:]).swapaxes(0, 1)

    def ids(v):
        return v.reshape(NG, TPG, P).transpose(0, 2, 1)

    arrays = {
        "x_t": x[:, order].T,
        "x_rows": x,
        "ids": np.concatenate([ids(src), ids(dst)], axis=2).reshape(NG * P, 2 * TPG),
        "dst_row": dst.reshape(NG, GROUP),
        "dst_col": by_tile(dst),
        "evec": by_tile(pad(given["edge_attr_3"], EP)),
        "lengths": pad(given["edge_weight"], EP).reshape(NG, GROUP),
        "attr_rows": np.concatenate([
            pad(given["edge_attr_2"], EP).reshape(NG, GROUP, 2).transpose(0, 2, 1),
            np.ones((NG, 1, GROUP), np.float32)], axis=1),
    }
    for name, key in (("w_up0", "L0_gnn_W_up0"), ("w_up1", "L0_gnn_W_up1"),
                      ("mlp_w0", "L0_gnn_mlp_w0"), ("mlp_b0", "L0_gnn_mlp_b0"),
                      ("mlp_w1", "L0_gnn_mlp_w1"), ("mlp_b1", "L0_gnn_mlp_b1"),
                      ("mlp_w2", "L0_gnn_mlp_w2"), ("mlp_b2", "L0_gnn_mlp_b2"),
                      ("w_out0", "L0_gnn_W_out0"), ("w_out1", "L0_gnn_W_out1"),
                      ("m_w1", "L1_gnn_mW1"), ("mb1", "L1_gnn_mb1"), ("m_w2", "L1_gnn_mW2"),
                      ("mb2", "L1_gnn_mb2"), ("u_w1", "L1_gnn_uW1"), ("ub1", "L1_gnn_ub1"),
                      ("u_w2", "L1_gnn_uW2"), ("ub2", "L1_gnn_ub2"), ("gamma", "L1_gnn_gamma"),
                      ("beta", "L1_gnn_beta")):
        arrays[name] = given[key]
    arrays = {f"in_{k}": np.ascontiguousarray(v) for k, v in arrays.items()}

    nc = bacc.Bacc("TRN2", target_bir_lowering=False, num_devices=1)
    a = {k[3:]: nc.dram_tensor(k, v.shape, mybir.dt.from_np(v.dtype), kind="ExternalInput").ap()
         for k, v in arrays.items()}
    out = nc.dram_tensor("out_rows", [NP, F], F32, kind="ExternalOutput").ap()
    gnn_kernel(nc, a, out)
    r = run_bass_kernel_spmd(nc, [arrays], core_ids=[0])
    return r.results[0]["out_rows"][:N]
```
